# Optimizing a Trainium2 kernel written in Bass

```python
import numpy as np
import jax
import jax.numpy as jnp

def _softmax(x, axis=-1):
    return jax.nn.softmax(x, axis=axis)

def _gelu(x):
    return jax.nn.gelu(x, approximate=True)

def _silu(x):
    return jax.nn.silu(x)

def _sigmoid(x):
    return jax.nn.sigmoid(x)

def _layernorm(x, axis=-1, eps=1e-05):
    m = jnp.mean(x, axis=axis, keepdims=True)
    v = jnp.var(x, axis=axis, keepdims=True)
    return (x - m) / jnp.sqrt(v + eps)

def _scatter_add(tgt, idx, src, axis=0):
    return tgt.at[idx].add(src)

def _segment_sum(src, seg, n):
    return jax.ops.segment_sum(src, seg, n)
kernel_name = 'mk_decoder_preln_d2_seqx_r8_87f63c'

def setup_inputs(seed: int=0):
    np.random.seed(seed)
    _w = jnp.asarray

    def _rec_inputs():
        import jax
        import jax.numpy as jnp
        _rk = jax.random.key(seed)
        x = -0.0002928 + 1 * jax.random.normal(jax.random.fold_in(_rk, 1), (32, 128, 128), jnp.float32)
        _lenS = 128 - jax.random.randint(jax.random.fold_in(_rk, 7), (32,), 0, max(1, 128 // 4) + 1, jnp.int32)
        _lenS2 = 77 - jax.random.randint(jax.random.fold_in(_rk, 8), (32,), 0, max(1, 77 // 4) + 1, jnp.int32)
        _ctx_1024P = jax.random.normal(jax.random.fold_in(_rk, 11), (32, 16, 128), jnp.float32)
        _ctx_1024c = jax.random.dirichlet(jax.random.fold_in(_rk, 511), 0.3 * jnp.ones((16,), jnp.float32), (32, 77))
        _ctx_1024t = jnp.einsum('bsk,bkd->bsd', _ctx_1024c, _ctx_1024P)
        _ctx_1024t = _ctx_1024t * jax.lax.rsqrt(jnp.mean(jnp.square(_ctx_1024t)) + 1e-12) * 0.953939
        ctx_1024 = -8.57375e-05 + 0.999917 * (_ctx_1024t + 0.3 * jax.random.normal(jax.random.fold_in(_rk, 611), (32, 77, 128), jnp.float32))
        _validS = jnp.arange(128)[None, :] < _lenS[:, None]
        _validS2 = jnp.arange(77)[None, :] < _lenS2[:, None]
        _causal = jnp.tril(jnp.ones((128, 128), dtype=bool))
        mask_Bx1xS2_if1 = jnp.where(jnp.ones((32, 1, 77), dtype=bool), 1, 0).astype(jnp.int32)
        mask_Bx1xSxS2_ik0 = jnp.where(jnp.broadcast_to(_validS2[:, None, None, :], (32, 1, 128, 77)), 0, 1).astype(jnp.int32)
        return (x, ctx_1024, mask_Bx1xS2_if1, mask_Bx1xSxS2_ik0)
    x, ctx_1024, mask_Bx1xS2_if1, mask_Bx1xSxS2_ik0 = _rec_inputs()

    def _L0_attn_setup():
        import jax, jax.numpy as jnp
        import numpy as np
        from functools import partial
        D_MODEL = 128
        D_STATE = 16
        D_CONV = 4
        EXPAND = 2
        D_INNER = EXPAND * D_MODEL
        DT_RANK = (D_MODEL + 15) // 16
        BATCH, SEQ = (2, 128)

        def _mamba_params(key):
            ks = jax.random.split(key, 9)
            s = lambda k, shape, scale: jax.random.normal(k, shape, jnp.float32) * scale
            return dict(in_w=s(ks[0], (2 * D_INNER, D_MODEL), D_MODEL ** (-0.5)), conv_w=s(ks[1], (D_INNER, 1, D_CONV), D_CONV ** (-0.5)), conv_b=s(ks[2], (D_INNER,), 0.02), xproj_w=s(ks[3], (DT_RANK + 2 * D_STATE, D_INNER), D_INNER ** (-0.5)), dt_w=s(ks[4], (D_INNER, DT_RANK), DT_RANK ** (-0.5)), dt_b=s(ks[5], (D_INNER,), 0.02), A_log=jnp.log(jnp.broadcast_to(jnp.arange(1, D_STATE + 1, dtype=jnp.float32), (D_INNER, D_STATE))), D=jnp.ones((D_INNER,), jnp.float32), out_w=s(ks[8], (D_MODEL, D_INNER), D_INNER ** (-0.5)))

        def _mamba(x, in_w, conv_w, conv_b, xproj_w, dt_w, dt_b, A_log, D, out_w):
            B, L, _ = x.shape
            xz = jnp.einsum('bld,ed->ble', x, in_w)
            u, z = jnp.split(xz, 2, axis=-1)
            u_c = jnp.swapaxes(u, 1, 2)
            u_c = jax.lax.conv_general_dilated(u_c, conv_w, window_strides=(1,), padding=[(D_CONV - 1, 0)], dimension_numbers=('NCH', 'OIH', 'NCH'), feature_group_count=D_INNER)
            u_c = u_c + conv_b[None, :, None]
            u = jax.nn.silu(jnp.swapaxes(u_c, 1, 2))
            x_dbl = jnp.einsum('bld,ed->ble', u, xproj_w)
            dt = jax.nn.softplus(jnp.einsum('blr,dr->bld', x_dbl[..., :DT_RANK], dt_w) + dt_b)
            Bm = x_dbl[..., DT_RANK:DT_RANK + D_STATE]
            Cm = x_dbl[..., DT_RANK + D_STATE:]
            A = -jnp.exp(A_log)
            dA = jnp.exp(dt[..., None] * A)
            dBu = dt[..., None] * Bm[:, :, None, :] * u[..., None]

            def step(h, ins):
                dA_t, dBu_t, C_t = ins
                h = dA_t * h + dBu_t
                y = jnp.einsum('bdn,bn->bd', h, C_t)
                return (h, y)
            h0 = jnp.zeros((B, D_INNER, D_STATE), dA.dtype)
            _, ys = jax.lax.scan(step, h0, (jnp.swapaxes(dA, 0, 1), jnp.swapaxes(dBu, 0, 1), jnp.swapaxes(Cm, 0, 1)))
            y = jnp.swapaxes(ys, 0, 1) + u * D
            y = y * jax.nn.silu(z)
            return jnp.einsum('bld,ed->ble', y, out_w)
        key = jax.random.key(seed)
        kx, kf, kb, kg = jax.random.split(key, 4)
        inp = {'x': jax.random.normal(kx, (BATCH, SEQ, D_MODEL), jnp.float32), 'gamma': jnp.ones((D_MODEL,), jnp.float32), 'beta': jnp.zeros((D_MODEL,), jnp.float32)}
        for pref, k in (('f_', kf), ('b_', kb)):
            for name, val in _mamba_params(k).items():
                inp[pref + name] = val
        return inp
    _L0_attn_all = _L0_attn_setup()
    _L0_attn_in = {k: v for k, v in _L0_attn_all.items() if k in ('gamma', 'beta', 'f_in_w', 'f_conv_w', 'f_conv_b', 'f_xproj_w', 'f_dt_w', 'f_dt_b', 'f_A_log', 'f_D', 'f_out_w', 'b_in_w', 'b_conv_w', 'b_conv_b', 'b_xproj_w', 'b_dt_w', 'b_dt_b', 'b_A_log', 'b_D', 'b_out_w')}
    del _L0_attn_all

    def _L0_xattn_setup():
        import jax, jax.numpy as jnp
        import numpy as np
        B, T1, T2, NFEAT, H = (8, 64, 1500, 128, 16)
        DK = NFEAT // H
        key = jax.random.key(seed)
        ks = jax.random.split(key, 8)
        s = 0.02
        return {'x': jax.random.normal(ks[0], (B, T1, NFEAT), dtype=jnp.float32), 'memory': jax.random.normal(ks[1], (B, T2, NFEAT), dtype=jnp.float32), 'memory_mask': jnp.ones((B, 1, T2), dtype=jnp.int32), 'Wq': jax.random.normal(ks[2], (NFEAT, NFEAT), dtype=jnp.float32) * s, 'bq': jnp.zeros((NFEAT,), dtype=jnp.float32), 'Wkv': jax.random.normal(ks[3], (NFEAT, 2 * NFEAT), dtype=jnp.float32) * s, 'bkv': jnp.zeros((2 * NFEAT,), dtype=jnp.float32), 'Wout': jax.random.normal(ks[4], (NFEAT, NFEAT), dtype=jnp.float32) * s, 'bout': jnp.zeros((NFEAT,), dtype=jnp.float32)}
    _L0_xattn_all = _L0_xattn_setup()
    _L0_xattn_in = {k: v for k, v in _L0_xattn_all.items() if k in ('Wq', 'bq', 'Wkv', 'bkv', 'Wout', 'bout')}
    del _L0_xattn_all

    def _L0_ffn_setup():
        import jax, jax.numpy as jnp
        import numpy as np
        E = 8
        H = 128
        M = 256
        K = 2
        SE = 1
        BSZ, SEQ = (2, 128)
        W_SCALE = 0.02
        key = jax.random.key(seed)
        ks = jax.random.split(key, 9)
        return {'x': jax.random.normal(ks[0], (BSZ, SEQ, H), jnp.float32), 'gate_w': jax.random.normal(ks[1], (E, H), jnp.float32) * W_SCALE, 'beta': jnp.zeros((E,), jnp.float32), 'gate_proj_w': jax.random.normal(ks[2], (E, H, M), jnp.float32) * W_SCALE, 'up_proj_w': jax.random.normal(ks[3], (E, H, M), jnp.float32) * W_SCALE, 'down_proj_w': jax.random.normal(ks[4], (E, M, H), jnp.float32) * W_SCALE, 'shared_gate_w': jax.random.normal(ks[5], (SE, H, M), jnp.float32) * W_SCALE, 'shared_up_w': jax.random.normal(ks[6], (SE, H, M), jnp.float32) * W_SCALE, 'shared_down_w': jax.random.normal(ks[7], (SE, M, H), jnp.float32) * W_SCALE}
    _L0_ffn_all = _L0_ffn_setup()
    _L0_ffn_in = {k: v for k, v in _L0_ffn_all.items() if k in ('gate_w', 'beta', 'gate_proj_w', 'up_proj_w', 'down_proj_w', 'shared_gate_w', 'shared_up_w', 'shared_down_w')}
    del _L0_ffn_all

    def _L1_attn_setup():
        import jax, jax.numpy as jnp
        import numpy as np
        DIM, H, KV, HD, WIN = (128, 16, 4, 64, 64)
        EPS = 1e-06

        def rmsnorm(x, w, eps=EPS):
            return x * jax.lax.rsqrt(jnp.mean(x * x, axis=-1, keepdims=True) + eps) * w
        key = jax.random.key(seed)
        ks = jax.random.split(key, 7)
        B, T = (4, 256)
        s = 0.02
        return {'x': jax.random.normal(ks[0], (B, T, DIM), dtype=jnp.float32), 'wq': jax.random.normal(ks[1], (H * HD, DIM), dtype=jnp.float32) * s, 'wk': jax.random.normal(ks[2], (KV * HD, DIM), dtype=jnp.float32) * s, 'wv': jax.random.normal(ks[3], (KV * HD, DIM), dtype=jnp.float32) * s, 'wo': jax.random.normal(ks[4], (DIM, H * HD), dtype=jnp.float32) * s, 'q_norm_w': jnp.ones((HD,), dtype=jnp.float32), 'k_norm_w': jnp.ones((HD,), dtype=jnp.float32)}
    _L1_attn_all = _L1_attn_setup()
    _L1_attn_in = {k: v for k, v in _L1_attn_all.items() if k in ('wq', 'wk', 'wv', 'wo', 'q_norm_w', 'k_norm_w')}
    del _L1_attn_all

    def _L1_xattn_setup():
        import jax, jax.numpy as jnp
        import numpy as np
        D_MODEL = 128
        NUM_HEADS = 16
        BATCH = 2
        SEQ = 256
        NEG_INF = -1000000000.0

        def _split_heads(x):
            b, s, d = x.shape
            return x.reshape(b, s, NUM_HEADS, d // NUM_HEADS).transpose(0, 2, 1, 3)
        key = jax.random.key(seed)
        ks = jax.random.split(key, 12)
        s = 1.0 / np.sqrt(D_MODEL)
        inp = {'Q': jax.random.normal(ks[0], (BATCH, SEQ, D_MODEL), jnp.float32), 'K': jax.random.normal(ks[1], (BATCH, SEQ, D_MODEL), jnp.float32), 'V': jax.random.normal(ks[2], (BATCH, SEQ, D_MODEL), jnp.float32), 'mask': jnp.broadcast_to(jnp.tril(jnp.ones((SEQ, SEQ), jnp.int32))[None, None], (BATCH, 1, SEQ, SEQ)).astype(jnp.int32), 'Wq': jax.random.normal(ks[3], (D_MODEL, D_MODEL), jnp.float32) * s, 'bq': jax.random.normal(ks[4], (D_MODEL,), jnp.float32) * s, 'Wk': jax.random.normal(ks[5], (D_MODEL, D_MODEL), jnp.float32) * s, 'bk': jax.random.normal(ks[6], (D_MODEL,), jnp.float32) * s, 'Wv': jax.random.normal(ks[7], (D_MODEL, D_MODEL), jnp.float32) * s, 'bv': jax.random.normal(ks[8], (D_MODEL,), jnp.float32) * s, 'Wo': jax.random.normal(ks[9], (D_MODEL, D_MODEL), jnp.float32) * s, 'bo': jax.random.normal(ks[10], (D_MODEL,), jnp.float32) * s}
        return inp
    _L1_xattn_all = _L1_xattn_setup()
    _L1_xattn_in = {k: v for k, v in _L1_xattn_all.items() if k in ('Wq', 'bq', 'Wk', 'bk', 'Wv', 'bv', 'Wo', 'bo')}
    del _L1_xattn_all

    def _L1_ffn_setup():
        import jax, jax.numpy as jnp
        import numpy as np
        LN_EPS = 1e-12
        key = jax.random.key(seed)
        ks = jax.random.split(key, 8)
        B, S, H, I, E = (4, 256, 128, 512, 8)
        sH = 1.0 / np.sqrt(H)
        sI = 1.0 / np.sqrt(I)
        return {'hidden_states': jax.random.normal(ks[0], (B, S, H), dtype=jnp.float32), 'Wr': jax.random.uniform(ks[1], (E, H), jnp.float32, -sH, sH), 'W1': jax.random.uniform(ks[2], (E, H, I), jnp.float32, -sH, sH), 'b1': jax.random.uniform(ks[3], (E, I), jnp.float32, -sH, sH), 'Wo': jax.random.uniform(ks[4], (I, H), jnp.float32, -sI, sI), 'bo': jax.random.uniform(ks[5], (H,), jnp.float32, -sI, sI), 'gamma': jnp.ones((H,), jnp.float32), 'beta': jnp.zeros((H,), jnp.float32)}
    _L1_ffn_all = _L1_ffn_setup()
    _L1_ffn_in = {k: v for k, v in _L1_ffn_all.items() if k in ('Wr', 'W1', 'b1', 'Wo', 'bo', 'gamma', 'beta')}
    del _L1_ffn_all
    return {'x': x, 'ctx_1024': ctx_1024, 'mask_Bx1xS2_if1': mask_Bx1xS2_if1, 'mask_Bx1xSxS2_ik0': mask_Bx1xSxS2_ik0, 'L0_attn_gamma': _L0_attn_in['gamma'], 'L0_attn_beta': _L0_attn_in['beta'], 'L0_attn_f_in_w': _L0_attn_in['f_in_w'], 'L0_attn_f_conv_w': _L0_attn_in['f_conv_w'], 'L0_attn_f_conv_b': _L0_attn_in['f_conv_b'], 'L0_attn_f_xproj_w': _L0_attn_in['f_xproj_w'], 'L0_attn_f_dt_w': _L0_attn_in['f_dt_w'], 'L0_attn_f_dt_b': _L0_attn_in['f_dt_b'], 'L0_attn_f_A_log': _L0_attn_in['f_A_log'], 'L0_attn_f_D': _L0_attn_in['f_D'], 'L0_attn_f_out_w': _L0_attn_in['f_out_w'], 'L0_attn_b_in_w': _L0_attn_in['b_in_w'], 'L0_attn_b_conv_w': _L0_attn_in['b_conv_w'], 'L0_attn_b_conv_b': _L0_attn_in['b_conv_b'], 'L0_attn_b_xproj_w': _L0_attn_in['b_xproj_w'], 'L0_attn_b_dt_w': _L0_attn_in['b_dt_w'], 'L0_attn_b_dt_b': _L0_attn_in['b_dt_b'], 'L0_attn_b_A_log': _L0_attn_in['b_A_log'], 'L0_attn_b_D': _L0_attn_in['b_D'], 'L0_attn_b_out_w': _L0_attn_in['b_out_w'], 'L0_xattn_Wq': _L0_xattn_in['Wq'], 'L0_xattn_bq': _L0_xattn_in['bq'], 'L0_xattn_Wkv': _L0_xattn_in['Wkv'], 'L0_xattn_bkv': _L0_xattn_in['bkv'], 'L0_xattn_Wout': _L0_xattn_in['Wout'], 'L0_xattn_bout': _L0_xattn_in['bout'], 'L0_ffn_gate_w': _L0_ffn_in['gate_w'], 'L0_ffn_beta': _L0_ffn_in['beta'], 'L0_ffn_gate_proj_w': _L0_ffn_in['gate_proj_w'], 'L0_ffn_up_proj_w': _L0_ffn_in['up_proj_w'], 'L0_ffn_down_proj_w': _L0_ffn_in['down_proj_w'], 'L0_ffn_shared_gate_w': _L0_ffn_in['shared_gate_w'], 'L0_ffn_shared_up_w': _L0_ffn_in['shared_up_w'], 'L0_ffn_shared_down_w': _L0_ffn_in['shared_down_w'], 'L1_attn_wq': _L1_attn_in['wq'], 'L1_attn_wk': _L1_attn_in['wk'], 'L1_attn_wv': _L1_attn_in['wv'], 'L1_attn_wo': _L1_attn_in['wo'], 'L1_attn_q_norm_w': _L1_attn_in['q_norm_w'], 'L1_attn_k_norm_w': _L1_attn_in['k_norm_w'], 'L1_xattn_Wq': _L1_xattn_in['Wq'], 'L1_xattn_bq': _L1_xattn_in['bq'], 'L1_xattn_Wk': _L1_xattn_in['Wk'], 'L1_xattn_bk': _L1_xattn_in['bk'], 'L1_xattn_Wv': _L1_xattn_in['Wv'], 'L1_xattn_bv': _L1_xattn_in['bv'], 'L1_xattn_Wo': _L1_xattn_in['Wo'], 'L1_xattn_bo': _L1_xattn_in['bo'], 'L1_ffn_Wr': _L1_ffn_in['Wr'], 'L1_ffn_W1': _L1_ffn_in['W1'], 'L1_ffn_b1': _L1_ffn_in['b1'], 'L1_ffn_Wo': _L1_ffn_in['Wo'], 'L1_ffn_bo': _L1_ffn_in['bo'], 'L1_ffn_gamma': _L1_ffn_in['gamma'], 'L1_ffn_beta': _L1_ffn_in['beta']}

def reference(x, ctx_1024, mask_Bx1xS2_if1, mask_Bx1xSxS2_ik0, L0_attn_gamma, L0_attn_beta, L0_attn_f_in_w, L0_attn_f_conv_w, L0_attn_f_conv_b, L0_attn_f_xproj_w, L0_attn_f_dt_w, L0_attn_f_dt_b, L0_attn_f_A_log, L0_attn_f_D, L0_attn_f_out_w, L0_attn_b_in_w, L0_attn_b_conv_w, L0_attn_b_conv_b, L0_attn_b_xproj_w, L0_attn_b_dt_w, L0_attn_b_dt_b, L0_attn_b_A_log, L0_attn_b_D, L0_attn_b_out_w, L0_xattn_Wq, L0_xattn_bq, L0_xattn_Wkv, L0_xattn_bkv, L0_xattn_Wout, L0_xattn_bout, L0_ffn_gate_w, L0_ffn_beta, L0_ffn_gate_proj_w, L0_ffn_up_proj_w, L0_ffn_down_proj_w, L0_ffn_shared_gate_w, L0_ffn_shared_up_w, L0_ffn_shared_down_w, L1_attn_wq, L1_attn_wk, L1_attn_wv, L1_attn_wo, L1_attn_q_norm_w, L1_attn_k_norm_w, L1_xattn_Wq, L1_xattn_bq, L1_xattn_Wk, L1_xattn_bk, L1_xattn_Wv, L1_xattn_bv, L1_xattn_Wo, L1_xattn_bo, L1_ffn_Wr, L1_ffn_W1, L1_ffn_b1, L1_ffn_Wo, L1_ffn_bo, L1_ffn_gamma, L1_ffn_beta):
    import jax
    import jax.numpy as jnp

    def _L0_attn_ref(x, gamma, beta, f_in_w, f_conv_w, f_conv_b, f_xproj_w, f_dt_w, f_dt_b, f_A_log, f_D, f_out_w, b_in_w, b_conv_w, b_conv_b, b_xproj_w, b_dt_w, b_dt_b, b_A_log, b_D, b_out_w):
        import jax, jax.numpy as jnp
        import numpy as np
        from functools import partial
        D_MODEL = 128
        D_STATE = 16
        D_CONV = 4
        EXPAND = 2
        D_INNER = EXPAND * D_MODEL
        DT_RANK = (D_MODEL + 15) // 16
        BATCH, SEQ = (2, 128)

        def _mamba_params(key):
            ks = jax.random.split(key, 9)
            s = lambda k, shape, scale: jax.random.normal(k, shape, jnp.float32) * scale
            return dict(in_w=s(ks[0], (2 * D_INNER, D_MODEL), D_MODEL ** (-0.5)), conv_w=s(ks[1], (D_INNER, 1, D_CONV), D_CONV ** (-0.5)), conv_b=s(ks[2], (D_INNER,), 0.02), xproj_w=s(ks[3], (DT_RANK + 2 * D_STATE, D_INNER), D_INNER ** (-0.5)), dt_w=s(ks[4], (D_INNER, DT_RANK), DT_RANK ** (-0.5)), dt_b=s(ks[5], (D_INNER,), 0.02), A_log=jnp.log(jnp.broadcast_to(jnp.arange(1, D_STATE + 1, dtype=jnp.float32), (D_INNER, D_STATE))), D=jnp.ones((D_INNER,), jnp.float32), out_w=s(ks[8], (D_MODEL, D_INNER), D_INNER ** (-0.5)))

        def _mamba(x, in_w, conv_w, conv_b, xproj_w, dt_w, dt_b, A_log, D, out_w):
            B, L, _ = x.shape
            xz = jnp.einsum('bld,ed->ble', x, in_w)
            u, z = jnp.split(xz, 2, axis=-1)
            u_c = jnp.swapaxes(u, 1, 2)
            u_c = jax.lax.conv_general_dilated(u_c, conv_w, window_strides=(1,), padding=[(D_CONV - 1, 0)], dimension_numbers=('NCH', 'OIH', 'NCH'), feature_group_count=D_INNER)
            u_c = u_c + conv_b[None, :, None]
            u = jax.nn.silu(jnp.swapaxes(u_c, 1, 2))
            x_dbl = jnp.einsum('bld,ed->ble', u, xproj_w)
            dt = jax.nn.softplus(jnp.einsum('blr,dr->bld', x_dbl[..., :DT_RANK], dt_w) + dt_b)
            Bm = x_dbl[..., DT_RANK:DT_RANK + D_STATE]
            Cm = x_dbl[..., DT_RANK + D_STATE:]
            A = -jnp.exp(A_log)
            dA = jnp.exp(dt[..., None] * A)
            dBu = dt[..., None] * Bm[:, :, None, :] * u[..., None]

            def step(h, ins):
                dA_t, dBu_t, C_t = ins
                h = dA_t * h + dBu_t
                y = jnp.einsum('bdn,bn->bd', h, C_t)
                return (h, y)
            h0 = jnp.zeros((B, D_INNER, D_STATE), dA.dtype)
            _, ys = jax.lax.scan(step, h0, (jnp.swapaxes(dA, 0, 1), jnp.swapaxes(dBu, 0, 1), jnp.swapaxes(Cm, 0, 1)))
            y = jnp.swapaxes(ys, 0, 1) + u * D
            y = y * jax.nn.silu(z)
            return jnp.einsum('bld,ed->ble', y, out_w)
        res = x
        mu = jnp.mean(x, axis=-1, keepdims=True)
        var = jnp.mean(jnp.square(x - mu), axis=-1, keepdims=True)
        xn = (x - mu) * jax.lax.rsqrt(var + 1e-05) * gamma + beta
        out_fwd = _mamba(xn, f_in_w, f_conv_w, f_conv_b, f_xproj_w, f_dt_w, f_dt_b, f_A_log, f_D, f_out_w)
        out_bwd = _mamba(xn[:, ::-1, :], b_in_w, b_conv_w, b_conv_b, b_xproj_w, b_dt_w, b_dt_b, b_A_log, b_D, b_out_w)[:, ::-1, :]
        return res + out_fwd + out_bwd

    def _L0_xattn_ref(x, memory, memory_mask, Wq, bq, Wkv, bkv, Wout, bout):
        import jax, jax.numpy as jnp
        import numpy as np
        B, T1, T2, NFEAT, H = (8, 64, 1500, 128, 16)
        DK = NFEAT // H
        b, t1, _ = x.shape
        t2 = memory.shape[1]
        q = x @ Wq + bq
        kv = memory @ Wkv + bkv
        k, v = jnp.split(kv, 2, axis=-1)
        q_h = q.reshape(b, t1, H, DK).transpose(0, 2, 1, 3)
        k_h = k.reshape(b, t2, H, DK).transpose(0, 2, 1, 3)
        v_h = v.reshape(b, t2, H, DK).transpose(0, 2, 1, 3)
        q_h = q_h * DK ** (-0.5)
        scores = jnp.einsum('bhqd,bhkd->bhqk', q_h, k_h)
        mask0 = memory_mask[:, None, :, :] == 0
        scores = jnp.where(mask0, -jnp.inf, scores)
        attn = jax.nn.softmax(scores, axis=-1)
        attn = jnp.where(mask0, 0.0, attn)
        ctx = jnp.einsum('bhqk,bhkd->bhqd', attn, v_h)
        ctx = ctx.transpose(0, 2, 1, 3).reshape(b, t1, H * DK)
        return ctx @ Wout + bout

    def _L0_ffn_ref(x, gate_w, beta, gate_proj_w, up_proj_w, down_proj_w, shared_gate_w, shared_up_w, shared_down_w):
        import jax, jax.numpy as jnp
        import numpy as np
        E = 8
        H = 128
        M = 256
        K = 2
        SE = 1
        BSZ, SEQ = (2, 128)
        W_SCALE = 0.02
        B0, S0, H0 = x.shape
        xt = x.reshape(-1, H0)
        B = xt.shape[0]
        logits = xt @ gate_w.T
        _, idx = jax.lax.top_k(logits + beta, K)
        probs = jax.nn.sigmoid(jnp.take_along_axis(logits, idx, axis=-1))
        c = jnp.zeros((B, E), xt.dtype).at[jnp.arange(B)[:, None], idx].add(probs)
        g = jnp.einsum('bh,ehm->bem', xt, gate_proj_w)
        u = jnp.einsum('bh,ehm->bem', xt, up_proj_w)
        h = jax.nn.silu(g) * u
        eo = jnp.einsum('bem,emh->beh', h, down_proj_w)
        combined = jnp.einsum('beh,be->bh', eo, c)
        sg = jnp.einsum('bh,ehm->bem', xt, shared_gate_w)
        su = jnp.einsum('bh,ehm->bem', xt, shared_up_w)
        sh = jax.nn.silu(sg) * su
        shared_out = jnp.einsum('bem,emh->beh', sh, shared_down_w).sum(axis=1)
        return (combined + shared_out).reshape(B0, S0, H0)

    def _L1_attn_ref(x, wq, wk, wv, wo, q_norm_w, k_norm_w):
        import jax, jax.numpy as jnp
        import numpy as np
        DIM, H, KV, HD, WIN = (128, 16, 4, 64, 64)
        EPS = 1e-06

        def rmsnorm(x, w, eps=EPS):
            return x * jax.lax.rsqrt(jnp.mean(x * x, axis=-1, keepdims=True) + eps) * w
        B, T, D = x.shape
        rep = H // KV
        q = (x @ wq.T).reshape(B, T, H, HD)
        k = (x @ wk.T).reshape(B, T, KV, HD)
        v = (x @ wv.T).reshape(B, T, KV, HD)
        q = rmsnorm(q, q_norm_w)
        k = rmsnorm(k, k_norm_w)
        k = jnp.repeat(k, rep, axis=2)
        v = jnp.repeat(v, rep, axis=2)
        scores = jnp.einsum('bqhd,bkhd->bhqk', q, k) / jnp.sqrt(jnp.float32(HD))
        i = jnp.arange(T)[:, None]
        j = jnp.arange(T)[None, :]
        mask = (i >= j) & (i - j < WIN)
        scores = jnp.where(mask, scores, -jnp.inf)
        attn = jax.nn.softmax(scores, axis=-1)
        y = jnp.einsum('bhqk,bkhd->bqhd', attn, v).reshape(B, T, H * HD)
        return y @ wo.T

    def _L1_xattn_ref(Q, K, V, mask, Wq, bq, Wk, bk, Wv, bv, Wo, bo):
        import jax, jax.numpy as jnp
        import numpy as np
        D_MODEL = 128
        NUM_HEADS = 16
        BATCH = 2
        SEQ = 256
        NEG_INF = -1000000000.0

        def _split_heads(x):
            b, s, d = x.shape
            return x.reshape(b, s, NUM_HEADS, d // NUM_HEADS).transpose(0, 2, 1, 3)
        q = _split_heads(Q @ Wq.T + bq)
        k = _split_heads(K @ Wk.T + bk)
        v = _split_heads(V @ Wv.T + bv)
        d_k = q.shape[-1]
        scores = jnp.einsum('bhqd,bhkd->bhqk', q, k) / jnp.sqrt(jnp.float32(d_k))
        scores = jnp.where(mask == 0, jnp.float32(NEG_INF), scores)
        weights = jax.nn.softmax(scores, axis=-1)
        out = jnp.einsum('bhqk,bhkd->bhqd', weights, v)
        b, h, s, dk = out.shape
        out = out.transpose(0, 2, 1, 3).reshape(b, s, h * dk)
        return out @ Wo.T + bo

    def _L1_ffn_ref(hidden_states, Wr, W1, b1, Wo, bo, gamma, beta):
        import jax, jax.numpy as jnp
        import numpy as np
        LN_EPS = 1e-12
        B, S, H = hidden_states.shape
        E = Wr.shape[0]
        x = hidden_states.reshape(-1, H)
        router_logits = x @ Wr.T
        expert_idx = jnp.argmax(jax.nn.softmax(router_logits, axis=-1), axis=-1)
        inter = jnp.zeros((x.shape[0], W1.shape[2]), dtype=x.dtype)
        for e in range(E):
            mask = (expert_idx == e)[:, None].astype(x.dtype)
            inter = inter + mask * jax.nn.gelu(x @ W1[e] + b1[e], approximate=False)
        y = inter @ Wo + bo + x
        mu = jnp.mean(y, axis=-1, keepdims=True)
        var = jnp.mean(jnp.square(y - mu), axis=-1, keepdims=True)
        out = (y - mu) * jax.lax.rsqrt(var + LN_EPS) * gamma + beta
        return out.reshape(B, S, H)
    x = x + _L0_attn_ref(_layernorm(x, axis=-1), L0_attn_gamma, L0_attn_beta, L0_attn_f_in_w, L0_attn_f_conv_w, L0_attn_f_conv_b, L0_attn_f_xproj_w, L0_attn_f_dt_w, L0_attn_f_dt_b, L0_attn_f_A_log, L0_attn_f_D, L0_attn_f_out_w, L0_attn_b_in_w, L0_attn_b_conv_w, L0_attn_b_conv_b, L0_attn_b_xproj_w, L0_attn_b_dt_w, L0_attn_b_dt_b, L0_attn_b_A_log, L0_attn_b_D, L0_attn_b_out_w)
    x = x + _L0_xattn_ref(_layernorm(x, axis=-1), ctx_1024, mask_Bx1xS2_if1, L0_xattn_Wq, L0_xattn_bq, L0_xattn_Wkv, L0_xattn_bkv, L0_xattn_Wout, L0_xattn_bout)
    x = x + _L0_ffn_ref(_layernorm(x, axis=-1), L0_ffn_gate_w, L0_ffn_beta, L0_ffn_gate_proj_w, L0_ffn_up_proj_w, L0_ffn_down_proj_w, L0_ffn_shared_gate_w, L0_ffn_shared_up_w, L0_ffn_shared_down_w)
    x = x + _L1_attn_ref(_layernorm(x, axis=-1), L1_attn_wq, L1_attn_wk, L1_attn_wv, L1_attn_wo, L1_attn_q_norm_w, L1_attn_k_norm_w)
    x = x + _L1_xattn_ref(_layernorm(x, axis=-1), ctx_1024, ctx_1024, mask_Bx1xSxS2_ik0, L1_xattn_Wq, L1_xattn_bq, L1_xattn_Wk, L1_xattn_bk, L1_xattn_Wv, L1_xattn_bv, L1_xattn_Wo, L1_xattn_bo)
    x = x + _L1_ffn_ref(_layernorm(x, axis=-1), L1_ffn_Wr, L1_ffn_W1, L1_ffn_b1, L1_ffn_Wo, L1_ffn_bo, L1_ffn_gamma, L1_ffn_beta)
    return x

_drawn_inputs = setup_inputs


def setup_inputs(seed=0):
    import zlib

    import numpy as np

    out = dict(_drawn_inputs(seed))
    spreads = {'L0_attn_gamma': (1.0, 0.2),
     'L0_attn_beta': (0.0, 0.1),
     'L0_attn_f_D': (1.0, 0.2),
     'L0_attn_b_D': (1.0, 0.2),
     'L0_xattn_bq': (0.0, 0.8),
     'L0_xattn_bkv': (0.0, 0.609),
     'L0_xattn_bout': (0.0, 0.1),
     'L0_ffn_beta': (0.0, 0.8),
     'L1_attn_q_norm_w': (1.0, 0.6),
     'L1_attn_k_norm_w': (1.0, 0.6),
     'L1_ffn_gamma': (1.0, 0.6),
     'L1_ffn_beta': (0.0, 0.797)}
    factors = {'L0_attn_f_conv_b': 4.965,
     'L0_attn_f_dt_b': 8.0,
     'L0_attn_b_conv_b': 5.245,
     'L0_attn_b_dt_b': 8.0,
     'L0_xattn_Wq': 8.0,
     'L0_xattn_Wkv': 4.125,
     'L0_xattn_Wout': 3.494,
     'L0_ffn_gate_w': 8.0,
     'L0_ffn_gate_proj_w': 8.0,
     'L0_ffn_up_proj_w': 8.0,
     'L0_ffn_down_proj_w': 8.0,
     'L0_ffn_shared_gate_w': 8.0,
     'L0_ffn_shared_up_w': 8.0,
     'L0_ffn_shared_down_w': 8.0,
     'L1_attn_wq': 28.192,
     'L1_attn_wk': 28.144,
     'L1_xattn_bq': 18.722,
     'L1_xattn_bk': 64.0,
     'L1_ffn_b1': 31.779,
     'L1_ffn_bo': 20.311,
     'L1_attn_wv': 7.091,
     'L1_attn_wo': 7.103,
     'L1_xattn_bv': 4.818,
     'L1_xattn_bo': 4.855,
     'L1_ffn_Wr': 2.691,
     'L1_ffn_W1': 2.952}
    for name, (base, spread) in spreads.items():
        noise = np.random.default_rng([zlib.crc32(name.encode()), seed]).standard_normal(out[name].shape)
        drawn = base * np.exp(spread * noise) if base else spread * noise
        out[name] = jnp.asarray(drawn.astype(out[name].dtype))
    for name, factor in factors.items():
        out[name] = (out[name] * factor).astype(out[name].dtype)
    return out
```

```python
from contextlib import ExitStack

import numpy as np

import concourse.bass as bass
from concourse import mybir

F32 = mybir.dt.float32
F32R = mybir.dt.float32r
BF16 = mybir.dt.bfloat16
I32 = mybir.dt.int32
ALU = mybir.AluOpType
ACT = mybir.ActivationFunctionType
AX = mybir.AxisListType

NB, T, D = 32, 128, 128
TC = 77
GS = 4
NG = NB // GS
GT = GS * T
LN_EPS = 1e-5
LN_STEPS = 10

DI, NS, DR, TAPS = 256, 16, 8, 4
CH = DI // 128
PAD = TAPS - 1

HX, DKX = 16, 8
HL, KVL, HDL, WIN = 16, 4, 64, 64
QH = 4
NQ = HX // QH
W4 = QH * DKX

E0, M0, K0 = 8, 256, 2
E1, M1 = 8, 512

MASKED = -1.0e30


def due(count):
    return not isinstance(count, int) or count > 0


class Alloc:

    def __init__(self, nc, ctx, prefix):
        self.nc, self.ctx, self.prefix = nc, ctx, prefix
        self.sems = []
        ctx.callback(self.clear)

    def clear(self):
        if self.sems:
            self.nc.clear_and_free_semaphores(self.sems)
            self.nc.all_engine_barrier()

    def sb(self, name, shape, dt=F32):
        return self.ctx.enter_context(self.nc.sbuf_tensor(self.prefix + name, shape, dt))

    def ps(self, name, shape, dt=F32):
        return self.ctx.enter_context(self.nc.psum_tensor(self.prefix + name, shape, dt))

    def sem(self, name):
        self.sems.append(self.nc.alloc_semaphore(self.prefix + name))
        return self.sems[-1]


def seqs(t, g):
    return t[:, bass.ts(g, GS)]


def bc(ap, axis, n):
    a = ap.unsqueeze(axis)
    shape = list(a.shape)
    shape[axis] = n
    return a.to_broadcast(shape)


class Shared:

    def __init__(self, nc, A):
        self.nc = nc
        self.x = A.sb("x", [128, NB, D])
        self.bn = A.sb("bn", [128, NB, 6])
        self.mean, self.var, self.rstd = (A.sb(n, [128, NB]) for n in ("mean", "var", "rstd"))
        self.t0, self.t1 = A.sb("t0", [128, NB]), A.sb("t1", [128, NB])
        self.minus_half = A.sb("minus_half", [128, 128])
        self.ident = A.sb("ident", [128, 128])
        self.ident_bf = A.sb("ident_bf", [128, 128], BF16)

    def next_stats(self, dve, g, sem):
        for i in range(GS):
            b = bass.ds(g * GS + i, 1)
            ins = self.nc.vector.bn_stats(self.bn[:, b, :], self.x[:, b, :])
        ins.then_inc(sem, 1)

    def ln_scalars(self, pool, sem, eps):
        P = self.nc.gpsimd
        me, mo, qe, qo = (self.bn[:, :, k] for k in (1, 4, 2, 5))
        P.tensor_tensor(self.t0[:, :], me, mo, ALU.add).then_inc(sem, 1)
        pool.wait_ge(sem, 1)
        P.tensor_tensor(self.t1[:, :], me, mo, ALU.subtract).then_inc(sem, 1)
        pool.wait_ge(sem, 2)
        P.tensor_scalar(self.mean[:, :], self.t0[:, :], 0.5, None, ALU.mult).then_inc(sem, 1)
        pool.wait_ge(sem, 3)
        P.tensor_scalar(self.t1[:, :], self.t1[:, :], 0.5, None, ALU.mult).then_inc(sem, 1)
        pool.wait_ge(sem, 4)
        P.tensor_tensor(self.t0[:, :], qe, qo, ALU.add).then_inc(sem, 1)
        pool.wait_ge(sem, 5)
        P.tensor_tensor(self.t1[:, :], self.t1[:, :], self.t1[:, :], ALU.mult).then_inc(sem, 1)
        pool.wait_ge(sem, 6)
        P.tensor_scalar(self.t0[:, :], self.t0[:, :], 1.0 / D, None, ALU.mult).then_inc(sem, 1)
        pool.wait_ge(sem, 7)
        P.tensor_tensor(self.var[:, :], self.t0[:, :], self.t1[:, :], ALU.add).then_inc(sem, 1)
        pool.wait_ge(sem, 8)
        P.tensor_scalar(self.t0[:, :], self.var[:, :], eps, None, ALU.add).then_inc(sem, 1)
        pool.wait_ge(sem, 9)
        P.tensor_tensor(self.rstd[:, :], self.t0[:, :], self.minus_half[:, 0:NB], ALU.pow).then_inc(sem, 1)
        pool.wait_ge(sem, 10)


def load_layer(nc, S, x_d, ident_d):
    with ExitStack() as ctx:
        A = Alloc(nc, ctx, "l_")
        x_in = [A.sem(f"x_in{k}") for k in range(NG)]
        ident_in, ident_ready, half, stats = A.sem("ident_in"), A.sem("ident_ready"), A.sem("half"), A.sem("stats")
        with nc.Block() as block:

            @block.sync
            def _(sp):
                for g in range(NG):
                    sp.dma_start(S.x[:, g * GS:(g + 1) * GS, :],
                                 x_d[g * GS:(g + 1) * GS].rearrange("b t d -> t b d")).then_inc(x_in[g], 16)
                sp.dma_start(S.ident[:, :], ident_d).then_inc(ident_in, 16)

            @block.gpsimd
            def _(pool):
                nc.gpsimd.memset(S.minus_half[:, :], -0.5).then_inc(half, 1)

            @block.vector
            def _(dve):
                for g in range(NG):
                    dve.wait_ge(x_in[g], 16)
                    S.next_stats(dve, g, stats)
                dve.wait_ge(ident_in, 16)
                nc.vector.tensor_copy(S.ident_bf[:, :], S.ident[:, :]).then_inc(ident_ready, 1)


def walk_groups(eng, body):
    body(0, 0)
    body(1, 1)
    with eng.Fori(1, NG // 2) as j:
        body(2 * j, 0)
        body(2 * j + 1, 1)


def split_pass(mm, out, w_hi, w_lo, x_hi, x_lo, start, stop):
    mm(out, w_hi, x_hi, start=start, stop=False)
    mm(out, w_hi, x_lo, start=False, stop=False)
    return mm(out, w_lo, x_hi, start=False, stop=stop)


class Seq:

    def __init__(self, j, p):
        self.j, self.p = j, p
        self.n = 2 * j + p

    def plus(self, k):
        return Seq(self.j + (self.p + k) // 2, (self.p + k) % 2)

    def real(self):
        return not isinstance(self.n, int) or 0 <= self.n < NB

    def quad(self, q):
        return NQ * self.n + q


def walk_sequences(eng, slot, ahead=2):
    turns = (ahead + 1) // 2
    def both(j):
        for p in range(2):
            for q in range(NQ):
                slot(Seq(j, p), q)
    for j in range(-turns, 1):
        both(j)
    with eng.Fori(1, NB // 2 - turns) as j:
        both(j)
    for j in range(NB // 2 - turns, NB // 2 + 1):
        both(j)


def mamba_layer(nc, S, w):
    NROW = 3 * 2 * NS + DR
    LAG, HCB = 2, 4
    with ExitStack() as ctx:
        A = Alloc(nc, ctx, "m_")
        convw = A.sb("convw", [128, 2, TAPS, DI])
        win_u = A.sb("win_u", [128, 2, DI])
        wtap = A.sb("wtap", [128, 2, TAPS, DI])
        win_z = A.sb("win_z", [128, 2, DI])
        convb = A.sb("convb", [128, 2, CH])
        xproj = A.sb("xproj", [128, 2, CH, NROW])
        dtw = A.sb("dtw", [128, 2, DI])
        dtb = A.sb("dtb", [128, 2, CH])
        alog = A.sb("alog", [128, 2, CH, NS])
        aexp = A.sb("aexp", [128, 2, CH, NS])
        aneg = A.sb("aneg", [128, 2, CH, NS])
        dskip = A.sb("dskip", [128, 2, CH])
        outw = A.sb("outw", [128, 2, CH, D])
        gamma = A.sb("gamma", [128, 1])
        beta = A.sb("beta", [128, 1])
        sel32 = A.sb("sel32", [96, 2 * NS])
        sel = A.sb("sel", [96, 2 * NS, 128], BF16)
        ve = A.sb("ve", [128, NB])
        r1sq = A.sb("r1sq", [128, NB])
        v2 = A.sb("v2", [128, NB])
        r2 = A.sb("r2", [128, NB])
        r12 = A.sb("r12", [128, NB])
        r1p = A.sb("r1p", [128, NB])
        mr1 = A.sb("mr1", [128, NB])
        xh = A.sb("xh", [128, GS, D])
        xnT = A.sb("xnT", [128, 2, GS, T + 2 * PAD])
        us = [A.sb(f"us{d}", [128, CH, GT]) for d in range(2)]
        zraw = A.sb("zraw", [128, CH, GT])
        zs = [A.sb(f"zs{d}", [128, CH, GT]) for d in range(2)]
        bcrow = [A.sb(f"bcrow{d}", [96, GT], BF16) for d in range(2)]
        rest = A.sb("rest", [96, GT])
        dtrow = A.sb("dtrow", [128, GT])
        pre = A.sb("pre", [128, CH, GT])
        soft = A.sb("soft", [128, CH, GT])
        relu = A.sb("relu", [128, CH, GT])
        dt = [A.sb(f"dt{d}", [128, CH, GT]) for d in range(2)]
        du = [A.sb(f"du{d}", [128, CH, GT]) for d in range(2)]
        da = [[A.sb(f"da{d}{k}", [128, CH * GS, T]) for k in range(2)] for d in range(2)]
        db = [A.sb(f"db{k}", [128, CH, GT]) for k in range(2)]
        h = [A.sb(f"h{k}", [128, CH, GT]) for k in range(2)]
        cs = [A.sb(f"cs{k}", [128, GT]) for k in range(2)]
        hc = [A.sb(f"hc{k}", [128, CH, GT]) for k in range(HCB)]
        y1 = A.sb("y1", [128, CH, GT])
        ys = A.sb("ys", [128, CH, GT])
        pb = [A.ps(f"pb{k}", [128, GT]) for k in range(2)]
        pc = [A.ps(f"pc{k}", [128, GT]) for k in range(2)]
        py = A.ps("py", [128, CH, GT])
        pm = [A.ps(f"pm{k}", [128, GT]) for k in range(2)]

        names = """weights prep stats rstd xh_ready xres_ready lnT_mm lnT_ready z_mm z_raw u_mm silu_ready
            row_mm row_hi row_rest row_mid row_ready dtrow_ready dt_mm dt_abs dt_relu dt_soft dt_ready
            du_ready b_mm c_mm c_ready da_ready db_ready h_ready hc_ready y_mm y1_ready ys_ready o_mm
            x_ready seg_zero aexp_ready""".split()
        s = {n: A.sem(n) for n in names}

        with nc.Block() as block:

            @block.sync
            def _(sp):
                for d, p in enumerate("fb"):
                    for dst, src in ((convw[:, d], w[p + "conv_w"].partition_broadcast(128)),
                                     (win_u[:, d], w[p + "in_wT"][:, 0:DI]),
                                     (win_z[:, d], w[p + "in_wT"][:, DI:2 * DI]),
                                     (convb[:, d], w[p + "conv_b"]),
                                     (xproj[:, d], w[p + "xprojT"]),
                                     (dtw[96:96 + DR, d], w[p + "dt_wT"]),
                                     (dtb[:, d], w[p + "dt_b"]),
                                     (alog[:, d], w[p + "A_log"]),
                                     (dskip[:, d], w[p + "D"]),
                                     (outw[:, d], w[p + "out_wT"])):
                        sp.dma_start(dst, src).then_inc(s["weights"], 16)
                sp.dma_start(gamma[:, :], w["gamma"]).then_inc(s["weights"], 16)
                sp.dma_start(beta[:, :], w["beta"]).then_inc(s["weights"], 16)
                sp.dma_start(sel32[:, :], w["sel32"]).then_inc(s["weights"], 16)

            W_ALL = 16 * 23


            def drive(eng, front, scan, par):
                def group(g, p, last=False):
                    def nxt1(n):
                        par[0] = p
                        front(g, 1, at=n)

                    def nxt0(n):
                        par[0] = 1 - p
                        front(g + 1, 0, at=n)
                    scan(g, 0, nxt1)
                    scan(g, 1, None if last else nxt0)
                par[0] = 0
                front(0, 0)
                group(0, 0)
                group(1, 1)
                with eng.Fori(1, NG // 2 - 1) as j:
                    group(2 * j, 0)
                    group(2 * j + 1, 1)
                group(NG - 2, 0)
                group(NG - 1, 1, last=True)

            @block.tensor
            def _(pe):
                mm, tr = nc.tensor.matmul, nc.tensor.transpose
                pe.wait_ge(s["weights"], W_ALL)
                pe.wait_ge(s["prep"], 2)

                def front(g, d, at=None):
                    u = 2 * g + d
                    if d == 0 and at in (None, 0):
                        pe.wait_ge(s["xh_ready"], g + 1)
                        if due(u - 1):
                            pe.wait_ge(s["x_ready"], u - 1)
                        for i in range(GS):
                            last = tr(pm[0][:, i * T:(i + 1) * T], xh[:, i, :], S.ident[:, :])
                        last.then_inc(s["lnT_mm"], 1)
                    if at in (None, 2):
                        pe.wait_ge(s["lnT_ready"], g + 1)
                        if due(CH * u):
                            pe.wait_ge(s["dt_relu"], CH * u)
                        if due(CH * u):
                            pe.wait_ge(s["dt_abs"], CH * u)
                        rhs = xnT[:, par[0], :, PAD:PAD + T]
                        if due(u - 1):
                            pe.wait_ge(s["x_ready"], u - 1)
                        for c in range(CH):
                            mm(pm[1 - c][:, :], win_z[:, d, c * 128:(c + 1) * 128], rhs,
                               start=True, stop=True).then_inc(s["z_mm"], 1)
                    if at in (None, 3, 4):
                        for c in range(CH):
                            if at is not None and at != 3 + c:
                                continue
                            pe.wait_ge(s["z_raw"], CH * u + c + 1)
                            for k in range(TAPS):
                                off = k if d == 0 else 2 * PAD - k
                                ins = mm(pm[1 - c][:, :], wtap[:, d, k, c * 128:(c + 1) * 128],
                                         xnT[:, par[0], :, off:off + T],
                                         start=k == 0, stop=k == TAPS - 1)
                            ins.then_inc(s["u_mm"], 1)
                    if at in (None, 7):
                        pe.wait_ge(s["silu_ready"], 3 * u + 2)
                        for c in range(CH):
                            ins = mm(pm[1][0:NROW, :], xproj[:, d, c, :], us[d][:, c, :],
                                     start=c == 0, stop=c == CH - 1)
                        ins.then_inc(s["row_mm"], 1)
                    if at in (None, 10):
                        pe.wait_ge(s["dtrow_ready"], u + 1)
                        for c in range(CH):
                            if c == 1:
                                pe.wait_ge(s["row_rest"], u + 1)
                            mm(pm[c][:, :], dtw[96:96 + DR, d, c * 128:(c + 1) * 128],
                               dtrow[96:96 + DR, :], start=True, stop=True).then_inc(s["dt_mm"], 1)

                par = [0]

                def spread(u, n, d):
                    N = NS * u + n
                    if n == 0:
                        pe.wait_ge(s["row_ready"], u + 1)
                    if due(N - 1):
                        pe.wait_ge(s["db_ready"], N - 1)
                    mm(pb[n % 2][:, :], sel[:, n, :], bcrow[d][:, :],
                       start=True, stop=True).then_inc(s["b_mm"], 1)
                    if due(N - 1):
                        pe.wait_ge(s["c_ready"], N - 1)
                    mm(pc[n % 2][:, :], sel[:, NS + n, :], bcrow[d][:, :],
                       start=True, stop=True).then_inc(s["c_mm"], 1)

                def add_state(u, n):
                    pe.wait_ge(s["hc_ready"], NS * u + n + 1)
                    if n == 0:
                        if due(CH * u):
                            pe.wait_ge(s["y1_ready"], CH * u)
                    for c in range(CH):
                        ins = mm(py[:, c, :], S.ident[:, :], hc[n % HCB][:, c, :],
                                 start=n == 0, stop=n == NS - 1)
                    ins.then_inc(s["y_mm"], 1)

                def scan(g, d, nxt):
                    u = 2 * g + d
                    spread(u, 0, d)
                    for n in range(NS + LAG):
                        if n + 1 < NS:
                            spread(u, n + 1, d)
                        if nxt:
                            nxt(n)
                        if n >= LAG:
                            add_state(u, n - LAG)
                    pe.wait_ge(s["ys_ready"], u + 1)
                    if nxt:
                        pe.wait_ge(s["dt_abs"], CH * (u + 1) + 1)
                        pe.wait_ge(s["dt_relu"], CH * (u + 1) + 1)
                    for i in range(GS):
                        for c in range(CH):
                            ins = mm(pm[0][:, i * D:(i + 1) * D], ys[:, c, i * T:(i + 1) * T],
                                     outw[:, d, c, :], start=c == 0, stop=c == CH - 1)
                    ins.then_inc(s["o_mm"], 1)

                drive(pe, front, scan, par)

            @block.scalar
            def _(act):
                A_ = nc.scalar.activation
                act.wait_ge(s["weights"], W_ALL)
                A_(aexp[:, :, :, :], alog[:, :, :, :], ACT.Exp).then_inc(s["aexp_ready"], 1)
                act.wait_ge(s["prep"], 3)
                act.wait_ge(s["seg_zero"], 5)
                par = [0]

                def front(g, d, at=None):
                    u = 2 * g + d
                    if d == 0 and at in (None, 1):
                        act.wait_ge(s["lnT_mm"], g + 1)
                        if due(2 * CH * (g - 1)):
                            act.wait_ge(s["u_mm"], 2 * CH * (g - 1))
                        A_(xnT[:, par[0], :, PAD:PAD + T], pm[0][:, :].rearrange("p (i t) -> p i t", t=T),
                           ACT.Identity, bias=beta[:, 0:1], scale=gamma[:, 0:1]).then_inc(s["lnT_ready"], 1)
                    if at in (None, 6):
                        if due(u - 1):
                            act.wait_ge(s["ys_ready"], u - 1)
                        for c in range(CH):
                            act.wait_ge(s["u_mm"], CH * u + c + 1)
                            A_(us[d][:, c, :], pm[1 - c][:, :], ACT.Silu,
                               bias=convb[:, d, c:c + 1]).then_inc(s["silu_ready"], 1)
                        act.wait_ge(s["z_raw"], CH * u + CH)
                        A_(zs[d][:, :, :], zraw[:, :, :], ACT.Silu).then_inc(s["silu_ready"], 1)
                    if at in (None, 8):
                        act.wait_ge(s["row_mm"], u + 1)
                        if due(CH * u):
                            act.wait_ge(s["dt_mm"], CH * u)
                        A_(dtrow[96:96 + DR, :], pm[1][96:96 + DR, :], ACT.Copy).then_inc(s["dtrow_ready"], 1)
                        if due(NS * (u - 1)):
                            act.wait_ge(s["c_mm"], NS * (u - 1))
                        A_(bcrow[d][0:96, :], pm[1][0:96, :], ACT.Copy).then_inc(s["row_hi"], 1)
                    if at in (None, 10):
                        act.wait_ge(s["row_rest"], u + 1)
                        for q in (1, 2):
                            A_(bcrow[d][32 * q:32 * q + 32, :], rest[32 * q:32 * q + 32, :],
                               ACT.Copy).then_inc(s["row_mid"], 1)
                    if at in (None, 11):
                        for c in range(CH):
                            act.wait_ge(s["dt_mm"], CH * u + c + 1)
                            if c == 0:
                                if due(u):
                                    act.wait_ge(s["dt_ready"], u)
                            A_(pre[:, c, :], pm[c][:, :], ACT.Abs,
                               bias=dtb[:, d, c:c + 1]).then_inc(s["dt_abs"], 1)
                        act.wait_ge(s["dt_abs"], CH * (u + 1))
                        if due(2 * u):
                            act.wait_ge(s["dt_soft"], 2 * u)
                        A_(soft[:, :, :], pre[:, :, :], ACT.Exp, scale=-1.0).then_inc(s["dt_soft"], 1)
                        act.wait_ge(s["dt_soft"], 2 * u + 1)
                        A_(pre[:, :, :], soft[:, :, :], ACT.Ln, bias=1.0).then_inc(s["dt_soft"], 1)

                def scan(g, d, nxt):
                    u = 2 * g + d
                    lo = 1 - d
                    for n in range(NS):
                        N = NS * u + n
                        act.wait_ge(s["c_mm"], N + 1)
                        if due(N - 1):
                            act.wait_ge(s["hc_ready"], N - 1)
                        A_(cs[n % 2][:, :], pc[n % 2][:, :], ACT.Copy).then_inc(s["c_ready"], 1)
                        if n == 0:
                            act.wait_ge(s["dt_ready"], u + 1)
                        if due(N - 1):
                            act.wait_ge(s["h_ready"], N - 1)
                        for c in range(CH):
                            dst = da[d][n % 2][:, c * GS:(c + 1) * GS, lo:lo + T - 1]
                            src = dt[d][:, c, :].rearrange("p (i t) -> p i t", t=T)[:, :, lo:lo + T - 1]
                            A_(dst, src, ACT.Exp, scale=aneg[:, d, c, n:n + 1]).then_inc(s["da_ready"], 1)
                        if nxt:
                            nxt(n)

                drive(act, front, scan, par)

            @block.vector
            def _(dve):
                V = nc.vector
                dve.wait_ge(s["weights"], W_ALL)
                for d in range(2):
                    ins = V.tensor_tensor(wtap[:, d], convw[:, d], bc(win_u[:, d], 1, TAPS), ALU.mult)
                ins.then_inc(s["prep"], 1)
                V.tensor_copy(sel[:, :, :], bc(sel32[:, :], 2, 128)).then_inc(s["prep"], 1)
                dve.wait_ge(s["aexp_ready"], 1)
                V.tensor_scalar(aneg[:, :, :, :], aexp[:, :, :, :], -1.0, None, ALU.mult).then_inc(s["prep"], 1)
                dve.wait_ge(s["rstd"], LN_STEPS + 7)
                par = [0]

                def front(g, d, at=None):
                    u = 2 * g + d
                    if d == 0 and at in (None, 0):
                        if due(g):
                            dve.wait_ge(s["lnT_mm"], g)
                        for i in range(GS):
                            b = bass.ds(g * GS + i, 1)
                            ins = V.tensor_scalar(xh[:, i:i + 1, :], S.x[:, b, :], S.mean[:, b],
                                                  r12[:, b], ALU.subtract, ALU.mult)
                        ins.then_inc(s["xh_ready"], 1)
                        dve.wait_ge(s["xh_ready"], g + 1)
                        for i in range(GS):
                            b = bass.ds(g * GS + i, 1)
                            ins = V.tensor_scalar(S.x[:, b, :], S.x[:, b, :], r1p[:, b], mr1[:, b],
                                                  ALU.mult, ALU.subtract)
                        ins.then_inc(s["xres_ready"], 1)
                    if at in (None, 2):
                        if due(3 * u):
                            dve.wait_ge(s["silu_ready"], 3 * u)
                        for c in range(CH):
                            dve.wait_ge(s["z_mm"], CH * u + c + 1)
                            V.tensor_copy(zraw[:, c, :], pm[1 - c][:, :]).then_inc(s["z_raw"], 1)
                    if at in (None, 9):
                        dve.wait_ge(s["row_hi"], u + 1)
                        if due(2 * u):
                            dve.wait_ge(s["row_mid"], 2 * u)
                        if due(u):
                            dve.wait_ge(s["row_ready"], u)
                        V.tensor_tensor(rest[0:96, :], pm[1][0:96, :], bcrow[d][0:96, :],
                                        ALU.subtract).then_inc(s["row_rest"], 1)
                    if at in (None, 11):
                        dve.wait_ge(s["row_mid"], 2 * u + 2)
                        V.tensor_tensor(bcrow[d][64:96, :], rest[64:96, :], bcrow[d][64:96, :],
                                        ALU.subtract).then_inc(s["row_ready"], 1)
                    if at in (None, 12):
                        if due(u):
                            dve.wait_ge(s["dt_ready"], u)
                        for c in range(CH):
                            dve.wait_ge(s["dt_mm"], CH * u + c + 1)
                            dve.wait_ge(s["dt_abs"], CH * u + c + 1)
                            V.tensor_scalar(relu[:, c, :], pm[c][:, :], dtb[:, d, c:c + 1], 0.0,
                                            ALU.add, ALU.max).then_inc(s["dt_relu"], 1)
                    if at in (None, 13):
                        dve.wait_ge(s["dt_relu"], CH * (u + 1))
                        if due(u - 1):
                            dve.wait_ge(s["du_ready"], u - 1)
                        dve.wait_ge(s["dt_soft"], 2 * u + 2)
                        if due(CH * NS * (u - 1)):
                            dve.wait_ge(s["da_ready"], CH * NS * (u - 1))
                        V.tensor_tensor(dt[d][:, :, :], relu[:, :, :], pre[:, :, :],
                                        ALU.add).then_inc(s["dt_ready"], 1)
                    if at in (None, 14):
                        dve.wait_ge(s["dt_ready"], u + 1)
                        dve.wait_ge(s["silu_ready"], 3 * u + CH)
                        if due(NS * (u - 1)):
                            dve.wait_ge(s["db_ready"], NS * (u - 1))
                        V.tensor_tensor(du[d][:, :, :], dt[d][:, :, :], us[d][:, :, :],
                                        ALU.mult).then_inc(s["du_ready"], 1)

                def step(u, n, d):
                    N = NS * u + n
                    if n == 0:
                        dve.wait_ge(s["du_ready"], u + 1)
                    dve.wait_ge(s["b_mm"], N + 1)
                    if due(N - 1):
                        dve.wait_ge(s["h_ready"], N - 1)
                    V.tensor_tensor(db[n % 2][:, :, :], du[d][:, :, :], bc(pb[n % 2][:, :], 1, CH),
                                    ALU.mult).then_inc(s["db_ready"], 1)

                def scan(g, d, nxt):
                    u = 2 * g + d
                    step(u, 0, d)
                    for n in range(NS):
                        N = NS * u + n
                        if n + 1 < NS:
                            step(u, n + 1, d)
                        if nxt:
                            nxt(n)
                        dve.wait_ge(s["da_ready"], CH * (N + 1))
                        dve.wait_ge(s["db_ready"], N + 1)
                        if due(N - 1):
                            dve.wait_ge(s["hc_ready"], N - 1)
                        way = slice(None, None, -1 if d else None)
                        V.tensor_tensor_scan(
                            h[n % 2][:, :, :].rearrange("p c t -> p (c t)")[:, way],
                            da[d][n % 2][:, :, :].rearrange("p c t -> p (c t)")[:, way],
                            db[n % 2][:, :, :].rearrange("p c t -> p (c t)")[:, way],
                            0.0, ALU.mult, ALU.add).then_inc(s["h_ready"], 1)
                    dve.wait_ge(s["y_mm"], NS * (u + 1))
                    if due(u):
                        dve.wait_ge(s["ys_ready"], u)
                    for c in range(CH):
                        V.scalar_tensor_tensor(y1[:, c, :], us[d][:, c, :], dskip[:, d, c:c + 1],
                                               py[:, c, :], ALU.mult, ALU.add).then_inc(s["y1_ready"], 1)
                    dve.wait_ge(s["y1_ready"], CH * (u + 1))
                    dve.wait_ge(s["silu_ready"], 3 * u + 3)
                    if due(u):
                        dve.wait_ge(s["o_mm"], u)
                    V.tensor_tensor(ys[:, :, :], y1[:, :, :], zs[d][:, :, :],
                                    ALU.mult).then_inc(s["ys_ready"], 1)
                    dve.wait_ge(s["o_mm"], u + 1)
                    dve.wait_ge(s["xres_ready"], g + 1)
                    if due(u):
                        dve.wait_ge(s["x_ready"], u)
                    V.tensor_tensor(seqs(S.x, g), seqs(S.x, g),
                                    pm[0][:, :].rearrange("p (i t) -> p i t", t=T),
                                    ALU.add).then_inc(s["x_ready"], 1)
                    if d == 1:
                        dve.wait_ge(s["x_ready"], u + 1)
                        S.next_stats(dve, g, s["stats"])

                drive(dve, front, scan, par)

            @block.gpsimd
            def _(pool):
                P = nc.gpsimd
                P.memset(xnT[:, :, :, :], 0.0).then_inc(s["seg_zero"], 1)
                for d in range(2):
                    for k in range(2):
                        P.memset(da[d][k][:, :, :], 0.0).then_inc(s["seg_zero"], 1)
                r1, var = S.rstd, S.var
                S.ln_scalars(pool, s["rstd"], LN_EPS)
                P.tensor_tensor(r1sq[:, :], r1[:, :], r1[:, :], ALU.mult).then_inc(s["rstd"], 1)
                pool.wait_ge(s["rstd"], LN_STEPS + 1)
                P.tensor_tensor(v2[:, :], var[:, :], r1sq[:, :], ALU.mult).then_inc(s["rstd"], 1)
                pool.wait_ge(s["rstd"], LN_STEPS + 2)
                P.tensor_scalar(ve[:, :], v2[:, :], LN_EPS, None, ALU.add).then_inc(s["rstd"], 1)
                pool.wait_ge(s["rstd"], LN_STEPS + 3)
                P.tensor_tensor(r2[:, :], ve[:, :], S.minus_half[:, 0:NB], ALU.pow).then_inc(s["rstd"], 1)
                pool.wait_ge(s["rstd"], LN_STEPS + 4)
                P.tensor_tensor(r12[:, :], r1[:, :], r2[:, :], ALU.mult).then_inc(s["rstd"], 1)
                pool.wait_ge(s["rstd"], LN_STEPS + 5)
                P.tensor_scalar(r1p[:, :], r1[:, :], 1.0, None, ALU.add).then_inc(s["rstd"], 1)
                pool.wait_ge(s["rstd"], LN_STEPS + 6)
                P.tensor_tensor(mr1[:, :], S.mean[:, :], r1[:, :], ALU.mult).then_inc(s["rstd"], 1)
                pool.wait_ge(s["rstd"], LN_STEPS + 7)
                par = [0]

                def front(g, d, at=None):
                    pass

                def scan(g, d, nxt):
                    u = 2 * g + d
                    for n in range(NS):
                        N = NS * u + n
                        if nxt:
                            nxt(n)
                        pool.wait_ge(s["h_ready"], N + 1)
                        pool.wait_ge(s["c_ready"], N + 1)
                        if due(N + 1 - HCB):
                            pool.wait_ge(s["y_mm"], N + 1 - HCB)
                        P.tensor_tensor(hc[n % HCB][:, :, :], h[n % 2][:, :, :], bc(cs[n % 2][:, :], 1, CH),
                                        ALU.mult).then_inc(s["hc_ready"], 1)

                drive(pool, front, scan, par)


def cross_attention_layer(nc, S, w, full_mask):
    SCALE = DKX ** -0.5
    QK = QH * TC
    with ExitStack() as ctx:
        A = Alloc(nc, ctx, f"x{full_mask}_")
        wq, wk, wv, wo = (A.sb(n, [128, 128]) for n in ("wq", "wk", "wv", "wo"))
        bq, bqs, bk = (A.sb(n, [128, 1]) for n in ("bq", "bqs", "bk"))
        bv = A.sb("bv", [TC, 128])
        bo = A.sb("bo", [128, 128])
        hmask = A.sb("hmask", [128, HX])
        if full_mask:
            mask = [A.sb(f"mask{p}", [128, TC], I32) for p in range(2)]
            out_of = [A.sb(f"out_of{p}", [128, TC], I32) for p in range(2)]
            fill = A.sb("fill", [128, 1])
        else:
            mrow = A.sb("mrow", [128, NB * TC], I32)
            keep = A.sb("keep", [128, NB * TC])
            some = A.sb("some", [128, NB])
            brow = A.sb("brow", [1, NB * TC], BF16)
            ones = A.sb("ones", [1, 128], BF16)
        ctxT = [A.sb(f"ctxT{p}", [128, TC]) for p in range(2)]
        xh = A.sb("xh", [128, 1, D])
        xT = A.sb("xT", [128, T])
        qT = [A.sb(f"qT{p}", [128, T]) for p in range(2)]
        kT = A.sb("kT", [128, TC])
        kd = [A.sb(f"kd{p}", [128, HX, TC]) for p in range(2)]
        v_early = [A.sb(f"v_early{p}", [TC, 128]) for p in range(2)]
        VSTEP = W4 + DKX
        va = [A.sb(f"va{p}", [TC, NQ, QH * VSTEP]) for p in range(2)]
        top, den, rden = ([A.sb(f"{n}{q}", [128, QH]) for q in range(NQ)] for n in ("top", "den", "rden"))
        pr = [A.sb(f"pr{q}", [128, QH, TC]) for q in range(NQ)]
        prT = [A.sb(f"prT{q}", [TC, QH * T]) for q in range(2)]
        cT = A.sb("cT", [128, T])
        ps = [A.ps(f"ps{k}", [128, 512]) for k in range(2)]
        pt = [A.ps(f"pt{k}", [128, QH * T]) for k in range(2)]
        py = [A.ps(f"py{k}", [128, 512]) for k in range(2)]
        px = A.ps("px", [128, 512])
        pqkv = A.ps("pqkv", [128, 512])
        s = {n: A.sem(n) for n in """weights prep rstd xh_ready xb_ready t_mm xT_ready qkv_mm q_ready
            ve_ready v_ready kd_ready s_mm filled top_ready sub_ready exp_ready den_ready rden_ready norm_ready
            pt_mm prT_ready y_mm cT_ready o_mm x_ready stats out_of_ready keep va_zero""".split()}
        ctx_in = [A.sem(f"ctx_in{p}") for p in range(2)]
        mask_in = [A.sem(f"mask_in{p}") for p in range(2)]
        loads = [(wq, w["wq"]), (wk, w["wk"]), (wv, w["wv"]), (wo, w["wo"]), (bq, w["bq"]), (bk, w["bk"]),
                 (bv, w["bv"].partition_broadcast(TC)), (bo, w["bo"].partition_broadcast(128)),
                 (hmask, w["hmask"])]
        if not full_mask:
            loads += [(mrow, w["mrow"].partition_broadcast(128))]
        W_ALL = 16 * len(loads)
        V0 = T + TC

        with nc.Block() as block:

            @block.sync
            def _(sp):
                for dst, src in loads:
                    sp.dma_start(dst[:, :], src).then_inc(s["weights"], 16)

                def load(b):
                    if due(b.n - 1):
                        sp.wait_ge(s["qkv_mm"], b.n - 1)
                    sp.dma_start(ctxT[b.p][:, :], w["ctxT"][:, bass.ds(b.n * TC, TC)]).then_inc(ctx_in[b.p], 16)
                    if full_mask:
                        if due(b.n - 1):
                            sp.wait_ge(s["out_of_ready"], b.n - 1)
                        sp.dma_start(mask[b.p][:, :], w["mask"][bass.ds(b.n, 1)].squeeze(0)
                                     ).then_inc(mask_in[b.p], 16)
                load(Seq(0, 0))
                load(Seq(0, 1))
                with sp.Fori(1, NB // 2) as j:
                    load(Seq(j, 0))
                    load(Seq(j, 1))

            @block.tensor
            def _(pe):
                mm, tr = nc.tensor.matmul, nc.tensor.transpose
                pe.wait_ge(s["weights"], W_ALL)
                pe.wait_ge(s["prep"], 1)

                def turn(b, q):
                    t = b.quad(q)
                    pe.wait_ge(s["norm_ready"], t + 1)
                    if due(t - 1):
                        pe.wait_ge(s["prT_ready"], t - 1)
                    for i in range(QH):
                        ins = tr(pt[q % 2][0:TC, i * T:(i + 1) * T], pr[q][:, i, :], S.ident[:, :])
                    ins.then_inc(s["pt_mm"], 1)

                def scores(b, q):
                    t = b.quad(q)
                    pe.wait_ge(s["kd_ready"], t + 1)
                    if q == 0:
                        pe.wait_ge(s["q_ready"], b.n + 1)
                    if due(t - 1):
                        pe.wait_ge(s["sub_ready"], t - 1)
                    out = ps[q % 2][:, 0:QK]
                    ins = mm(out, qT[b.p][:, :], kd[b.p][:, QH * q:QH * q + QH, :],
                             start=True, stop=bool(full_mask))
                    if not full_mask:
                        row = bc(brow[0:1, bass.ds(b.n * TC, TC)], 1, QH)
                        ins = mm(out, ones[:, :], row, start=False, stop=True)
                    ins.then_inc(s["s_mm"], 1)

                def values(b, q):
                    t = b.quad(q)
                    pe.wait_ge(s["prT_ready"], t + 1)
                    if q == 0:
                        pe.wait_ge(s["v_ready"], b.n + 1)
                        if due(b.n - 1):
                            pe.wait_ge(s["cT_ready"], b.n - 1)
                    for i in range(QH):
                        ins = mm(py[b.p][W4 * q:W4 * q + W4, 0:T], va[b.p][:, q, W4 * i:W4 * i + W4],
                                 prT[q % 2][:, i * T:(i + 1) * T], start=i == 0, stop=i == QH - 1)
                    ins.then_inc(s["y_mm"], 1)

                def slot(b, q):
                    if b.real():
                        turn(b, q)
                    nxt = b.plus(1)
                    if nxt.real():
                        scores(nxt, q)
                    n = b.plus(3)
                    o = b.plus(-1)
                    if q == 1 and n.real():
                        pe.wait_ge(s["xh_ready"], n.n + 1)
                        if due(n.n - 4):
                            pe.wait_ge(s["x_ready"], n.n - 4)
                        tr(px[:, 0:T], xh[:, 0, :], S.ident[:, :]).then_inc(s["t_mm"], 1)
                    if q == 2 and n.real():
                        pe.wait_ge(s["xT_ready"], n.n + 1)
                        pe.wait_ge(ctx_in[n.p], 16 * (n.j + 1))
                        if due(n.n):
                            pe.wait_ge(s["q_ready"], n.n)
                        if due(n.n):
                            pe.wait_ge(s["ve_ready"], n.n)
                        mm(pqkv[:, 0:T], wq[:, :], xT[:, :], start=True, stop=True)
                        mm(pqkv[:, T:V0], wk[:, :], ctxT[n.p][:, :], start=True, stop=True)
                        mm(pqkv[0:TC, V0:V0 + 128], ctxT[n.p][:, :], wv[:, :], start=True, stop=True
                           ).then_inc(s["qkv_mm"], 1)
                    if q == 2 and o.real():
                        pe.wait_ge(s["cT_ready"], o.n + 1)
                        if due(o.n):
                            pe.wait_ge(s["x_ready"], o.n)
                        if n.real():
                            pe.wait_ge(s["xT_ready"], n.n + 1)
                        mm(px[:, T:2 * T], cT[:, :], wo[:, :], start=True, stop=True).then_inc(s["o_mm"], 1)
                    last = b if q else b.plus(-1)
                    if last.real():
                        values(last, (q - 1) % NQ)

                walk_sequences(pe, slot, 3)

            @block.scalar
            def _(act):
                A_ = nc.scalar.activation
                act.wait_ge(s["weights"], W_ALL)
                act.wait_ge(s["prep"], 1)

                def slot(b, q):
                    e = b if q < 2 else b.plus(1)
                    if e.real():
                        qe = (q + 2) % NQ
                        act.wait_ge(s["sub_ready"], e.quad(qe) + 1)
                        A_(pr[qe][:, :, :], pr[qe][:, :, :], ACT.Exp).then_inc(s["exp_ready"], 1)
                    if b.real():
                        t = b.quad(q)
                        act.wait_ge(s["pt_mm"], t + 1)
                        if due(t - 1):
                            act.wait_ge(s["y_mm"], t - 1)
                        A_(prT[q % 2][:, :], pt[q % 2][0:TC, :], ACT.Copy).then_inc(s["prT_ready"], 1)
                    n = b.plus(3)
                    m = b.plus(2)
                    if q == 1 and n.real():
                        act.wait_ge(s["t_mm"], n.n + 1)
                        if due(n.n):
                            act.wait_ge(s["qkv_mm"], n.n)
                        A_(xT[:, :], px[:, 0:T], ACT.Copy).then_inc(s["xT_ready"], 1)
                    if q == 0 and m.real():
                        act.wait_ge(s["qkv_mm"], m.n + 1)
                        if due(NQ * m.n):
                            act.wait_ge(s["kd_ready"], NQ * m.n)
                        A_(kT[:, :], pqkv[:, T:V0], ACT.Identity, bias=bk[:, 0:1])
                        if due(NQ * (m.n - 1)):
                            act.wait_ge(s["s_mm"], NQ * (m.n - 1))
                        A_(qT[m.p][:, :], pqkv[:, 0:T], ACT.Identity, bias=bqs[:, 0:1], scale=SCALE
                           ).then_inc(s["q_ready"], 1)
                walk_sequences(act, slot, 3)

            @block.vector
            def _(dve):
                V = nc.vector
                dve.wait_ge(s["weights"], W_ALL)
                if full_mask:
                    V.memset(fill[:, :], -1.0e9)
                else:
                    V.memset(ones[:, :], 1.0)
                    V.tensor_scalar(brow[:, :], mrow[0:1, :], 0.0, MASKED, ALU.is_equal, ALU.mult)
                    V.tensor_scalar(keep[:, :], mrow[:, :], 0.0, None, ALU.not_equal).then_inc(s["keep"], 1)
                    dve.wait_ge(s["keep"], 1)
                    V.tensor_reduce(some[:, :], keep[:, :].rearrange("p (b k) -> p b k", k=TC), AX.X, ALU.max)
                V.tensor_scalar(bqs[:, :], bq[:, :], SCALE, None, ALU.mult).then_inc(s["prep"], 1)
                dve.wait_ge(s["prep"], 1)
                dve.wait_ge(s["rstd"], LN_STEPS)
                dve.wait_ge(s["va_zero"], 2)

                def slot(b, q):
                    d = b if q < 3 else b.plus(1)
                    a = b if q < 1 else b.plus(1)
                    qd, qa = (q + 1) % NQ, (q + 3) % NQ
                    if a.real():
                        dve.wait_ge(s["s_mm"], a.quad(qa) + 1)
                        if full_mask and qa == 0:
                            dve.wait_ge(s["out_of_ready"], a.n + 1)
                    if d.real():
                        t = d.quad(qd)
                        dve.wait_ge(s["exp_ready"], t + 1)
                        if due(t - 3):
                            dve.wait_ge(s["rden_ready"], t - 3)
                        V.tensor_reduce(den[qd][:, :], pr[qd][:, :, :], AX.X, ALU.add).then_inc(s["den_ready"], 1)
                    if a.real():
                        t = a.quad(qa)
                        sc = ps[qa % 2][:, 0:QK].rearrange("p (h k) -> p h k", k=TC)
                        if full_mask:
                            V.copy_predicated(sc, bc(out_of[a.p][:, :], 1, QH),
                                              bc(fill[:, :], 1, QH).to_broadcast([128, QH, TC])
                                              ).then_inc(s["filled"], 1)
                    if d.real():
                        t = d.quad(qd)
                        dve.wait_ge(s["den_ready"], t + 1)
                        if due(t - 3):
                            dve.wait_ge(s["norm_ready"], t - 3)
                        V.reciprocal(rden[qd][:, :], den[qd][:, :]).then_inc(s["rden_ready"], 1)
                    if a.real():
                        t = a.quad(qa)
                        if full_mask:
                            dve.wait_ge(s["filled"], t + 1)
                        V.tensor_reduce(top[qa][:, :], sc, AX.X, ALU.max).then_inc(s["top_ready"], 1)
                        dve.wait_ge(s["top_ready"], t + 1)
                        if due(t - 3):
                            dve.wait_ge(s["pt_mm"], t - 3)
                        V.tensor_tensor(pr[qa][:, :, :], sc, bc(top[qa][:, :], 2, TC), ALU.subtract
                                        ).then_inc(s["sub_ready"], 1)
                    n = b.plus(3)
                    m = b.plus(2)
                    c = b.plus(1)
                    o = b.plus(-1)
                    if q == 0 and n.real():
                        if due(n.n):
                            dve.wait_ge(s["t_mm"], n.n)
                        i = bass.ds(n.n, 1)
                        V.tensor_scalar(xh[:, :, :], S.x[:, i, :], S.mean[:, i], S.rstd[:, i],
                                        ALU.subtract, ALU.mult).then_inc(s["xh_ready"], 1)
                    if q == 0 and c.real() and full_mask:
                        dve.wait_ge(mask_in[c.p], 16 * (c.j + 1))
                        if due(NQ * (c.n - 1)):
                            dve.wait_ge(s["filled"], NQ * (c.n - 1))
                        V.tensor_scalar(out_of[c.p][:, :], mask[c.p][:, :], 0.0, None, ALU.is_equal
                                        ).then_inc(s["out_of_ready"], 1)
                    if q == 1 and o.real():
                        dve.wait_ge(s["y_mm"], NQ * (o.n + 1))
                        if due(o.n):
                            dve.wait_ge(s["o_mm"], o.n)
                        y = py[o.p][:, 0:T]
                        if full_mask:
                            V.tensor_copy(cT[:, :], y).then_inc(s["cT_ready"], 1)
                        else:
                            V.tensor_scalar(cT[:, :], y, some[:, bass.ds(o.n, 1)], None, ALU.mult
                                            ).then_inc(s["cT_ready"], 1)
                    if q == 1 and m.real():
                        dve.wait_ge(s["q_ready"], m.n + 1)
                        if due(m.n - 1):
                            dve.wait_ge(s["v_ready"], m.n - 1)
                        V.tensor_tensor(v_early[m.p][:, :], pqkv[0:TC, V0:V0 + 128], bv[:, :], ALU.add
                                        ).then_inc(s["ve_ready"], 1)
                    if q == 2 and c.real():
                        dve.wait_ge(s["ve_ready"], c.n + 1)
                        if due(NQ * (c.n - 1)):
                            dve.wait_ge(s["y_mm"], NQ * (c.n - 1))
                        V.tensor_copy(va[c.p][:, :, :].rearrange("p a (i x) -> p a i x", x=VSTEP)[:, :, :, 0:DKX],
                                      v_early[c.p][:, :].rearrange("p (a i d) -> p a i d", i=QH, d=DKX)
                                      ).then_inc(s["v_ready"], 1)
                    if q == 3 and o.real():
                        i = bass.ds(o.n, 1)
                        dve.wait_ge(s["o_mm"], o.n + 1)
                        dve.wait_ge(s["xb_ready"], o.n + 1)
                        V.tensor_tensor(S.x[:, i, :], S.x[:, i, :], bc(px[:, T:2 * T], 1, 1), ALU.add
                                        ).then_inc(s["x_ready"], 1)
                        dve.wait_ge(s["x_ready"], o.n + 1)
                        V.bn_stats(S.bn[:, i, :], S.x[:, i, :]).then_inc(s["stats"], 1)

                walk_sequences(dve, slot, 3)

            @block.gpsimd
            def _(pool):
                P = nc.gpsimd
                pool.wait_ge(s["weights"], W_ALL)
                S.ln_scalars(pool, s["rstd"], LN_EPS)
                for p in range(2):
                    P.memset(va[p][:, :, :], 0.0).then_inc(s["va_zero"], 1)

                def slot(b, q):
                    d = b if q < 3 else b.plus(1)
                    if d.real():
                        qd = (q + 1) % NQ
                        pool.wait_ge(s["rden_ready"], d.quad(qd) + 1)
                        P.tensor_tensor(pr[qd][:, :, :], pr[qd][:, :, :], bc(rden[qd][:, :], 2, TC), ALU.mult
                                        ).then_inc(s["norm_ready"], 1)
                    m = b.plus(2)
                    if m.real():
                        pool.wait_ge(s["q_ready"], m.n + 1)
                        if due(NQ * (m.n - 2) + q + 1):
                            pool.wait_ge(s["s_mm"], NQ * (m.n - 2) + q + 1)
                        quad = slice(QH * q, QH * q + QH)
                        P.tensor_tensor(kd[m.p][:, quad, :], bc(kT[:, :], 1, QH), bc(hmask[:, quad], 2, TC), ALU.mult
                                        ).then_inc(s["kd_ready"], 1)
                    if q == 3 and m.real():
                        i = bass.ds(m.n, 1)
                        pool.wait_ge(s["xh_ready"], m.n + 1)
                        P.tensor_tensor(S.x[:, i, :], S.x[:, i, :], bc(bo[:, :], 1, 1), ALU.add
                                        ).then_inc(s["xb_ready"], 1)

                walk_sequences(pool, slot, 3)


def moe_top2_layer(nc, S, w):
    NE, MC = E0 + 1, M0 // 128
    BELOW = -1.0e38
    with ExitStack() as ctx:
        A = Alloc(nc, ctx, "c_")
        gu = A.sb("gu", [128, NE, 2, M0])
        gu_hi, gu_lo = (A.sb(n, [128, NE, 2, M0], F32R) for n in ("gu_hi", "gu_lo"))
        down = A.sb("down", [128, NE, MC, D])
        router = A.sb("router", [128, E0])
        bias = A.sb("bias", [128, E0])
        order = A.sb("order", [128, E0])
        xh = [A.sb(f"xh{p}", [128, GS, D]) for p in range(2)]
        xT = [A.sb(f"xT{p}", [128, GT]) for p in range(2)]
        x_hi, x_lo = (A.sb(n, [128, NG, GT], F32R) for n in ("x_hi", "x_lo"))
        logits, sigm, sel, best, first, second, c = (
            A.sb(n, [128, NB, E0]) for n in ("logits", "sigm", "sel", "best", "first", "second", "c"))
        top, pick = A.sb("top", [128, NB]), A.sb("pick", [128, NB])
        weights = A.sem("weights")
        with ExitStack() as ctx1:
            B = Alloc(nc, ctx1, "c1_")
            pt = [B.ps(f"pt{k}", [128, GT]) for k in range(2)]
            pl = B.ps("pl", [128, NB, E0])
            s = {n: B.sem(n) for n in """rstd xh_ready t_mm xT_ready hi_ready lo_ready l_mm gu_hi_ready
                gu_lo_ready l_ready sigm_ready route""".split()}
            with nc.Block() as block:

                @block.sync
                def _(sp):
                    for dst, src in ((router[:, :], w["router"]), (bias[:, :], w["bias"].partition_broadcast(128)),
                                     (order[:, :], w["order"].partition_broadcast(128)),
                                     (gu[:, :, :, :], w["gu"]), (down[:, :, :, :], w["down"])):
                        sp.dma_start(dst, src).then_inc(weights, 16)

                @block.tensor
                def _(pe):
                    pe.wait_ge(weights, 16 * 5)

                    def body(g, p):
                        pe.wait_ge(s["xh_ready"], g + 1)
                        if due(g - 1):
                            pe.wait_ge(s["xT_ready"], g - 1)
                        for i in range(GS):
                            ins = nc.tensor.transpose(pt[p][:, i * T:(i + 1) * T], xh[p][:, i, :], S.ident[:, :])
                        ins.then_inc(s["t_mm"], 1)
                        pe.wait_ge(s["xT_ready"], g + 1)
                        for i in range(GS):
                            ins = nc.tensor.matmul(pl[:, bass.ds(g * GS + i, 1), :], xT[p][:, i * T:(i + 1) * T],
                                                   router[:, :], start=True, stop=True)
                        ins.then_inc(s["l_mm"], 1)
                    walk_groups(pe, body)

                @block.scalar
                def _(act):
                    A_ = nc.scalar.activation

                    def body(g, p):
                        act.wait_ge(s["t_mm"], g + 1)
                        if due(g - 1):
                            act.wait_ge(s["l_mm"], g - 1)
                        if due(g - 1):
                            act.wait_ge(s["lo_ready"], g - 1)
                        A_(xT[p][:, :], pt[p][:, :], ACT.Copy).then_inc(s["xT_ready"], 1)
                        act.wait_ge(s["xT_ready"], g + 1)
                        A_(x_hi[:, bass.ds(g, 1), :], bc(xT[p][:, :], 1, 1), ACT.Copy).then_inc(s["hi_ready"], 1)
                    walk_groups(act, body)
                    act.wait_ge(weights, 16 * 5)
                    A_(gu_hi[:, :, :, :], gu[:, :, :, :], ACT.Copy).then_inc(s["gu_hi_ready"], 1)
                    act.wait_ge(s["l_ready"], 1)
                    A_(sigm[:, :, :], logits[:, :, :], ACT.Sigmoid).then_inc(s["sigm_ready"], 1)

                @block.vector
                def _(dve):
                    V = nc.vector
                    dve.wait_ge(s["rstd"], LN_STEPS)

                    def body(g, p):
                        if due(g - 1):
                            dve.wait_ge(s["t_mm"], g - 1)
                        for i in range(GS):
                            b = bass.ds(g * GS + i, 1)
                            ins = V.tensor_scalar(xh[p][:, i:i + 1, :], S.x[:, b, :], S.mean[:, b],
                                                  S.rstd[:, b], ALU.subtract, ALU.mult)
                        ins.then_inc(s["xh_ready"], 1)
                    walk_groups(dve, body)
                    dve.wait_ge(s["l_mm"], NG)
                    dve.wait_ge(weights, 16 * 5)
                    V.tensor_copy(logits[:, :, :], pl[:, :, :]).then_inc(s["l_ready"], 1)
                    dve.wait_ge(s["l_ready"], 1)

                    V.tensor_tensor(sel[:, :, :], logits[:, :, :], bc(bias[:, :], 1, NB), ALU.add).then_inc(s["route"], 1)
                    dve.wait_ge(s["route"], 1)
                    V.tensor_reduce(top[:, :], sel[:, :, :], AX.X, ALU.max).then_inc(s["route"], 1)
                    dve.wait_ge(s["route"], 2)
                    V.tensor_tensor(best[:, :, :], sel[:, :, :], bc(top[:, :], 2, E0), ALU.is_equal).then_inc(s["route"], 1)
                    dve.wait_ge(s["route"], 3)
                    V.tensor_tensor(best[:, :, :], best[:, :, :], bc(order[:, :], 1, NB), ALU.mult).then_inc(s["route"], 1)
                    dve.wait_ge(s["route"], 4)
                    V.tensor_reduce(pick[:, :], best[:, :, :], AX.X, ALU.max).then_inc(s["route"], 1)
                    dve.wait_ge(s["route"], 5)
                    V.tensor_tensor(first[:, :, :], best[:, :, :], bc(pick[:, :], 2, E0), ALU.is_equal).then_inc(s["route"], 1)
                    dve.wait_ge(s["route"], 6)
                    V.scalar_tensor_tensor(sel[:, :, :], first[:, :, :], BELOW, sel[:, :, :], ALU.mult, ALU.add).then_inc(s["route"], 1)
                    dve.wait_ge(s["route"], 7)
                    V.tensor_reduce(top[:, :], sel[:, :, :], AX.X, ALU.max).then_inc(s["route"], 1)
                    dve.wait_ge(s["route"], 8)
                    V.tensor_tensor(best[:, :, :], sel[:, :, :], bc(top[:, :], 2, E0), ALU.is_equal).then_inc(s["route"], 1)
                    dve.wait_ge(s["route"], 9)
                    V.tensor_tensor(best[:, :, :], best[:, :, :], bc(order[:, :], 1, NB), ALU.mult).then_inc(s["route"], 1)
                    dve.wait_ge(s["route"], 10)
                    V.tensor_reduce(pick[:, :], best[:, :, :], AX.X, ALU.max).then_inc(s["route"], 1)
                    dve.wait_ge(s["route"], 11)
                    V.tensor_tensor(second[:, :, :], best[:, :, :], bc(pick[:, :], 2, E0), ALU.is_equal).then_inc(s["route"], 1)
                    dve.wait_ge(s["route"], 12)
                    V.tensor_tensor(first[:, :, :], first[:, :, :], second[:, :, :], ALU.add).then_inc(s["route"], 1)
                    dve.wait_ge(s["route"], 13)
                    dve.wait_ge(s["sigm_ready"], 1)
                    V.tensor_tensor(c[:, :, :], first[:, :, :], sigm[:, :, :], ALU.mult)
                    dve.wait_ge(s["gu_hi_ready"], 1)
                    V.tensor_tensor(gu_lo[:, :, :, :], gu[:, :, :, :], gu_hi[:, :, :, :].bitcast(F32),
                                    ALU.subtract).then_inc(s["gu_lo_ready"], 1)

                @block.gpsimd
                def _(pool):
                    S.ln_scalars(pool, s["rstd"], LN_EPS)

                    def body(g, p):
                        pool.wait_ge(s["hi_ready"], g + 1)
                        b = bass.ds(g, 1)
                        nc.gpsimd.tensor_tensor(x_lo[:, b, :], bc(xT[p][:, :], 1, 1), x_hi[:, b, :].bitcast(F32),
                                                ALU.subtract).then_inc(s["lo_ready"], 1)
                    walk_groups(pool, body)

        act_of = [A.sb(f"act_of{k}", [128, GT]) for k in range(2)]
        h = [A.sb(f"h{k}", [128, MC, GT]) for k in range(2)]
        total = A.sb("total", [128, GS, D])
        pg = [A.ps(f"pg{k}", [128, GT]) for k in range(2)]
        pu = [A.ps(f"pu{k}", [128, GT]) for k in range(2)]
        pd = [A.ps(f"pd{k}", [128, GS, D]) for k in range(2)]
        s = {n: A.sem(n) for n in "g_mm u_mm silu_ready h_ready d_mm total_ready x_ready stats".split()}

        def walk(eng, unit):
            def both(j):
                for p in range(2):
                    for e in range(NE):
                        unit(2 * j + p, e, (p * NE + e) % 2)
            both(0)
            with eng.Fori(1, NG // 2) as j:
                both(j)

        with nc.Block() as block:

            @block.tensor
            def _(pe):
                mm = nc.tensor.matmul

                def project(g, e, k):
                    U = NE * g + e
                    xs = [x[:, bass.ds(g, 1), :] for x in (x_hi, x_lo)]
                    for c_ in range(MC):
                        cols = slice(c_ * 128, (c_ + 1) * 128)
                        if due(MC * (U - 1) + c_ + 1):
                            pe.wait_ge(s["silu_ready"], MC * (U - 1) + c_ + 1)
                        split_pass(mm, pg[c_][:, :], gu_hi[:, e, 0, cols], gu_lo[:, e, 0, cols], *xs,
                                   True, True).then_inc(s["g_mm"], 1)
                        if due(MC * (U - 1) + c_ + 1):
                            pe.wait_ge(s["h_ready"], MC * (U - 1) + c_ + 1)
                        split_pass(mm, pu[c_][:, :], gu_hi[:, e, 1, cols], gu_lo[:, e, 1, cols], *xs,
                                   True, True).then_inc(s["u_mm"], 1)

                def back(g, e, k):
                    U = NE * g + e
                    pe.wait_ge(s["h_ready"], MC * (U + 1))
                    if due(U - 1):
                        pe.wait_ge(s["total_ready"], U - 1)
                    for i in range(GS):
                        for c_ in range(MC):
                            ins = mm(pd[k][:, i, :], h[k][:, c_, i * T:(i + 1) * T], down[:, e, c_, :],
                                     start=c_ == 0, stop=c_ == MC - 1)
                    ins.then_inc(s["d_mm"], 1)

                def unit(g, e, k):
                    project(g, e, k)
                    if e:
                        back(g, e - 1, 1 - k)
                    elif not (isinstance(g, int) and g == 0):
                        back(g - 1, NE - 1, 1 - k)
                walk(pe, unit)
                back(NG - 1, NE - 1, (NG * NE - 1) % 2)

            @block.scalar
            def _(act):
                def unit(g, e, k):
                    U = NE * g + e
                    for c_ in range(MC):
                        act.wait_ge(s["g_mm"], MC * U + c_ + 1)
                        if due(MC * (U - 1) + c_ + 1):
                            act.wait_ge(s["h_ready"], MC * (U - 1) + c_ + 1)
                        nc.scalar.activation(act_of[c_][:, :], pg[c_][:, :], ACT.Silu).then_inc(s["silu_ready"], 1)
                walk(act, unit)

            @block.vector
            def _(dve):
                V = nc.vector

                def gated(g, e, k):
                    U = NE * g + e
                    for c_ in range(MC):
                        dve.wait_ge(s["silu_ready"], MC * U + c_ + 1)
                        dve.wait_ge(s["u_mm"], MC * U + c_ + 1)
                        if due(U - 1):
                            dve.wait_ge(s["d_mm"], U - 1)
                        V.tensor_tensor(h[k][:, c_, :], act_of[c_][:, :], pu[c_][:, :], ALU.mult
                                        ).then_inc(s["h_ready"], 1)

                def add(g, e, k):
                    U = NE * g + e
                    dve.wait_ge(s["d_mm"], U + 1)
                    if due(U):
                        dve.wait_ge(s["total_ready"], U)
                    if e == NE - 1:
                        V.tensor_tensor(total[:, :, :], total[:, :, :], pd[k][:, :, :], ALU.add
                                        ).then_inc(s["total_ready"], 1)
                        dve.wait_ge(s["total_ready"], U + 1)
                        V.tensor_tensor(seqs(S.x, g), seqs(S.x, g), total[:, :, :], ALU.add
                                        ).then_inc(s["x_ready"], 1)
                        dve.wait_ge(s["x_ready"], g + 1)
                        S.next_stats(dve, g, s["stats"])
                        return
                    if e == 0:
                        if due(g):
                            dve.wait_ge(s["x_ready"], g)
                    for i in range(GS):
                        weight = c[:, bass.ds(g * GS + i, 1), e]
                        if e == 0:
                            ins = V.tensor_scalar(total[:, i, :], pd[k][:, i, :], weight, None, ALU.mult)
                        else:
                            ins = V.scalar_tensor_tensor(total[:, i, :], pd[k][:, i, :], weight, total[:, i, :],
                                                         ALU.mult, ALU.add)
                    ins.then_inc(s["total_ready"], 1)

                def unit(g, e, k):
                    gated(g, e, k)
                    if e:
                        add(g, e - 1, 1 - k)
                    elif not (isinstance(g, int) and g == 0):
                        add(g - 1, NE - 1, 1 - k)
                walk(dve, unit)
                add(NG - 1, NE - 1, (NG * NE - 1) % 2)


def window_attention_layer(nc, S, w):
    NP = HL // 2
    NH = HL + KVL
    EPS = 1e-6
    with ExitStack() as ctx:
        A = Alloc(nc, ctx, "d_")
        wq = A.sb("wq", [128, HL * HDL])
        wkv = A.sb("wkv", [128, 2 * KVL * HDL])
        wo = A.sb("wo", [128, NP, D])
        outside32 = A.sb("outside32", [128, T])
        outside = A.sb("outside", [128, T], BF16)
        qnw, knw, kscale = (A.sb(n, [128, 1]) for n in ("qnw", "knw", "kscale"))
        xh = A.sb("xh", [128, 1, D])
        xT = A.sb("xT", [128, T])
        sq = A.sb("sq", [128, NH, HDL])
        ssq, mean_sq, r = (A.sb(n, [128, NH]) for n in ("ssq", "mean_sq", "r"))
        qn = A.sb("qn", [128, HL, HDL])
        kn = A.sb("kn", [128, KVL, 2, HDL])
        v_early = [A.sb(f"v_early{p}", [128, KVL, HDL]) for p in range(2)]
        v = [A.sb(f"v{p}", [128, KVL, HDL]) for p in range(2)]
        qT = [A.sb(f"qT{p}", [128, NP, T]) for p in range(2)]
        kT = [A.sb(f"kT{p}", [128, KVL, 2, T]) for p in range(2)]
        top, den, rden = ([A.sb(f"{n}{q}", [128, QH]) for q in range(NQ)] for n in ("top", "den", "rden"))
        pr = [A.sb(f"pr{q}", [128, QH, T]) for q in range(NQ)]
        prT = [A.sb(f"prT{q}", [128, QH, T]) for q in range(2)]
        cT = [A.sb(f"cT{p}", [128, NP, T]) for p in range(2)]
        ps = [A.ps(f"ps{k}", [128, QH, T]) for k in range(2)]
        pt = A.ps("pt", [128, QH, T])
        py = A.ps("py", [128, 512])
        pq = [A.ps(f"pq{k}", [128, 512]) for k in range(2)]
        pkv = A.ps("pkv", [128, 512])
        px = A.ps("px", [128, 512])
        s = {n: A.sem(n) for n in """weights prep kscale rstd xh_ready t_mm xT_ready qkv_mm sq_ready ssq_ready
            ms_ready r_ready qn_ready kn_ready ve_ready v_ready qkT_mm qT_ready kT_ready s_mm top_ready sub_ready
            exp_ready den_ready rden_ready norm_ready pt_mm prT_ready y_mm cT_ready o_mm x_ready stats kT_zero""".split()}
        loads = ((wq[:, :], w["wq"]), (wkv[:, :], w["wkv"]), (wo[:, :, :], w["wo"]),
                 (outside32[:, :], w["outside"]), (qnw[:, :], w["qnw"]), (knw[:, :], w["knw"]))
        W_ALL = 16 * len(loads)

        with nc.Block() as block:

            @block.sync
            def _(sp):
                for dst, src in loads:
                    sp.dma_start(dst, src).then_inc(s["weights"], 16)

            @block.tensor
            def _(pe):
                mm, tr = nc.tensor.matmul, nc.tensor.transpose
                pe.wait_ge(s["weights"], W_ALL)
                pe.wait_ge(s["prep"], 1)

                def turn(b, q):
                    t = b.quad(q)
                    pe.wait_ge(s["norm_ready"], t + 1)
                    if due(t):
                        pe.wait_ge(s["prT_ready"], t)
                    for i in range(QH):
                        ins = tr(pt[:, i, :], pr[q][:, i, :], S.ident[:, :])
                    ins.then_inc(s["pt_mm"], 1)

                def scores(b, q):
                    t = b.quad(q)
                    if q == 0:
                        pe.wait_ge(s["qT_ready"], 2 * (b.n + 1))
                        pe.wait_ge(s["kT_ready"], 2 * (b.n + 1))
                    if due(t - 1):
                        pe.wait_ge(s["sub_ready"], t - 1)
                    mm(ps[q % 2][:, :, :], S.ident_bf[:, :], bc(outside[:, :], 1, QH), start=True, stop=False)
                    for k in range(2):
                        ins = mm(ps[q % 2][:, 2 * k:2 * k + 2, :], qT[b.p][:, 2 * q + k, :], kT[b.p][:, q, :, :],
                                 start=False, stop=k == 1)
                    ins.then_inc(s["s_mm"], 1)

                def values(b, q):
                    t = b.quad(q)
                    pe.wait_ge(s["prT_ready"], t + 1)
                    if q == 0:
                        pe.wait_ge(s["v_ready"], b.n + 1)
                    if due(t):
                        pe.wait_ge(s["cT_ready"], t)
                    for k in range(2):
                        ins = mm(py[64 * k:64 * k + 64, 0:2 * T], v[b.p][:, q, :], prT[q % 2][:, k:QH:2, :],
                                 start=True, stop=True)
                    ins.then_inc(s["y_mm"], 1)

                def slot(b, q):
                    if b.real():
                        turn(b, q)
                    nxt = b.plus(1)
                    if nxt.real():
                        scores(nxt, q)
                    n = b.plus(3)
                    o = b.plus(-1)
                    if q == 1 and n.real():
                        pe.wait_ge(s["xh_ready"], n.n + 1)
                        if due(n.n - 4):
                            pe.wait_ge(s["x_ready"], n.n - 4)
                        tr(px[:, 0:T], xh[:, 0, :], S.ident[:, :]).then_inc(s["t_mm"], 1)
                    if q == 2 and n.real():
                        pe.wait_ge(s["xT_ready"], n.n + 1)
                        if due(2 * n.n):
                            pe.wait_ge(s["qT_ready"], 2 * n.n)
                        if due(2 * n.n):
                            pe.wait_ge(s["kT_ready"], 2 * n.n)
                        for k in range(2):
                            mm(pq[k][:, :], xT[:, :], wq[:, 512 * k:512 * k + 512], start=True, stop=True
                               ).then_inc(s["qkv_mm"], 1)
                        mm(pkv[:, :], xT[:, :], wkv[:, :], start=True, stop=True).then_inc(s["qkv_mm"], 1)
                    m = b.plus(2)
                    if q == 1 and m.real():
                        pe.wait_ge(s["qn_ready"], 2 * (m.n + 1))
                        pe.wait_ge(s["kn_ready"], m.n + 1)
                        pe.wait_ge(s["ve_ready"], m.n + 1)
                        for k in range(2):
                            for i in range(4):
                                pair = 4 * k + i
                                ins = tr(pq[k][:, i * T:(i + 1) * T], qn[:, 2 * pair:2 * pair + 2, :], S.ident[:, :])
                            ins.then_inc(s["qkT_mm"], 1)
                        for i in range(KVL):
                            ins = tr(pkv[:, i * T:(i + 1) * T], kn[:, i, :, :], S.ident[:, :])
                        ins.then_inc(s["qkT_mm"], 1)
                    if q == 2 and o.real():
                        pe.wait_ge(s["cT_ready"], NQ * (o.n + 1))
                        if due(o.n):
                            pe.wait_ge(s["x_ready"], o.n)
                        if n.real():
                            pe.wait_ge(s["xT_ready"], n.n + 1)
                        for i in range(NP):
                            ins = mm(px[:, T:2 * T], cT[o.p][:, i, :], wo[:, i, :], start=i == 0, stop=i == NP - 1)
                        ins.then_inc(s["o_mm"], 1)
                    last = b if q else b.plus(-1)
                    if last.real():
                        values(last, (q - 1) % NQ)

                walk_sequences(pe, slot, 3)

            @block.scalar
            def _(act):
                A_ = nc.scalar.activation
                act.wait_ge(s["kscale"], 2)
                act.wait_ge(s["kT_zero"], 2)

                def slot(b, q):
                    y = b if q >= 2 else b.plus(-1)
                    if y.real():
                        qy = (q - 2) % NQ
                        t = y.quad(qy)
                        act.wait_ge(s["y_mm"], t + 1)
                        if due(y.n - 1):
                            act.wait_ge(s["o_mm"], y.n - 1)
                        A_(cT[y.p][:, 2 * qy:2 * qy + 2, :], py[:, 0:2 * T].rearrange("p (i t) -> p i t", t=T),
                           ACT.Copy).then_inc(s["cT_ready"], 1)
                    e = b if q < 2 else b.plus(1)
                    if e.real():
                        qe = (q + 2) % NQ
                        act.wait_ge(s["sub_ready"], e.quad(qe) + 1)
                        A_(pr[qe][:, :, :], pr[qe][:, :, :], ACT.Exp).then_inc(s["exp_ready"], 1)
                    if b.real():
                        t = b.quad(q)
                        act.wait_ge(s["pt_mm"], t + 1)
                        if due(t - 1):
                            act.wait_ge(s["y_mm"], t - 1)
                        A_(prT[q % 2][:, :, :], pt[:, :, :], ACT.Copy).then_inc(s["prT_ready"], 1)
                    n = b.plus(3)
                    m = b.plus(2)
                    if q == 1 and n.real():
                        act.wait_ge(s["t_mm"], n.n + 1)
                        if due(3 * n.n):
                            act.wait_ge(s["qkv_mm"], 3 * n.n)
                        A_(xT[:, :], px[:, 0:T], ACT.Copy).then_inc(s["xT_ready"], 1)
                    if q == 1 and m.real():
                        if due(NQ * (m.n - 1)):
                            act.wait_ge(s["s_mm"], NQ * (m.n - 1))
                        for k in range(2):
                            act.wait_ge(s["qkT_mm"], 3 * m.n + k + 1)
                            A_(qT[m.p][:, 4 * k:4 * k + 4, :], pq[k][:, :].rearrange("p (i t) -> p i t", t=T),
                               ACT.Copy).then_inc(s["qT_ready"], 1)
                        act.wait_ge(s["qkT_mm"], 3 * m.n + 3)
                        for k in range(2):
                            half = slice(64 * k, 64 * k + 64)
                            A_(kT[m.p][half, :, k, :], pkv[half, :].rearrange("p (i t) -> p i t", t=T), ACT.Copy,
                               scale=kscale[half, 0:1]).then_inc(s["kT_ready"], 1)
                    if q == 2 and n.real():
                        if due(n.n):
                            act.wait_ge(s["ssq_ready"], n.n)
                        for k in range(2):
                            act.wait_ge(s["qkv_mm"], 3 * n.n + k + 1)
                            A_(sq[:, 8 * k:8 * k + 8, :], pq[k][:, :].rearrange("p (h d) -> p h d", d=HDL),
                               ACT.Square).then_inc(s["sq_ready"], 1)
                        act.wait_ge(s["qkv_mm"], 3 * n.n + 3)
                        A_(sq[:, HL:NH, :], pkv[:, 0:256].rearrange("p (h d) -> p h d", d=HDL),
                           ACT.Square).then_inc(s["sq_ready"], 1)
                    if q == 3 and n.real():
                        if due(n.n - 1):
                            act.wait_ge(s["v_ready"], n.n - 1)
                        A_(v_early[n.p][:, :, :], pkv[:, 256:512].rearrange("p (h d) -> p h d", d=HDL),
                           ACT.Copy).then_inc(s["ve_ready"], 1)

                walk_sequences(act, slot, 3)

            @block.vector
            def _(dve):
                V = nc.vector
                dve.wait_ge(s["weights"], W_ALL)
                V.tensor_copy(outside[:, :], outside32[:, :]).then_inc(s["prep"], 1)
                V.tensor_tensor(kscale[:, :], qnw[:, :], knw[:, :], ALU.mult).then_inc(s["kscale"], 1)
                dve.wait_ge(s["kscale"], 1)
                V.tensor_scalar(kscale[:, :], kscale[:, :], HDL ** -0.5, None, ALU.mult).then_inc(s["kscale"], 1)
                dve.wait_ge(s["rstd"], LN_STEPS)

                def slot(b, q):
                    d = b if q < 3 else b.plus(1)
                    if d.real():
                        qd = (q + 1) % NQ
                        t = d.quad(qd)
                        dve.wait_ge(s["exp_ready"], t + 1)
                        V.tensor_reduce(den[qd][:, :], pr[qd][:, :, :], AX.X, ALU.add).then_inc(s["den_ready"], 1)
                        dve.wait_ge(s["den_ready"], t + 1)
                        if due(t - 3):
                            dve.wait_ge(s["norm_ready"], t - 3)
                        V.reciprocal(rden[qd][:, :], den[qd][:, :]).then_inc(s["rden_ready"], 1)
                    a = b if q < 1 else b.plus(1)
                    if a.real():
                        qa = (q + 3) % NQ
                        t = a.quad(qa)
                        dve.wait_ge(s["s_mm"], t + 1)
                        V.tensor_reduce(top[qa][:, :], ps[qa % 2][:, :, :], AX.X, ALU.max
                                        ).then_inc(s["top_ready"], 1)
                        dve.wait_ge(s["top_ready"], t + 1)
                        if due(t - 3):
                            dve.wait_ge(s["pt_mm"], t - 3)
                        V.tensor_tensor(pr[qa][:, :, :], ps[qa % 2][:, :, :], bc(top[qa][:, :], 2, T),
                                        ALU.subtract).then_inc(s["sub_ready"], 1)
                    n = b.plus(3)
                    m = b.plus(2)
                    if q == 0 and n.real():
                        if due(n.n):
                            dve.wait_ge(s["t_mm"], n.n)
                        i = bass.ds(n.n, 1)
                        V.tensor_scalar(xh[:, :, :], S.x[:, i, :], S.mean[:, i], S.rstd[:, i],
                                        ALU.subtract, ALU.mult).then_inc(s["xh_ready"], 1)
                    if q == 3 and n.real():
                        dve.wait_ge(s["sq_ready"], 3 * (n.n + 1))
                        if due(n.n):
                            dve.wait_ge(s["ms_ready"], n.n)
                        V.tensor_reduce(ssq[:, :], sq[:, :, :], AX.X, ALU.add).then_inc(s["ssq_ready"], 1)
                        dve.wait_ge(s["ssq_ready"], n.n + 1)
                        if due(n.n):
                            dve.wait_ge(s["r_ready"], n.n)
                        V.tensor_scalar(mean_sq[:, :], ssq[:, :], 1.0 / HDL, EPS, ALU.mult, ALU.add
                                        ).then_inc(s["ms_ready"], 1)
                    if q == 0 and m.real():
                        dve.wait_ge(s["r_ready"], m.n + 1)
                        if due(3 * m.n):
                            dve.wait_ge(s["qkT_mm"], 3 * m.n)
                        for k in range(2):
                            V.tensor_tensor(qn[:, 8 * k:8 * k + 8, :], pq[k][:, :].rearrange("p (h d) -> p h d", d=HDL),
                                            bc(r[:, 8 * k:8 * k + 8], 2, HDL), ALU.mult).then_inc(s["qn_ready"], 1)
                        dve.wait_ge(s["ve_ready"], m.n + 1)
                        V.tensor_tensor(kn[:, :, :, :],
                                        bc(pkv[:, 0:256].rearrange("p (h d) -> p h d", d=HDL), 2, 2),
                                        bc(bc(r[:, HL:NH], 2, 2), 3, HDL).to_broadcast([128, KVL, 2, HDL]), ALU.mult
                                        ).then_inc(s["kn_ready"], 1)
                    c = b.plus(1)
                    if q == 2 and c.real():
                        dve.wait_ge(s["ve_ready"], c.n + 1)
                        if due(NQ * (c.n - 1)):
                            dve.wait_ge(s["y_mm"], NQ * (c.n - 1))
                        V.tensor_copy(v[c.p][:, :, :], v_early[c.p][:, :, :]).then_inc(s["v_ready"], 1)
                    o = b.plus(-1)
                    if q == 3 and o.real():
                        i = bass.ds(o.n, 1)
                        dve.wait_ge(s["o_mm"], o.n + 1)
                        V.tensor_tensor(S.x[:, i, :], S.x[:, i, :], bc(px[:, T:2 * T], 1, 1), ALU.add
                                        ).then_inc(s["x_ready"], 1)
                        dve.wait_ge(s["x_ready"], o.n + 1)
                        V.bn_stats(S.bn[:, i, :], S.x[:, i, :]).then_inc(s["stats"], 1)

                walk_sequences(dve, slot, 3)

            @block.gpsimd
            def _(pool):
                P = nc.gpsimd
                S.ln_scalars(pool, s["rstd"], LN_EPS)
                for p in range(2):
                    P.memset(kT[p][:, :, :, :], 0.0).then_inc(s["kT_zero"], 1)

                def slot(b, q):
                    d = b if q < 3 else b.plus(1)
                    if d.real():
                        qd = (q + 1) % NQ
                        t = d.quad(qd)
                        pool.wait_ge(s["rden_ready"], t + 1)
                        P.tensor_tensor(pr[qd][:, :, :], pr[qd][:, :, :], bc(rden[qd][:, :], 2, T), ALU.mult
                                        ).then_inc(s["norm_ready"], 1)
                    n = b.plus(3)
                    if q == 3 and n.real():
                        pool.wait_ge(s["ms_ready"], n.n + 1)
                        if due(2 * n.n):
                            pool.wait_ge(s["qn_ready"], 2 * n.n)
                        if due(n.n):
                            pool.wait_ge(s["kn_ready"], n.n)
                        P.tensor_tensor(r[:, :], mean_sq[:, :], S.minus_half[:, 0:NH], ALU.pow
                                        ).then_inc(s["r_ready"], 1)

                walk_sequences(pool, slot, 3)


def moe_top1_layer(nc, S, w, out_d):
    FC = M1 // 128
    LO = 32
    OUT_EPS = 1e-12
    with ExitStack() as ctx:
        A = Alloc(nc, ctx, "f_")
        w1 = A.sb("w1", [128, E1, M1])
        w1_hi, w1_lo = (A.sb(n, [128, E1, M1], F32R) for n in ("w1_hi", "w1_lo"))
        b1 = A.sb("b1", [LO + E1, M1])
        b1_parts = A.sb("b1_parts", [128, M1], F32R)
        wo = A.sb("wo", [128, FC, D])
        bo, gamma, beta = (A.sb(n, [128, D]) for n in ("bo", "gamma", "beta"))
        router = A.sb("router", [128, E1])
        order = A.sb("order", [128, E1])
        pick_row32 = A.sb("pick_row32", [E1, E1])
        pick_row = A.sb("pick_row", [128, E1, 128], F32R)
        xh = [A.sb(f"xh{p}", [128, GS, D]) for p in range(2)]
        xT = [A.sb(f"xT{p}", [128, GT]) for p in range(2)]
        x_hi, x_lo = (A.sb(n, [128, NG, GT], F32R) for n in ("x_hi", "x_lo"))
        best = A.sb("best", [128, NB, E1])
        chosen = A.sb("chosen", [128, NB, 128])
        chosenT = A.sb("chosenT", [128, NG, GT], F32R)
        top, pick = A.sb("top", [128, NB]), A.sb("pick", [128, NB])
        weights = A.sem("weights")
        loads = ((router[:, :], w["router"]), (order[:, :], w["order"].partition_broadcast(128)),
                 (b1[0:E1, :], w["b1"]), (b1[LO:LO + E1, :], w["b1"]), (pick_row32[:, :], w["pick_row"]),
                 (bo[:, :], w["bo"].partition_broadcast(128)), (gamma[:, :], w["gamma"].partition_broadcast(128)),
                 (beta[:, :], w["beta"].partition_broadcast(128)), (w1[:, :, :], w["w1"]), (wo[:, :, :], w["wo"]))
        W_ALL = 16 * len(loads)
        with ExitStack() as ctx1:
            B = Alloc(nc, ctx1, "f1_")
            pt = [B.ps(f"pt{k}", [128, GT]) for k in range(2)]
            pl = B.ps("pl", [128, NB, E1])
            pc = [B.ps(f"pc{k}", [128, GT]) for k in range(2)]
            s = {n: B.sem(n) for n in """rstd xh_ready t_mm xT_ready hi_ready lo_ready l_mm w1_hi_ready w1_lo_ready
                b1_zero b1_hi_ready b1_lo_ready zero route chosen_ready c_mm chosenT_ready pick_row_ready""".split()}
            with nc.Block() as block:

                @block.sync
                def _(sp):
                    for dst, src in loads:
                        sp.dma_start(dst, src).then_inc(weights, 16)

                @block.tensor
                def _(pe):
                    pe.wait_ge(weights, W_ALL)

                    def body(g, p):
                        pe.wait_ge(s["xh_ready"], g + 1)
                        if due(g - 1):
                            pe.wait_ge(s["xT_ready"], g - 1)
                        for i in range(GS):
                            ins = nc.tensor.transpose(pt[p][:, i * T:(i + 1) * T], xh[p][:, i, :], S.ident[:, :])
                        ins.then_inc(s["t_mm"], 1)
                        pe.wait_ge(s["xT_ready"], g + 1)
                        for i in range(GS):
                            ins = nc.tensor.matmul(pl[:, bass.ds(g * GS + i, 1), :], xT[p][:, i * T:(i + 1) * T],
                                                   router[:, :], start=True, stop=True)
                        ins.then_inc(s["l_mm"], 1)
                    walk_groups(pe, body)
                    pe.wait_ge(s["chosen_ready"], 1)
                    for g in range(NG):
                        if due(g - 1):
                            pe.wait_ge(s["chosenT_ready"], g - 1)
                        for i in range(GS):
                            ins = nc.tensor.transpose(pc[g % 2][:, i * T:(i + 1) * T],
                                                      chosen[:, g * GS + i, :], S.ident[:, :])
                        ins.then_inc(s["c_mm"], 1)

                @block.scalar
                def _(act):
                    A_ = nc.scalar.activation

                    def body(g, p):
                        act.wait_ge(s["t_mm"], g + 1)
                        if due(g - 1):
                            act.wait_ge(s["l_mm"], g - 1)
                        if due(g - 1):
                            act.wait_ge(s["lo_ready"], g - 1)
                        A_(xT[p][:, :], pt[p][:, :], ACT.Copy).then_inc(s["xT_ready"], 1)
                        act.wait_ge(s["xT_ready"], g + 1)
                        A_(x_hi[:, bass.ds(g, 1), :], bc(xT[p][:, :], 1, 1), ACT.Copy).then_inc(s["hi_ready"], 1)
                    walk_groups(act, body)
                    act.wait_ge(weights, W_ALL)
                    A_(w1_hi[:, :, :], w1[:, :, :], ACT.Copy).then_inc(s["w1_hi_ready"], 1)
                    for g in range(NG):
                        act.wait_ge(s["c_mm"], g + 1)
                        A_(chosenT[:, g, :], pc[g % 2][:, :], ACT.Copy).then_inc(s["chosenT_ready"], 1)

                @block.vector
                def _(dve):
                    V = nc.vector
                    V.memset(chosen[:, :, :], 0.0).then_inc(s["zero"], 1)
                    V.memset(pick_row[:, :, :].bitcast(F32), 0.0)
                    V.memset(b1_parts[:, :].bitcast(F32), 0.0).then_inc(s["b1_zero"], 1)
                    dve.wait_ge(s["rstd"], LN_STEPS)

                    def body(g, p):
                        if due(g - 1):
                            dve.wait_ge(s["t_mm"], g - 1)
                        for i in range(GS):
                            b = bass.ds(g * GS + i, 1)
                            ins = V.tensor_scalar(xh[p][:, i:i + 1, :], S.x[:, b, :], S.mean[:, b],
                                                  S.rstd[:, b], ALU.subtract, ALU.mult)
                        ins.then_inc(s["xh_ready"], 1)
                    walk_groups(dve, body)
                    dve.wait_ge(weights, W_ALL)
                    dve.wait_ge(s["b1_zero"], 1)
                    V.tensor_copy(b1_parts[0:E1, :], b1[0:E1, :]).then_inc(s["b1_hi_ready"], 1)
                    V.tensor_copy(b1_parts[LO:LO + E1, :], b1[LO:LO + E1, :]).then_inc(s["b1_hi_ready"], 1)
                    dve.wait_ge(s["b1_hi_ready"], 2)
                    V.tensor_tensor(b1_parts[LO:LO + E1, :], b1[LO:LO + E1, :],
                                    b1_parts[LO:LO + E1, :].bitcast(F32), ALU.subtract).then_inc(s["b1_lo_ready"], 1)
                    V.tensor_copy(pick_row[0:E1, :, :], bc(pick_row32[:, :], 2, 128)).then_inc(s["pick_row_ready"], 1)
                    dve.wait_ge(s["l_mm"], NG)
                    dve.wait_ge(s["zero"], 1)
                    V.tensor_reduce(top[:, :], pl[:, :, :], AX.X, ALU.max).then_inc(s["route"], 1)
                    dve.wait_ge(s["route"], 1)
                    V.tensor_tensor(best[:, :, :], pl[:, :, :], bc(top[:, :], 2, E1), ALU.is_equal).then_inc(s["route"], 1)
                    dve.wait_ge(s["route"], 2)
                    V.tensor_tensor(best[:, :, :], best[:, :, :], bc(order[:, :], 1, NB), ALU.mult).then_inc(s["route"], 1)
                    dve.wait_ge(s["route"], 3)
                    V.tensor_reduce(pick[:, :], best[:, :, :], AX.X, ALU.max).then_inc(s["route"], 1)
                    dve.wait_ge(s["route"], 4)
                    for first in (0, LO):
                        ins = V.tensor_tensor(chosen[:, :, first:first + E1], best[:, :, :], bc(pick[:, :], 2, E1),
                                              ALU.is_equal)
                    ins.then_inc(s["chosen_ready"], 1)
                    dve.wait_ge(s["w1_hi_ready"], 1)
                    V.tensor_tensor(w1_lo[:, :, :], w1[:, :, :], w1_hi[:, :, :].bitcast(F32), ALU.subtract
                                    ).then_inc(s["w1_lo_ready"], 1)

                @block.gpsimd
                def _(pool):
                    S.ln_scalars(pool, s["rstd"], LN_EPS)

                    def body(g, p):
                        pool.wait_ge(s["hi_ready"], g + 1)
                        b = bass.ds(g, 1)
                        nc.gpsimd.tensor_tensor(x_lo[:, b, :], bc(xT[p][:, :], 1, 1), x_hi[:, b, :].bitcast(F32),
                                                ALU.subtract).then_inc(s["lo_ready"], 1)
                    walk_groups(pool, body)

        xm_hi, xm_lo = ([A.sb(f"{n}{k}", [128, GT], F32R) for k in range(2)] for n in ("xm_hi", "xm_lo"))
        gelu = A.sb("gelu", [128, FC, GT])
        y = A.sb("y", [128, GS, D])
        norm = A.sb("norm", [128, GS, D])
        scaled = A.sb("scaled", [128, GS, D])
        resid = A.sb("resid", [128, GS, D])
        ybn = A.sb("ybn", [128, GS, 6])
        ymv = A.sb("ymv", [128, GS, 2])
        yve, yr = A.sb("yve", [128, GS]), A.sb("yr", [128, GS])
        pi = [A.ps(f"pi{f}", [128, GT]) for f in range(FC)]
        pm = [A.ps(f"pm{k}", [128, GT]) for k in range(2)]
        py = A.ps("py", [128, GS, D])
        s = {n: A.sem(n) for n in """m_mm hi_ready lo_ready i_mm gelu_ready o_mm xn_ready xnb_ready y_ready bn_ready
            mv_ready ve_ready r_ready norm_ready scaled_ready resid_ready x_ready""".split()}
        stored = A.sem("stored")

        def walk(eng, unit):
            def group(g):
                for e in range(E1):
                    unit(g, e)
            group(0)
            with eng.Fori(1, NG) as g:
                group(g)

        def behind(g, e, at):
            return e == at and not (isinstance(g, int) and g == 0)

        with nc.Block() as block:

            @block.sync
            def _(sp):
                for g in range(NG):
                    sp.wait_ge(s["x_ready"], g + 1)
                    sp.dma_start(out_d[g * GS:(g + 1) * GS].rearrange("b t d -> t b d"),
                                 S.x[:, g * GS:(g + 1) * GS, :]).then_inc(stored, 16)
                sp.wait_ge(stored, 16 * NG)

            @block.tensor
            def _(pe):
                mm = nc.tensor.matmul

                def spread(g, e):
                    U = E1 * g + e
                    if due(U - 1):
                        pe.wait_ge(s["lo_ready"], U - 1)
                    mm(pm[e % 2][:, :], pick_row[:, e, :], chosenT[:, bass.ds(g, 1), :],
                       start=True, stop=True).then_inc(s["m_mm"], 1)

                def project_out(g):
                    pe.wait_ge(s["gelu_ready"], FC * (g + 1))
                    pe.wait_ge(s["y_ready"], g)
                    for i in range(GS):
                        for f in range(FC):
                            ins = mm(py[:, i, :], gelu[:, f, i * T:(i + 1) * T], wo[:, f, :],
                                     start=f == 0, stop=f == FC - 1)
                    ins.then_inc(s["o_mm"], 1)

                def unit(g, e):
                    U = E1 * g + e
                    if e == 0:
                        spread(g, 0)
                        spread(g, 1)
                        for f in range(FC):
                            if due(FC * (g - 1) + f + 1):
                                pe.wait_ge(s["gelu_ready"], FC * (g - 1) + f + 1)
                            mm(pi[f][:, :], b1_parts[:, f * 128:(f + 1) * 128], chosenT[:, bass.ds(g, 1), :],
                               start=True, stop=False)
                    pe.wait_ge(s["hi_ready"], U + 1)
                    pe.wait_ge(s["lo_ready"], U + 1)
                    for f in range(FC):
                        cols = slice(f * 128, (f + 1) * 128)
                        split_pass(mm, pi[f][:, :], w1_hi[:, e, cols], w1_lo[:, e, cols], xm_hi[e % 2][:, :],
                                   xm_lo[e % 2][:, :], False, e == E1 - 1).then_inc(s["i_mm"], 1)
                    if 2 <= e + 2 < E1:
                        spread(g, e + 2)
                    if behind(g, e, 1):
                        project_out(g - 1)
                walk(pe, unit)
                project_out(NG - 1)

            @block.scalar
            def _(act):
                def unit(g, e):
                    if e < E1 - 1:
                        return
                    if due(g):
                        act.wait_ge(s["o_mm"], g)
                    for f in range(FC):
                        act.wait_ge(s["i_mm"], FC * (E1 * g + E1 - 1) + f + 1)
                        nc.scalar.activation(gelu[:, f, :], pi[f][:, :], ACT.Gelu).then_inc(s["gelu_ready"], 1)
                walk(act, unit)

            @block.vector
            def _(dve):
                V = nc.vector

                def finish(g):
                    dve.wait_ge(s["norm_ready"], g)
                    for i in range(GS):
                        b = bass.ds(g * GS + i, 1)
                        ins = V.tensor_scalar(y[:, i:i + 1, :], S.x[:, b, :], S.mean[:, b], S.rstd[:, b],
                                              ALU.subtract, ALU.mult)
                    ins.then_inc(s["xn_ready"], 1)
                    dve.wait_ge(s["xn_ready"], g + 1)
                    V.tensor_tensor(y[:, :, :], y[:, :, :], bc(bo[:, :], 1, GS), ALU.add).then_inc(s["xnb_ready"], 1)
                    dve.wait_ge(s["xnb_ready"], g + 1)
                    dve.wait_ge(s["o_mm"], g + 1)
                    V.tensor_tensor(y[:, :, :], y[:, :, :], py[:, :, :], ALU.add).then_inc(s["y_ready"], 1)
                    dve.wait_ge(s["y_ready"], g + 1)
                    for i in range(GS):
                        ins = V.bn_stats(ybn[:, i, :], y[:, i, :])
                    ins.then_inc(s["bn_ready"], 1)

                def scale(g):
                    for i in range(GS):
                        ins = V.bn_aggr(ymv[:, i, :], ybn[:, i, :])
                    ins.then_inc(s["mv_ready"], 1)
                    dve.wait_ge(s["mv_ready"], g + 1)
                    V.tensor_scalar(yve[:, :], ymv[:, :, 1], OUT_EPS, None, ALU.add).then_inc(s["ve_ready"], 1)
                    dve.wait_ge(s["r_ready"], g + 1)
                    for i in range(GS):
                        ins = V.tensor_scalar(norm[:, i, :], y[:, i, :], ymv[:, i, 0:1], yr[:, i:i + 1],
                                              ALU.subtract, ALU.mult)
                    ins.then_inc(s["norm_ready"], 1)
                    dve.wait_ge(s["norm_ready"], g + 1)
                    V.tensor_tensor(scaled[:, :, :], norm[:, :, :], bc(gamma[:, :], 1, GS), ALU.mult
                                    ).then_inc(s["scaled_ready"], 1)
                    dve.wait_ge(s["scaled_ready"], g + 1)
                    dve.wait_ge(s["resid_ready"], g + 1)
                    V.tensor_tensor(seqs(S.x, g), resid[:, :, :], scaled[:, :, :], ALU.add).then_inc(s["x_ready"], 1)

                def unit(g, e):
                    U = E1 * g + e
                    k = e % 2
                    dve.wait_ge(s["m_mm"], U + 1)
                    if due(FC * (U - 1)):
                        dve.wait_ge(s["i_mm"], FC * (U - 1))
                    if behind(g, e, 4):
                        dve.wait_ge(s["bn_ready"], g)
                    for part, x, ready in ((xm_hi, x_hi, "hi_ready"), (xm_lo, x_lo, "lo_ready")):
                        V.tensor_tensor(bc(part[k][:, :], 1, 1), x[:, bass.ds(g, 1), :].bitcast(F32),
                                        bc(pm[k][:, :], 1, 1), ALU.mult).then_inc(s[ready], 1)
                    if behind(g, e, 3):
                        finish(g - 1)
                    if behind(g, e, 4):
                        scale(g - 1)
                walk(dve, unit)
                finish(NG - 1)
                dve.wait_ge(s["bn_ready"], NG)
                scale(NG - 1)

            @block.gpsimd
            def _(pool):
                P = nc.gpsimd

                def finish(g):
                    if due(g):
                        pool.wait_ge(s["x_ready"], g)
                    P.tensor_tensor(resid[:, :, :], seqs(S.x, g), bc(beta[:, :], 1, GS), ALU.add
                                    ).then_inc(s["resid_ready"], 1)
                    pool.wait_ge(s["ve_ready"], g + 1)
                    P.tensor_tensor(yr[:, :], yve[:, :], S.minus_half[:, 0:GS], ALU.pow).then_inc(s["r_ready"], 1)
                finish(0)
                with pool.Fori(1, NG) as g:
                    finish(g)


def program(nc, a, out):
    with ExitStack() as ctx:
        S = Shared(nc, Alloc(nc, ctx, ""))
        load_layer(nc, S, a["x"], a["ident"])
        mamba_layer(nc, S, {k[2:]: v for k, v in a.items() if k.startswith("A_")})
        cross_attention_layer(nc, S, {k[2:]: v for k, v in a.items() if k.startswith("B_")}, 0)
        moe_top2_layer(nc, S, {k[2:]: v for k, v in a.items() if k.startswith("C_")})
        window_attention_layer(nc, S, {k[2:]: v for k, v in a.items() if k.startswith("D_")})
        cross_attention_layer(nc, S, {k[2:]: v for k, v in a.items() if k.startswith("E_")}, 1)
        moe_top1_layer(nc, S, {k[2:]: v for k, v in a.items() if k.startswith("F_")}, out)


def layout(inputs):
    f = {k: np.asarray(v) for k, v in inputs.items()}
    a = {"x": f["x"], "ident": np.eye(128, dtype=np.float32)}

    def col(v):
        return v.reshape(-1, 128).T

    a["A_sel32"] = np.tile(np.eye(2 * NS, dtype=np.float32), (3, 1))
    a["A_gamma"], a["A_beta"] = col(f["L0_attn_gamma"]), col(f["L0_attn_beta"])
    for p in "fb":
        q, r = f"A_{p}", f"L0_attn_{p}_"
        a[q + "conv_w"] = f[r + "conv_w"][:, 0, :].T
        a[q + "in_wT"] = f[r + "in_w"].T
        a[q + "conv_b"] = col(f[r + "conv_b"])
        rows = f[r + "xproj_w"]
        spread = np.concatenate([rows[DR:], rows[DR:], rows[DR:], rows[:DR]]).T
        a[q + "xprojT"] = spread.reshape(CH, 128, -1).transpose(1, 0, 2)
        a[q + "dt_wT"] = f[r + "dt_w"].T
        a[q + "dt_b"] = col(f[r + "dt_b"])
        a[q + "A_log"] = f[r + "A_log"].reshape(CH, 128, NS).transpose(1, 0, 2)
        a[q + "D"] = col(f[r + "D"])
        a[q + "out_wT"] = f[r + "out_w"].T.reshape(CH, 128, D).transpose(1, 0, 2)
    wkv, bkv = f["L0_xattn_Wkv"], f["L0_xattn_bkv"]
    ctxT = f["ctx_1024"].transpose(2, 0, 1).reshape(D, NB * TC)
    head_of = np.repeat(np.eye(HX, dtype=np.float32), DKX, axis=0)
    mask = f["mask_Bx1xS2_if1"][:, 0, :]
    a.update({"B_wq": f["L0_xattn_Wq"], "B_wk": wkv[:, :D], "B_wv": wkv[:, D:], "B_wo": f["L0_xattn_Wout"],
              "B_bq": col(f["L0_xattn_bq"]), "B_bk": col(bkv[:D]), "B_bv": bkv[D:], "B_bo": f["L0_xattn_bout"],
              "B_hmask": head_of, "B_ctxT": ctxT, "B_mrow": mask.reshape(-1)})
    n = "L0_ffn_"
    gate, up, dn = (np.concatenate([f[n + r], f[n + s]]) for r, s in (
        ("gate_proj_w", "shared_gate_w"), ("up_proj_w", "shared_up_w"), ("down_proj_w", "shared_down_w")))
    a.update({"C_router": f[n + "gate_w"].T, "C_bias": f[n + "beta"], "C_order": E0 - np.arange(E0, dtype=np.float32),
              "C_gu": np.stack([gate, up], 1).transpose(2, 0, 1, 3),
              "C_down": dn.reshape(E0 + 1, M0 // 128, 128, D).transpose(2, 0, 1, 3)})
    n = "L1_attn_"
    i, j = np.arange(T)[:, None], np.arange(T)[None, :]
    a.update({"D_wq": f[n + "wq"].T, "D_wkv": np.concatenate([f[n + "wk"], f[n + "wv"]]).T,
              "D_wo": f[n + "wo"].T.reshape(HL // 2, 128, D).transpose(1, 0, 2),
              "D_outside": np.where((i >= j) & (i - j < WIN), 0.0, MASKED).astype(np.float32),
              "D_qnw": np.tile(f[n + "q_norm_w"], 2)[:, None], "D_knw": np.tile(f[n + "k_norm_w"], 2)[:, None]})
    a.update({"E_wq": f["L1_xattn_Wq"].T, "E_wk": f["L1_xattn_Wk"].T, "E_wv": f["L1_xattn_Wv"].T,
              "E_wo": f["L1_xattn_Wo"].T, "E_bq": col(f["L1_xattn_bq"]), "E_bk": col(f["L1_xattn_bk"]),
              "E_bv": f["L1_xattn_bv"], "E_bo": f["L1_xattn_bo"], "E_mask": f["mask_Bx1xSxS2_ik0"][:, 0],
              "E_hmask": np.repeat(np.eye(HX, dtype=np.float32), DKX, axis=0),
              "E_ctxT": f["ctx_1024"].transpose(2, 0, 1).reshape(D, NB * TC)})
    n = "L1_ffn_"
    a.update({"F_router": f[n + "Wr"].T, "F_order": E1 - np.arange(E1, dtype=np.float32),
              "F_pick_row": np.eye(E1, dtype=np.float32), "F_w1": f[n + "W1"].transpose(1, 0, 2),
              "F_wo": f[n + "Wo"].reshape(M1 // 128, 128, D).transpose(1, 0, 2)})
    a.update({"F_" + k: f[n + k] for k in ("b1", "bo", "gamma", "beta")})
    return {k: np.ascontiguousarray(v) for k, v in a.items()}


def kernel(**inputs):
    import concourse.bacc as bacc
    from concourse.bass_utils import run_bass_kernel_spmd

    nc = bacc.Bacc("TRN2", target_bir_lowering=False, num_devices=1)
    arrays, args = {}, {}
    for name, v in layout(inputs).items():
        arrays["in_" + name] = v
        args[name] = nc.dram_tensor("in_" + name, v.shape, mybir.dt.from_np(v.dtype), kind="ExternalInput").ap()
    out = nc.dram_tensor("out_x", (NB, T, D), F32, kind="ExternalOutput").ap()
    program(nc, args, out)
    r = run_bass_kernel_spmd(nc, [arrays], core_ids=[0])
    return r.results[0]["out_x"]
```

```python
from contextlib import ExitStack

import numpy as np

import concourse.bass as bass
from concourse import mybir

F32 = mybir.dt.float32
F32R = mybir.dt.float32r
BF16 = mybir.dt.bfloat16
I32 = mybir.dt.int32
ALU = mybir.AluOpType
ACT = mybir.ActivationFunctionType
AX = mybir.AxisListType

NB, T, D = 32, 128, 128
TC = 77
GS = 4
NG = NB // GS
GT = GS * T
LN_EPS = 1e-5
LN_STEPS = 10

DI, NS, DR, TAPS = 256, 16, 8, 4
CH = DI // 128
PAD = TAPS - 1

HX, DKX = 16, 8
HL, KVL, HDL, WIN = 16, 4, 64, 64
QH = 4
NQ = HX // QH
W4 = QH * DKX

E0, M0, K0 = 8, 256, 2
E1, M1 = 8, 512

MASKED = -1.0e30


def due(count):
    return not isinstance(count, int) or count > 0


class Alloc:

    def __init__(self, nc, ctx, prefix):
        self.nc, self.ctx, self.prefix = nc, ctx, prefix
        self.sems = []
        ctx.callback(self.clear)

    def clear(self):
        if self.sems:
            self.nc.clear_and_free_semaphores(self.sems)
            self.nc.all_engine_barrier()

    def sb(self, name, shape, dt=F32):
        return self.ctx.enter_context(self.nc.sbuf_tensor(self.prefix + name, shape, dt))

    def ps(self, name, shape, dt=F32):
        return self.ctx.enter_context(self.nc.psum_tensor(self.prefix + name, shape, dt))

    def sem(self, name):
        self.sems.append(self.nc.alloc_semaphore(self.prefix + name))
        return self.sems[-1]


def seqs(t, g):
    return t[:, bass.ts(g, GS)]


def bc(ap, axis, n):
    a = ap.unsqueeze(axis)
    shape = list(a.shape)
    shape[axis] = n
    return a.to_broadcast(shape)


class Shared:

    def __init__(self, nc, A):
        self.nc = nc
        self.x = A.sb("x", [128, NB, D])
        self.bn = A.sb("bn", [128, NB, 6])
        self.mean, self.var, self.rstd = (A.sb(n, [128, NB]) for n in ("mean", "var", "rstd"))
        self.t0, self.t1 = A.sb("t0", [128, NB]), A.sb("t1", [128, NB])
        self.minus_half = A.sb("minus_half", [128, 128])
        self.ident = A.sb("ident", [128, 128])
        self.ident_bf = A.sb("ident_bf", [128, 128], BF16)

    def next_stats(self, dve, g, sem):
        for i in range(GS):
            b = bass.ds(g * GS + i, 1)
            ins = self.nc.vector.bn_stats(self.bn[:, b, :], self.x[:, b, :])
        ins.then_inc(sem, 1)

    def ln_scalars(self, pool, sem, eps, cols, done):
        P = self.nc.gpsimd
        me, mo, qe, qo = (self.bn[:, cols, k] for k in (1, 4, 2, 5))
        t0, t1, mean, var, rstd = (t[:, cols] for t in (self.t0, self.t1, self.mean, self.var, self.rstd))
        P.tensor_tensor(t0, me, mo, ALU.add).then_inc(sem, 1)
        pool.wait_ge(sem, done + 1)
        P.tensor_tensor(t1, me, mo, ALU.subtract).then_inc(sem, 1)
        pool.wait_ge(sem, done + 2)
        P.tensor_scalar(mean, t0, 0.5, None, ALU.mult).then_inc(sem, 1)
        pool.wait_ge(sem, done + 3)
        P.tensor_scalar(t1, t1, 0.5, None, ALU.mult).then_inc(sem, 1)
        pool.wait_ge(sem, done + 4)
        P.tensor_tensor(t0, qe, qo, ALU.add).then_inc(sem, 1)
        pool.wait_ge(sem, done + 5)
        P.tensor_tensor(t1, t1, t1, ALU.mult).then_inc(sem, 1)
        pool.wait_ge(sem, done + 6)
        P.tensor_scalar(t0, t0, 1.0 / D, None, ALU.mult).then_inc(sem, 1)
        pool.wait_ge(sem, done + 7)
        P.tensor_tensor(var, t0, t1, ALU.add).then_inc(sem, 1)
        pool.wait_ge(sem, done + 8)
        P.tensor_scalar(t0, var, eps, None, ALU.add).then_inc(sem, 1)
        pool.wait_ge(sem, done + 9)
        P.tensor_tensor(rstd, t0, self.minus_half[:, cols], ALU.pow).then_inc(sem, 1)
        pool.wait_ge(sem, done + 10)


LN_PARTS = (slice(0, GS), slice(GS, NB))


class Weights:

    def __init__(self, nc, ctx, prefix):
        self.alloc = Alloc(nc, ctx, prefix)
        self.loaded = self.alloc.sem("loaded")
        self.parts = []

    def tile(self, name, shape, src, dt=F32):
        t = self.alloc.sb(name, shape, dt)
        self.parts.append((t[tuple(slice(None) for _ in shape)], src))
        return t

    def part(self, dst, src):
        self.parts.append((dst, src))

    def load(self, sp):
        for dst, src in self.parts:
            sp.dma_start(dst, src).then_inc(self.loaded, 16)

    def all(self):
        return 16 * len(self.parts)

def load_layer(nc, S, x_d, ident_d, *ahead):
    with ExitStack() as ctx:
        A = Alloc(nc, ctx, "l_")
        x_in = [A.sem(f"x_in{k}") for k in range(NG)]
        ident_in, ident_ready, half, stats = A.sem("ident_in"), A.sem("ident_ready"), A.sem("half"), A.sem("stats")
        with nc.Block() as block:

            @block.sync
            def _(sp):
                for g in range(NG):
                    sp.dma_start(S.x[:, g * GS:(g + 1) * GS, :],
                                 x_d[g * GS:(g + 1) * GS].rearrange("b t d -> t b d")).then_inc(x_in[g], 16)
                sp.dma_start(S.ident[:, :], ident_d).then_inc(ident_in, 16)
                for weights in ahead:
                    weights.load(sp)

            @block.gpsimd
            def _(pool):
                nc.gpsimd.memset(S.minus_half[:, :], -0.5).then_inc(half, 1)

            @block.vector
            def _(dve):
                for g in range(NG):
                    dve.wait_ge(x_in[g], 16)
                    S.next_stats(dve, g, stats)
                dve.wait_ge(ident_in, 16)
                nc.vector.tensor_copy(S.ident_bf[:, :], S.ident[:, :]).then_inc(ident_ready, 1)


def walk_groups(eng, body):
    body(0, 0)
    body(1, 1)
    with eng.Fori(1, NG // 2) as j:
        body(2 * j, 0)
        body(2 * j + 1, 1)


def split_pass(mm, out, w_hi, w_lo, x_hi, x_lo, start, stop):
    mm(out, w_hi, x_hi, start=start, stop=False)
    mm(out, w_hi, x_lo, start=False, stop=False)
    return mm(out, w_lo, x_hi, start=False, stop=stop)


class Seq:

    def __init__(self, j, p):
        self.j, self.p = j, p
        self.n = 2 * j + p

    def plus(self, k):
        return Seq(self.j + (self.p + k) // 2, (self.p + k) % 2)

    def real(self):
        return not isinstance(self.n, int) or 0 <= self.n < NB

    def quad(self, q):
        return NQ * self.n + q


def walk_sequences(eng, slot, ahead=2):
    turns = (ahead + 1) // 2
    def both(j):
        for p in range(2):
            for q in range(NQ):
                slot(Seq(j, p), q)
    for j in range(-turns, 1):
        both(j)
    with eng.Fori(1, NB // 2 - turns) as j:
        both(j)
    for j in range(NB // 2 - turns, NB // 2 + 1):
        both(j)


def mamba_weights(nc, ctx, w):
    W = Weights(nc, ctx, "mw_")
    NROW = 3 * 2 * NS + DR

    def both(name, shape):
        return W.alloc.sb(name, [128, 2] + shape)
    W.convw, W.win_u, W.win_z = both("convw", [TAPS, DI]), both("win_u", [DI]), both("win_z", [DI])
    W.convb, W.xproj, W.dtw = both("convb", [CH]), both("xproj", [CH, NROW]), both("dtw", [DI])
    W.dtb, W.alog, W.dskip = both("dtb", [CH]), both("alog", [CH, NS]), both("dskip", [CH])
    W.outw = both("outw", [CH, D])
    for d, p in enumerate("fb"):
        W.part(W.convw[:, d], w[p + "conv_w"].partition_broadcast(128))
        W.part(W.win_u[:, d], w[p + "in_wT"][:, 0:DI])
        W.part(W.win_z[:, d], w[p + "in_wT"][:, DI:2 * DI])
        W.part(W.convb[:, d], w[p + "conv_b"])
        W.part(W.xproj[:, d], w[p + "xprojT"])
        W.part(W.dtw[96:96 + DR, d], w[p + "dt_wT"])
        W.part(W.dtb[:, d], w[p + "dt_b"])
        W.part(W.alog[:, d], w[p + "A_log"])
        W.part(W.dskip[:, d], w[p + "D"])
        W.part(W.outw[:, d], w[p + "out_wT"])
    W.gamma = W.tile("gamma", [128, 1], w["gamma"])
    W.beta = W.tile("beta", [128, 1], w["beta"])
    W.sel32 = W.tile("sel32", [96, 2 * NS], w["sel32"])
    return W


def mamba_layer(nc, S, W):
    NROW = 3 * 2 * NS + DR
    STEPS = LN_STEPS + 7
    LAG, BUF = 3, 4
    with ExitStack() as ctx:
        A = Alloc(nc, ctx, "m_")
        wtap = A.sb("wtap", [128, 2, TAPS, DI])
        aexp = A.sb("aexp", [128, 2, CH, NS])
        aneg = A.sb("aneg", [128, 2, CH, NS])
        sel = A.sb("sel", [96, 2 * NS, 128], BF16)
        ve = A.sb("ve", [128, NB])
        r1sq = A.sb("r1sq", [128, NB])
        v2 = A.sb("v2", [128, NB])
        r2 = A.sb("r2", [128, NB])
        r12 = A.sb("r12", [128, NB])
        r1p = A.sb("r1p", [128, NB])
        mr1 = A.sb("mr1", [128, NB])
        xh = A.sb("xh", [128, GS, D])
        xnT = A.sb("xnT", [128, 2, GS, T + 2 * PAD])
        us = [A.sb(f"us{d}", [128, CH, GT]) for d in range(2)]
        zraw = A.sb("zraw", [128, CH, GT])
        zs = [A.sb(f"zs{d}", [128, CH, GT]) for d in range(2)]
        bcrow = [A.sb(f"bcrow{d}", [96, GT], BF16) for d in range(2)]
        rest = A.sb("rest", [96, GT])
        dtrow = A.sb("dtrow", [128, GT])
        pre = A.sb("pre", [128, CH, GT])
        soft = A.sb("soft", [128, CH, GT])
        relu = A.sb("relu", [128, CH, GT])
        dt = [A.sb(f"dt{d}", [128, CH, GT]) for d in range(2)]
        du = [A.sb(f"du{d}", [128, CH, GT]) for d in range(2)]
        da = [A.sb(f"da{k}", [128, CH * GT + 1]) for k in range(BUF)]
        db = [A.sb(f"db{k}", [128, CH * GT]) for k in range(BUF)]
        h = [A.sb(f"h{k}", [128, CH * GT]) for k in range(BUF)]
        cs = [A.sb(f"cs{k}", [128, GT]) for k in range(BUF)]
        hc = [A.sb(f"hc{k}", [128, CH, GT]) for k in range(BUF)]
        y1 = A.sb("y1", [128, CH, GT])
        ys = A.sb("ys", [128, CH, GT])
        pb = [A.ps(f"pb{k}", [128, GT]) for k in range(2)]
        pc = [A.ps(f"pc{k}", [128, GT]) for k in range(2)]
        py = A.ps("py", [128, CH, GT])
        pm = [A.ps(f"pm{k}", [128, GT]) for k in range(2)]

        names = """prep stats rstd xh_ready xres_ready lnT_mm lnT_ready z_mm z_raw u_mm silu_ready
            row_mm row_hi row_rest row_mid row_ready dtrow_ready dt_mm dt_abs dt_relu dt_soft dt_ready
            du_ready b_mm c_mm c_ready da_ready db_ready h_ready hc_ready y_mm y1_ready ys_ready o_mm
            x_ready seg_zero aexp_ready""".split()
        s = {n: A.sem(n) for n in names}

        with nc.Block() as block:


            def drive(eng, front, scan, par):
                def group(g, p, last=False):
                    def nxt1(n):
                        par[0] = p
                        front(g, 1, at=n)

                    def nxt0(n):
                        par[0] = 1 - p
                        front(g + 1, 0, at=n)
                    scan(g, 0, nxt1)
                    scan(g, 1, None if last else nxt0)
                par[0] = 0
                front(0, 0)
                group(0, 0)
                group(1, 1)
                with eng.Fori(1, NG // 2 - 1) as j:
                    group(2 * j, 0)
                    group(2 * j + 1, 1)
                group(NG - 2, 0)
                group(NG - 1, 1, last=True)

            @block.tensor
            def _(pe):
                mm, tr = nc.tensor.matmul, nc.tensor.transpose
                pe.wait_ge(W.loaded, W.all())
                pe.wait_ge(s["prep"], 2)

                def front(g, d, at=None):
                    u = 2 * g + d
                    if d == 0 and at in (None, 0):
                        pe.wait_ge(s["xh_ready"], g + 1)
                        if due(CH * (u - 1) + 1):
                            pe.wait_ge(s["dt_relu"], CH * (u - 1) + 1)
                        if due(CH * (u - 1) + 1):
                            pe.wait_ge(s["dt_abs"], CH * (u - 1) + 1)
                        for i in range(GS):
                            last = tr(pm[0][:, i * T:(i + 1) * T], xh[:, i, :], S.ident[:, :])
                        last.then_inc(s["lnT_mm"], 1)
                    if at in (None, 2):
                        pe.wait_ge(s["lnT_ready"], g + 1)
                        if due(CH * u):
                            pe.wait_ge(s["dt_relu"], CH * u)
                        if due(CH * u):
                            pe.wait_ge(s["dt_abs"], CH * u)
                        rhs = xnT[:, par[0], :, PAD:PAD + T]
                        for c in range(CH):
                            mm(pm[1 - c][:, :], W.win_z[:, d, c * 128:(c + 1) * 128], rhs,
                               start=True, stop=True).then_inc(s["z_mm"], 1)
                    for i in range(CH * TAPS):
                        if at is not None and at != 3 + i // 3:
                            continue
                        c, k = divmod(i, TAPS)
                        off = k if d == 0 else 2 * PAD - k
                        if k == 0:
                            pe.wait_ge(s["z_raw"], CH * u + c + 1)
                        ins = mm(pm[1 - c][:, :], wtap[:, d, k, c * 128:(c + 1) * 128],
                                 xnT[:, par[0], :, off:off + T], start=k == 0, stop=k == TAPS - 1)
                        if k == TAPS - 1:
                            ins.then_inc(s["u_mm"], 1)
                    if at in (None, 7):
                        pe.wait_ge(s["silu_ready"], 3 * u + 2)
                        for c in range(CH):
                            ins = mm(pm[1][0:NROW, :], W.xproj[:, d, c, :], us[d][:, c, :],
                                     start=c == 0, stop=c == CH - 1)
                        ins.then_inc(s["row_mm"], 1)
                    if at in (None, 10):
                        pe.wait_ge(s["dtrow_ready"], u + 1)
                        if due(u - 1):
                            pe.wait_ge(s["x_ready"], u - 1)
                        for c in range(CH):
                            if c == 1:
                                pe.wait_ge(s["row_rest"], u + 1)
                            mm(pm[c][:, :], W.dtw[96:96 + DR, d, c * 128:(c + 1) * 128],
                               dtrow[96:96 + DR, :], start=True, stop=True).then_inc(s["dt_mm"], 1)

                par = [0]

                def spread(u, n, d):
                    N = NS * u + n
                    if n == 0:
                        pe.wait_ge(s["row_ready"], u + 1)
                    if due(N - 1):
                        pe.wait_ge(s["db_ready"], N - 1)
                    mm(pb[n % 2][:, :], sel[:, n, :], bcrow[d][:, :],
                       start=True, stop=True).then_inc(s["b_mm"], 1)
                    if due(N - 1):
                        pe.wait_ge(s["c_ready"], N - 1)
                    mm(pc[n % 2][:, :], sel[:, NS + n, :], bcrow[d][:, :],
                       start=True, stop=True).then_inc(s["c_mm"], 1)

                def add_state(u, n):
                    pe.wait_ge(s["hc_ready"], NS * u + n + 1)
                    if n == 0:
                        if due(CH * u):
                            pe.wait_ge(s["y1_ready"], CH * u)
                    for c in range(CH):
                        ins = mm(py[:, c, :], S.ident[:, :], hc[n % BUF][:, c, :],
                                 start=n == 0, stop=n == NS - 1)
                    ins.then_inc(s["y_mm"], 1)

                def project_out(u, d, fronts):
                    pe.wait_ge(s["ys_ready"], u + 1)
                    if due(u):
                        pe.wait_ge(s["x_ready"], u)
                    if fronts:
                        pe.wait_ge(s["silu_ready"], 3 * (u + 2) + 2)
                    else:
                        pe.wait_ge(s["dt_abs"], 4 * NG * CH // 2)
                        pe.wait_ge(s["dt_relu"], 4 * NG * CH // 2)
                    for i in range(GS):
                        for c in range(CH):
                            ins = mm(pm[0][:, i * D:(i + 1) * D], ys[:, c, i * T:(i + 1) * T],
                                     W.outw[:, d, c, :], start=c == 0, stop=c == CH - 1)
                    ins.then_inc(s["o_mm"], 1)

                def scan(g, d, nxt):
                    u = 2 * g + d
                    first = isinstance(u, int) and u == 0
                    if first:
                        spread(u, 0, d)
                    for n in range(NS):
                        if n + 1 < NS:
                            spread(u, n + 1, d)
                        elif nxt:
                            spread(u + 1, 0, 1 - d)
                        if nxt:
                            nxt(n)
                        if n >= LAG:
                            add_state(u, n - LAG)
                        elif not first:
                            add_state(u - 1, NS + n - LAG)
                        if n == 8 and not first:
                            project_out(u - 1, 1 - d, nxt)
                    if not nxt:
                        for n in range(NS - LAG, NS):
                            add_state(u, n)
                        project_out(u, d, nxt)

                drive(pe, front, scan, par)

            @block.scalar
            def _(act):
                A_ = nc.scalar.activation
                act.wait_ge(W.loaded, W.all())
                A_(aexp[:, :, :, :], W.alog[:, :, :, :], ACT.Exp).then_inc(s["aexp_ready"], 1)
                act.wait_ge(s["prep"], 3)
                act.wait_ge(s["seg_zero"], BUF + 1)
                par = [0]

                def front(g, d, at=None):
                    u = 2 * g + d
                    if d == 0 and at in (None, 1):
                        act.wait_ge(s["lnT_mm"], g + 1)
                        if due(2 * CH * (g - 1)):
                            act.wait_ge(s["u_mm"], 2 * CH * (g - 1))
                        A_(xnT[:, par[0], :, PAD:PAD + T], pm[0][:, :].rearrange("p (i t) -> p i t", t=T),
                           ACT.Identity, bias=W.beta[:, 0:1], scale=W.gamma[:, 0:1]).then_inc(s["lnT_ready"], 1)
                    if at in (None, 6):
                        if due(u - 1):
                            act.wait_ge(s["ys_ready"], u - 1)
                        for c in range(CH):
                            act.wait_ge(s["u_mm"], CH * u + c + 1)
                            A_(us[d][:, c, :], pm[1 - c][:, :], ACT.Silu,
                               bias=W.convb[:, d, c:c + 1]).then_inc(s["silu_ready"], 1)
                        act.wait_ge(s["z_raw"], CH * u + CH)
                        A_(zs[d][:, :, :], zraw[:, :, :], ACT.Silu).then_inc(s["silu_ready"], 1)
                    if at in (None, 8):
                        act.wait_ge(s["row_mm"], u + 1)
                        if due(CH * u):
                            act.wait_ge(s["dt_mm"], CH * u)
                        A_(dtrow[96:96 + DR, :], pm[1][96:96 + DR, :], ACT.Copy).then_inc(s["dtrow_ready"], 1)
                        if due(NS * (u - 1)):
                            act.wait_ge(s["c_mm"], NS * (u - 1))
                        A_(bcrow[d][0:96, :], pm[1][0:96, :], ACT.Copy).then_inc(s["row_hi"], 1)
                    if at in (None, 10):
                        act.wait_ge(s["row_rest"], u + 1)
                        for q in (1, 2):
                            A_(bcrow[d][32 * q:32 * q + 32, :], rest[32 * q:32 * q + 32, :],
                               ACT.Copy).then_inc(s["row_mid"], 1)
                    if at in (None, 11):
                        for c in range(CH):
                            act.wait_ge(s["dt_mm"], CH * u + c + 1)
                            if c == 0:
                                if due(u):
                                    act.wait_ge(s["dt_ready"], u)
                            A_(pre[:, c, :], pm[c][:, :], ACT.Abs,
                               bias=W.dtb[:, d, c:c + 1]).then_inc(s["dt_abs"], 1)
                        act.wait_ge(s["dt_abs"], CH * (u + 1))
                        if due(2 * u):
                            act.wait_ge(s["dt_soft"], 2 * u)
                        A_(soft[:, :, :], pre[:, :, :], ACT.Exp, scale=-1.0).then_inc(s["dt_soft"], 1)
                        act.wait_ge(s["dt_soft"], 2 * u + 1)
                        A_(pre[:, :, :], soft[:, :, :], ACT.Ln, bias=1.0).then_inc(s["dt_soft"], 1)

                def scan(g, d, nxt):
                    u = 2 * g + d
                    lo = 1 - d
                    for n in range(NS):
                        N = NS * u + n
                        act.wait_ge(s["c_mm"], N + 1)
                        if due(N + 1 - BUF):
                            act.wait_ge(s["hc_ready"], N + 1 - BUF)
                        A_(cs[n % BUF][:, :], pc[n % 2][:, :], ACT.Copy).then_inc(s["c_ready"], 1)
                        if n == 0:
                            act.wait_ge(s["dt_ready"], u + 1)
                        if due(N + 1 - BUF):
                            act.wait_ge(s["h_ready"], N + 1 - BUF)
                        for c in range(CH):
                            dst = da[n % BUF][:, c * GT:(c + 1) * GT].rearrange("p (i t) -> p i t", t=T)[:, :, 1:T]
                            src = dt[d][:, c, :].rearrange("p (i t) -> p i t", t=T)[:, :, lo:lo + T - 1]
                            A_(dst, src, ACT.Exp, scale=aneg[:, d, c, n:n + 1]).then_inc(s["da_ready"], 1)
                        if nxt:
                            nxt(n)

                drive(act, front, scan, par)

            @block.vector
            def _(dve):
                V = nc.vector
                dve.wait_ge(W.loaded, W.all())
                for d in range(2):
                    ins = V.tensor_tensor(wtap[:, d], W.convw[:, d], bc(W.win_u[:, d], 1, TAPS), ALU.mult)
                ins.then_inc(s["prep"], 1)
                V.tensor_copy(sel[:, :, :], bc(W.sel32[:, :], 2, 128)).then_inc(s["prep"], 1)
                dve.wait_ge(s["aexp_ready"], 1)
                V.tensor_scalar(aneg[:, :, :, :], aexp[:, :, :, :], -1.0, None, ALU.mult).then_inc(s["prep"], 1)
                dve.wait_ge(s["rstd"], STEPS)
                par = [0]

                def norm(g):
                    if isinstance(g, int) and g == 1:
                        dve.wait_ge(s["rstd"], 2 * STEPS)
                    if due(g):
                        dve.wait_ge(s["lnT_mm"], g)
                    for i in range(GS):
                        b = bass.ds(g * GS + i, 1)
                        ins = V.tensor_scalar(xh[:, i:i + 1, :], S.x[:, b, :], S.mean[:, b],
                                              r12[:, b], ALU.subtract, ALU.mult)
                    ins.then_inc(s["xh_ready"], 1)
                    dve.wait_ge(s["xh_ready"], g + 1)
                    for i in range(GS):
                        b = bass.ds(g * GS + i, 1)
                        ins = V.tensor_scalar(S.x[:, b, :], S.x[:, b, :], r1p[:, b], mr1[:, b],
                                              ALU.mult, ALU.subtract)
                    ins.then_inc(s["xres_ready"], 1)

                def front(g, d, at=None):
                    u = 2 * g + d
                    if at is None:
                        norm(g)
                    if d == 1 and at == 5 and not (isinstance(g, int) and g + 1 == NG):
                        norm(g + 1)
                    if at in (None, 2):
                        if due(3 * u):
                            dve.wait_ge(s["silu_ready"], 3 * u)
                        for c in range(CH):
                            dve.wait_ge(s["z_mm"], CH * u + c + 1)
                            V.tensor_copy(zraw[:, c, :], pm[1 - c][:, :]).then_inc(s["z_raw"], 1)
                    if at in (None, 9):
                        dve.wait_ge(s["row_hi"], u + 1)
                        if due(2 * u):
                            dve.wait_ge(s["row_mid"], 2 * u)
                        if due(u):
                            dve.wait_ge(s["row_ready"], u)
                        V.tensor_tensor(rest[0:96, :], pm[1][0:96, :], bcrow[d][0:96, :],
                                        ALU.subtract).then_inc(s["row_rest"], 1)
                    if at in (None, 11):
                        dve.wait_ge(s["row_mid"], 2 * u + 2)
                        V.tensor_tensor(bcrow[d][64:96, :], rest[64:96, :], bcrow[d][64:96, :],
                                        ALU.subtract).then_inc(s["row_ready"], 1)
                    if at in (None, 12):
                        if due(u):
                            dve.wait_ge(s["dt_ready"], u)
                        for c in range(CH):
                            dve.wait_ge(s["dt_mm"], CH * u + c + 1)
                            dve.wait_ge(s["dt_abs"], CH * u + c + 1)
                            V.tensor_scalar(relu[:, c, :], pm[c][:, :], W.dtb[:, d, c:c + 1], 0.0,
                                            ALU.add, ALU.max).then_inc(s["dt_relu"], 1)
                    if at in (None, 13):
                        dve.wait_ge(s["dt_relu"], CH * (u + 1))
                        if due(u - 1):
                            dve.wait_ge(s["du_ready"], u - 1)
                        dve.wait_ge(s["dt_soft"], 2 * u + 2)
                        if due(CH * NS * (u - 1)):
                            dve.wait_ge(s["da_ready"], CH * NS * (u - 1))
                        V.tensor_tensor(dt[d][:, :, :], relu[:, :, :], pre[:, :, :],
                                        ALU.add).then_inc(s["dt_ready"], 1)
                    if at in (None, 14):
                        dve.wait_ge(s["dt_ready"], u + 1)
                        dve.wait_ge(s["silu_ready"], 3 * u + CH)
                        if due(NS * (u - 1)):
                            dve.wait_ge(s["db_ready"], NS * (u - 1))
                        V.tensor_tensor(du[d][:, :, :], dt[d][:, :, :], us[d][:, :, :],
                                        ALU.mult).then_inc(s["du_ready"], 1)

                def step(u, n, d):
                    N = NS * u + n
                    if n == 0:
                        dve.wait_ge(s["du_ready"], u + 1)
                    dve.wait_ge(s["b_mm"], N + 1)
                    if due(N + 1 - BUF):
                        dve.wait_ge(s["h_ready"], N + 1 - BUF)
                    V.tensor_tensor(db[n % BUF][:, :].rearrange("p (c t) -> p c t", c=CH), du[d][:, :, :],
                                    bc(pb[n % 2][:, :], 1, CH), ALU.mult).then_inc(s["db_ready"], 1)

                def sum_up(u, d):
                    dve.wait_ge(s["y_mm"], NS * (u + 1))
                    if due(u):
                        dve.wait_ge(s["ys_ready"], u)
                    for c in range(CH):
                        V.scalar_tensor_tensor(y1[:, c, :], us[d][:, c, :], W.dskip[:, d, c:c + 1],
                                               py[:, c, :], ALU.mult, ALU.add).then_inc(s["y1_ready"], 1)

                def gate(u, d):
                    dve.wait_ge(s["y1_ready"], CH * (u + 1))
                    dve.wait_ge(s["silu_ready"], 3 * u + 3)
                    if due(u):
                        dve.wait_ge(s["o_mm"], u)
                    V.tensor_tensor(ys[:, :, :], y1[:, :, :], zs[d][:, :, :],
                                    ALU.mult).then_inc(s["ys_ready"], 1)

                def add_out(u, g, d):
                    dve.wait_ge(s["o_mm"], u + 1)
                    dve.wait_ge(s["xres_ready"], g + 1)
                    if due(u):
                        dve.wait_ge(s["x_ready"], u)
                    V.tensor_tensor(seqs(S.x, g), seqs(S.x, g),
                                    pm[0][:, :].rearrange("p (i t) -> p i t", t=T),
                                    ALU.add).then_inc(s["x_ready"], 1)
                    if d == 1:
                        dve.wait_ge(s["x_ready"], u + 1)
                        S.next_stats(dve, g, s["stats"])

                def scan(g, d, nxt):
                    u = 2 * g + d
                    first = isinstance(u, int) and u == 0
                    if first:
                        step(u, 0, d)
                    for n in range(NS):
                        N = NS * u + n
                        if n + 1 < NS:
                            step(u, n + 1, d)
                        elif nxt:
                            step(u + 1, 0, 1 - d)
                        if nxt:
                            nxt(n)
                        if not first:
                            if n == 2:
                                sum_up(u - 1, 1 - d)
                            if n == 3:
                                gate(u - 1, 1 - d)
                            if n == 9:
                                add_out(u - 1, g if d else g - 1, 1 - d)
                        dve.wait_ge(s["da_ready"], CH * (N + 1))
                        dve.wait_ge(s["db_ready"], N + 1)
                        if due(N + 1 - BUF):
                            dve.wait_ge(s["hc_ready"], N + 1 - BUF)
                        way = slice(None, None, -1 if d else None)
                        V.tensor_tensor_scan(h[n % BUF][:, way], da[n % BUF][:, d:d + CH * GT][:, way],
                                             db[n % BUF][:, way], 0.0, ALU.mult, ALU.add
                                             ).then_inc(s["h_ready"], 1)
                    if not nxt:
                        sum_up(u, d)
                        gate(u, d)
                        add_out(u, g, d)

                drive(dve, front, scan, par)

            @block.gpsimd
            def _(pool):
                P = nc.gpsimd
                P.memset(xnT[:, :, :, :], 0.0).then_inc(s["seg_zero"], 1)
                for k in range(BUF):
                    P.memset(da[k][:, :], 0.0).then_inc(s["seg_zero"], 1)
                for part, cols in enumerate(LN_PARTS):
                    done = part * STEPS
                    S.ln_scalars(pool, s["rstd"], LN_EPS, cols, done)
                    r1, var, mean = S.rstd[:, cols], S.var[:, cols], S.mean[:, cols]
                    P.tensor_tensor(r1sq[:, cols], r1, r1, ALU.mult).then_inc(s["rstd"], 1)
                    pool.wait_ge(s["rstd"], done + LN_STEPS + 1)
                    P.tensor_tensor(v2[:, cols], var, r1sq[:, cols], ALU.mult).then_inc(s["rstd"], 1)
                    pool.wait_ge(s["rstd"], done + LN_STEPS + 2)
                    P.tensor_scalar(ve[:, cols], v2[:, cols], LN_EPS, None, ALU.add).then_inc(s["rstd"], 1)
                    pool.wait_ge(s["rstd"], done + LN_STEPS + 3)
                    P.tensor_tensor(r2[:, cols], ve[:, cols], S.minus_half[:, cols], ALU.pow).then_inc(s["rstd"], 1)
                    pool.wait_ge(s["rstd"], done + LN_STEPS + 4)
                    P.tensor_tensor(r12[:, cols], r1, r2[:, cols], ALU.mult).then_inc(s["rstd"], 1)
                    P.tensor_scalar(r1p[:, cols], r1, 1.0, None, ALU.add).then_inc(s["rstd"], 1)
                    P.tensor_tensor(mr1[:, cols], mean, r1, ALU.mult).then_inc(s["rstd"], 1)
                par = [0]

                def front(g, d, at=None):
                    pass

                def scan(g, d, nxt):
                    u = 2 * g + d
                    for n in range(NS):
                        N = NS * u + n
                        if nxt:
                            nxt(n)
                        pool.wait_ge(s["h_ready"], N + 1)
                        pool.wait_ge(s["c_ready"], N + 1)
                        if due(N + 1 - BUF):
                            pool.wait_ge(s["y_mm"], N + 1 - BUF)
                        P.tensor_tensor(hc[n % BUF][:, :, :],
                                        h[n % BUF][:, :].rearrange("p (c t) -> p c t", c=CH),
                                        bc(cs[n % BUF][:, :], 1, CH),
                                        ALU.mult).then_inc(s["hc_ready"], 1)

                drive(pool, front, scan, par)


def cross_weights(nc, ctx, w, full_mask):
    W = Weights(nc, ctx, f"xw{full_mask}_")
    W.wq, W.wk, W.wv, W.wo = (W.tile(n, [128, 128], w[n]) for n in ("wq", "wk", "wv", "wo"))
    W.bq, W.bk = W.tile("bq", [128, 1], w["bq"]), W.tile("bk", [128, 1], w["bk"])
    W.bv = W.tile("bv", [TC, 128], w["bv"].partition_broadcast(TC))
    W.bo = W.tile("bo", [128, 128], w["bo"].partition_broadcast(128))
    W.hmask = W.tile("hmask", [128, HX], w["hmask"])
    return W


def cross_attention_layer(nc, S, w, full_mask, W, ahead):
    SCALE = DKX ** -0.5
    QK = QH * TC
    with ExitStack() as ctx:
        A = Alloc(nc, ctx, f"x{full_mask}_")
        bqs = A.sb("bqs", [128, 1])
        if full_mask:
            mask = [A.sb(f"mask{p}", [128, TC], I32) for p in range(2)]
            out_of = [A.sb(f"out_of{p}", [128, TC], I32) for p in range(2)]
            fill = A.sb("fill", [128, 1])
        else:
            mrow = A.sb("mrow", [128, NB * TC], I32)
            keep = A.sb("keep", [128, NB * TC])
            some = A.sb("some", [128, NB])
            brow = A.sb("brow", [1, NB * TC], BF16)
            ones = A.sb("ones", [1, 128], BF16)
        ctxT = [A.sb(f"ctxT{p}", [128, TC]) for p in range(2)]
        xh = A.sb("xh", [128, 1, D])
        xT = A.sb("xT", [128, T])
        qT = [A.sb(f"qT{p}", [128, T]) for p in range(2)]
        kT = A.sb("kT", [128, TC])
        kd = [A.sb(f"kd{p}", [128, HX, TC]) for p in range(2)]
        v_early = [A.sb(f"v_early{p}", [TC, 128]) for p in range(2)]
        VSTEP = W4 + DKX
        va = [A.sb(f"va{p}", [TC, NQ, QH * VSTEP]) for p in range(2)]
        top, den, rden = ([A.sb(f"{n}{q}", [128, QH]) for q in range(NQ)] for n in ("top", "den", "rden"))
        pr = [A.sb(f"pr{q}", [128, QH, TC]) for q in range(NQ)]
        prT = [A.sb(f"prT{q}", [TC, QH * T]) for q in range(2)]
        cT = A.sb("cT", [128, T])
        ps = [A.ps(f"ps{k}", [128, 512]) for k in range(2)]
        pt = [A.ps(f"pt{k}", [128, QH * T]) for k in range(2)]
        py = [A.ps(f"py{k}", [128, 512]) for k in range(2)]
        px = A.ps("px", [128, 512])
        pqkv = A.ps("pqkv", [128, 512])
        s = {n: A.sem(n) for n in """mrow_in prep rstd xh_ready xb_ready t_mm xT_ready qkv_mm q_ready
            ve_ready v_ready kd_ready s_mm filled top_ready sub_ready exp_ready den_ready rden_ready norm_ready
            pt_mm prT_ready y_mm cT_ready o_mm x_ready stats out_of_ready keep va_zero""".split()}
        ctx_in = [A.sem(f"ctx_in{p}") for p in range(2)]
        mask_in = [A.sem(f"mask_in{p}") for p in range(2)]
        V0 = T + TC

        with nc.Block() as block:

            @block.sync
            def _(sp):
                if not full_mask:
                    sp.dma_start(mrow[:, :], w["mrow"].partition_broadcast(128)).then_inc(s["mrow_in"], 16)

                def load(b):
                    if due(b.n - 1):
                        sp.wait_ge(s["qkv_mm"], b.n - 1)
                    sp.dma_start(ctxT[b.p][:, :], w["ctxT"][:, bass.ds(b.n * TC, TC)]).then_inc(ctx_in[b.p], 16)
                    if full_mask:
                        if due(b.n - 1):
                            sp.wait_ge(s["out_of_ready"], b.n - 1)
                        sp.dma_start(mask[b.p][:, :], w["mask"][bass.ds(b.n, 1)].squeeze(0)
                                     ).then_inc(mask_in[b.p], 16)
                load(Seq(0, 0))
                load(Seq(0, 1))
                ahead.load(sp)
                with sp.Fori(1, NB // 2) as j:
                    load(Seq(j, 0))
                    load(Seq(j, 1))

            @block.tensor
            def _(pe):
                mm, tr = nc.tensor.matmul, nc.tensor.transpose
                pe.wait_ge(W.loaded, W.all())
                pe.wait_ge(s["prep"], 1)

                def turn(b, q):
                    t = b.quad(q)
                    pe.wait_ge(s["norm_ready"], t + 1)
                    if due(t - 1):
                        pe.wait_ge(s["prT_ready"], t - 1)
                    for i in range(QH):
                        ins = tr(pt[q % 2][0:TC, i * T:(i + 1) * T], pr[q][:, i, :], S.ident[:, :])
                    ins.then_inc(s["pt_mm"], 1)

                def scores(b, q):
                    t = b.quad(q)
                    pe.wait_ge(s["kd_ready"], t + 1)
                    if q == 0:
                        pe.wait_ge(s["q_ready"], b.n + 1)
                    if due(t - 1):
                        pe.wait_ge(s["sub_ready"], t - 1)
                    out = ps[q % 2][:, 0:QK]
                    ins = mm(out, qT[b.p][:, :], kd[b.p][:, QH * q:QH * q + QH, :],
                             start=True, stop=bool(full_mask))
                    if not full_mask:
                        row = bc(brow[0:1, bass.ds(b.n * TC, TC)], 1, QH)
                        ins = mm(out, ones[:, :], row, start=False, stop=True)
                    ins.then_inc(s["s_mm"], 1)

                def values(b, q):
                    t = b.quad(q)
                    pe.wait_ge(s["prT_ready"], t + 1)
                    if q == 0:
                        pe.wait_ge(s["v_ready"], b.n + 1)
                        if due(b.n - 1):
                            pe.wait_ge(s["cT_ready"], b.n - 1)
                    for i in range(QH):
                        ins = mm(py[b.p][W4 * q:W4 * q + W4, 0:T], va[b.p][:, q, W4 * i:W4 * i + W4],
                                 prT[q % 2][:, i * T:(i + 1) * T], start=i == 0, stop=i == QH - 1)
                    ins.then_inc(s["y_mm"], 1)

                def slot(b, q):
                    if b.real():
                        turn(b, q)
                    nxt = b.plus(1)
                    if nxt.real():
                        scores(nxt, q)
                    n = b.plus(3)
                    o = b.plus(-1)
                    if q == 1 and n.real():
                        pe.wait_ge(s["xh_ready"], n.n + 1)
                        if due(n.n - 4):
                            pe.wait_ge(s["x_ready"], n.n - 4)
                        tr(px[:, 0:T], xh[:, 0, :], S.ident[:, :]).then_inc(s["t_mm"], 1)
                    if q == 2 and n.real():
                        pe.wait_ge(s["xT_ready"], n.n + 1)
                        pe.wait_ge(ctx_in[n.p], 16 * (n.j + 1))
                        if due(n.n):
                            pe.wait_ge(s["q_ready"], n.n)
                        if due(n.n):
                            pe.wait_ge(s["ve_ready"], n.n)
                        mm(pqkv[:, 0:T], W.wq[:, :], xT[:, :], start=True, stop=True)
                        mm(pqkv[:, T:V0], W.wk[:, :], ctxT[n.p][:, :], start=True, stop=True)
                        mm(pqkv[0:TC, V0:V0 + 128], ctxT[n.p][:, :], W.wv[:, :], start=True, stop=True
                           ).then_inc(s["qkv_mm"], 1)
                    if q == 2 and o.real():
                        pe.wait_ge(s["cT_ready"], o.n + 1)
                        if due(o.n):
                            pe.wait_ge(s["x_ready"], o.n)
                        if n.real():
                            pe.wait_ge(s["xT_ready"], n.n + 1)
                        mm(px[:, T:2 * T], cT[:, :], W.wo[:, :], start=True, stop=True).then_inc(s["o_mm"], 1)
                    last = b if q else b.plus(-1)
                    if last.real():
                        values(last, (q - 1) % NQ)

                walk_sequences(pe, slot, 3)

            @block.scalar
            def _(act):
                A_ = nc.scalar.activation
                act.wait_ge(W.loaded, W.all())
                act.wait_ge(s["prep"], 1)

                def slot(b, q):
                    e = b if q < 2 else b.plus(1)
                    if e.real():
                        qe = (q + 2) % NQ
                        act.wait_ge(s["sub_ready"], e.quad(qe) + 1)
                        A_(pr[qe][:, :, :], pr[qe][:, :, :], ACT.Exp).then_inc(s["exp_ready"], 1)
                    if b.real():
                        t = b.quad(q)
                        act.wait_ge(s["pt_mm"], t + 1)
                        if due(t - 1):
                            act.wait_ge(s["y_mm"], t - 1)
                        A_(prT[q % 2][:, :], pt[q % 2][0:TC, :], ACT.Copy).then_inc(s["prT_ready"], 1)
                    n = b.plus(3)
                    m = b.plus(2)
                    if q == 1 and n.real():
                        act.wait_ge(s["t_mm"], n.n + 1)
                        if due(n.n):
                            act.wait_ge(s["qkv_mm"], n.n)
                        A_(xT[:, :], px[:, 0:T], ACT.Copy).then_inc(s["xT_ready"], 1)
                    if q == 0 and m.real():
                        act.wait_ge(s["qkv_mm"], m.n + 1)
                        if due(NQ * m.n):
                            act.wait_ge(s["kd_ready"], NQ * m.n)
                        A_(kT[:, :], pqkv[:, T:V0], ACT.Identity, bias=W.bk[:, 0:1])
                        if due(NQ * (m.n - 1)):
                            act.wait_ge(s["s_mm"], NQ * (m.n - 1))
                        A_(qT[m.p][:, :], pqkv[:, 0:T], ACT.Identity, bias=bqs[:, 0:1], scale=SCALE
                           ).then_inc(s["q_ready"], 1)
                walk_sequences(act, slot, 3)

            @block.vector
            def _(dve):
                V = nc.vector
                dve.wait_ge(W.loaded, W.all())
                for p in range(2):
                    V.memset(va[p][:, :, :], 0.0).then_inc(s["va_zero"], 1)
                if full_mask:
                    V.memset(fill[:, :], -1.0e9)
                else:
                    V.memset(ones[:, :], 1.0)
                    dve.wait_ge(s["mrow_in"], 16)
                    V.tensor_scalar(brow[:, :], mrow[0:1, :], 0.0, MASKED, ALU.is_equal, ALU.mult)
                    V.tensor_scalar(keep[:, :], mrow[:, :], 0.0, None, ALU.not_equal).then_inc(s["keep"], 1)
                    dve.wait_ge(s["keep"], 1)
                    V.tensor_reduce(some[:, :], keep[:, :].rearrange("p (b k) -> p b k", k=TC), AX.X, ALU.max)
                V.tensor_scalar(bqs[:, :], W.bq[:, :], SCALE, None, ALU.mult).then_inc(s["prep"], 1)
                dve.wait_ge(s["prep"], 1)
                dve.wait_ge(s["rstd"], LN_STEPS)
                dve.wait_ge(s["va_zero"], 2)

                def slot(b, q):
                    d = b if q < 3 else b.plus(1)
                    a = b if q < 1 else b.plus(1)
                    qd, qa = (q + 1) % NQ, (q + 3) % NQ
                    if a.real():
                        dve.wait_ge(s["s_mm"], a.quad(qa) + 1)
                        if full_mask and qa == 0:
                            dve.wait_ge(s["out_of_ready"], a.n + 1)
                    if d.real():
                        t = d.quad(qd)
                        dve.wait_ge(s["exp_ready"], t + 1)
                        if due(t - 3):
                            dve.wait_ge(s["rden_ready"], t - 3)
                        V.tensor_reduce(den[qd][:, :], pr[qd][:, :, :], AX.X, ALU.add).then_inc(s["den_ready"], 1)
                    if a.real():
                        t = a.quad(qa)
                        sc = ps[qa % 2][:, 0:QK].rearrange("p (h k) -> p h k", k=TC)
                        if full_mask:
                            V.copy_predicated(sc, bc(out_of[a.p][:, :], 1, QH),
                                              bc(fill[:, :], 1, QH).to_broadcast([128, QH, TC])
                                              ).then_inc(s["filled"], 1)
                    if d.real():
                        t = d.quad(qd)
                        dve.wait_ge(s["den_ready"], t + 1)
                        if due(t - 3):
                            dve.wait_ge(s["norm_ready"], t - 3)
                        V.reciprocal(rden[qd][:, :], den[qd][:, :]).then_inc(s["rden_ready"], 1)
                    if a.real():
                        t = a.quad(qa)
                        if full_mask:
                            dve.wait_ge(s["filled"], t + 1)
                        V.tensor_reduce(top[qa][:, :], sc, AX.X, ALU.max).then_inc(s["top_ready"], 1)
                    n = b.plus(3)
                    m = b.plus(2)
                    c = b.plus(1)
                    o = b.plus(-1)
                    if q == 0 and n.real():
                        if isinstance(n.n, int) and n.n == GS:
                            dve.wait_ge(s["rstd"], 2 * LN_STEPS)
                        if due(n.n):
                            dve.wait_ge(s["t_mm"], n.n)
                        i = bass.ds(n.n, 1)
                        V.tensor_scalar(xh[:, :, :], S.x[:, i, :], S.mean[:, i], S.rstd[:, i],
                                        ALU.subtract, ALU.mult).then_inc(s["xh_ready"], 1)
                    if q == 0 and c.real() and full_mask:
                        dve.wait_ge(mask_in[c.p], 16 * (c.j + 1))
                        if due(NQ * (c.n - 1)):
                            dve.wait_ge(s["filled"], NQ * (c.n - 1))
                        V.tensor_scalar(out_of[c.p][:, :], mask[c.p][:, :], 0.0, None, ALU.is_equal
                                        ).then_inc(s["out_of_ready"], 1)
                    if q == 1 and o.real():
                        dve.wait_ge(s["y_mm"], NQ * (o.n + 1))
                        if due(o.n):
                            dve.wait_ge(s["o_mm"], o.n)
                        y = py[o.p][:, 0:T]
                        if full_mask:
                            V.tensor_copy(cT[:, :], y).then_inc(s["cT_ready"], 1)
                        else:
                            V.tensor_scalar(cT[:, :], y, some[:, bass.ds(o.n, 1)], None, ALU.mult
                                            ).then_inc(s["cT_ready"], 1)
                    if q == 1 and m.real():
                        dve.wait_ge(s["q_ready"], m.n + 1)
                        if due(m.n - 1):
                            dve.wait_ge(s["v_ready"], m.n - 1)
                        V.tensor_tensor(v_early[m.p][:, :], pqkv[0:TC, V0:V0 + 128], W.bv[:, :], ALU.add
                                        ).then_inc(s["ve_ready"], 1)
                    if q == 2 and c.real():
                        dve.wait_ge(s["ve_ready"], c.n + 1)
                        if due(NQ * (c.n - 1)):
                            dve.wait_ge(s["y_mm"], NQ * (c.n - 1))
                        V.tensor_copy(va[c.p][:, :, :].rearrange("p a (i x) -> p a i x", x=VSTEP)[:, :, :, 0:DKX],
                                      v_early[c.p][:, :].rearrange("p (a i d) -> p a i d", i=QH, d=DKX)
                                      ).then_inc(s["v_ready"], 1)
                    if q == 3 and o.real():
                        i = bass.ds(o.n, 1)
                        dve.wait_ge(s["o_mm"], o.n + 1)
                        dve.wait_ge(s["xb_ready"], o.n + 1)
                        V.tensor_tensor(S.x[:, i, :], S.x[:, i, :], bc(px[:, T:2 * T], 1, 1), ALU.add
                                        ).then_inc(s["x_ready"], 1)
                        dve.wait_ge(s["x_ready"], o.n + 1)
                        V.bn_stats(S.bn[:, i, :], S.x[:, i, :]).then_inc(s["stats"], 1)
                    if a.real():
                        t = a.quad(qa)
                        dve.wait_ge(s["top_ready"], t + 1)
                        if due(t - 3):
                            dve.wait_ge(s["pt_mm"], t - 3)
                        V.tensor_tensor(pr[qa][:, :, :], sc, bc(top[qa][:, :], 2, TC), ALU.subtract
                                        ).then_inc(s["sub_ready"], 1)

                walk_sequences(dve, slot, 3)

            @block.gpsimd
            def _(pool):
                P = nc.gpsimd
                pool.wait_ge(W.loaded, W.all())
                for part, cols in enumerate(LN_PARTS):
                    S.ln_scalars(pool, s["rstd"], LN_EPS, cols, part * LN_STEPS)

                def slot(b, q):
                    d = b if q < 3 else b.plus(1)
                    if d.real():
                        qd = (q + 1) % NQ
                        pool.wait_ge(s["rden_ready"], d.quad(qd) + 1)
                        P.tensor_tensor(pr[qd][:, :, :], pr[qd][:, :, :], bc(rden[qd][:, :], 2, TC), ALU.mult
                                        ).then_inc(s["norm_ready"], 1)
                    m = b.plus(2)
                    if m.real():
                        pool.wait_ge(s["q_ready"], m.n + 1)
                        if due(NQ * (m.n - 2) + q + 1):
                            pool.wait_ge(s["s_mm"], NQ * (m.n - 2) + q + 1)
                        quad = slice(QH * q, QH * q + QH)
                        P.tensor_tensor(kd[m.p][:, quad, :], bc(kT[:, :], 1, QH), bc(W.hmask[:, quad], 2, TC), ALU.mult
                                        ).then_inc(s["kd_ready"], 1)
                    if q == 3 and m.real():
                        i = bass.ds(m.n, 1)
                        pool.wait_ge(s["xh_ready"], m.n + 1)
                        P.tensor_tensor(S.x[:, i, :], S.x[:, i, :], bc(W.bo[:, :], 1, 1), ALU.add
                                        ).then_inc(s["xb_ready"], 1)

                walk_sequences(pool, slot, 3)


def moe_top2_weights(nc, ctx, w):
    W = Weights(nc, ctx, "cw_")
    W.router = W.tile("router", [128, E0], w["router"])
    W.bias = W.tile("bias", [128, E0], w["bias"].partition_broadcast(128))
    W.order = W.tile("order", [128, E0], w["order"].partition_broadcast(128))
    W.gu = W.tile("gu", [128, E0 + 1, 2, M0], w["gu"])
    W.down = W.tile("down", [128, E0 + 1, M0 // 128, D], w["down"])
    return W


def moe_top2_layer(nc, S, W, ahead):
    NE, MC = E0 + 1, M0 // 128
    BELOW = -1.0e38
    with ExitStack() as ctx:
        A = Alloc(nc, ctx, "c_")
        gu_hi, gu_lo = (A.sb(n, [128, NE, 2, M0], F32R) for n in ("gu_hi", "gu_lo"))
        xh = [A.sb(f"xh{p}", [128, GS, D]) for p in range(2)]
        xT = [A.sb(f"xT{p}", [128, GT]) for p in range(2)]
        x_hi, x_lo = (A.sb(n, [128, NG, GT], F32R) for n in ("x_hi", "x_lo"))
        logits, sigm, sel, best, first, second, c = (
            A.sb(n, [128, NB, E0]) for n in ("logits", "sigm", "sel", "best", "first", "second", "c"))
        top, pick = A.sb("top", [128, NB]), A.sb("pick", [128, NB])
        with ExitStack() as ctx1:
            B = Alloc(nc, ctx1, "c1_")
            pt = [B.ps(f"pt{k}", [128, GT]) for k in range(2)]
            pl = B.ps("pl", [128, NB, E0])
            s = {n: B.sem(n) for n in """rstd xh_ready t_mm xT_ready hi_ready lo_ready l_mm gu_hi_ready
                gu_lo_ready l_ready sigm_ready route""".split()}
            with nc.Block() as block:

                @block.sync
                def _(sp):
                    ahead.load(sp)

                @block.tensor
                def _(pe):
                    pe.wait_ge(W.loaded, W.all())

                    def body(g, p):
                        pe.wait_ge(s["xh_ready"], g + 1)
                        if due(g - 1):
                            pe.wait_ge(s["xT_ready"], g - 1)
                        for i in range(GS):
                            ins = nc.tensor.transpose(pt[p][:, i * T:(i + 1) * T], xh[p][:, i, :], S.ident[:, :])
                        ins.then_inc(s["t_mm"], 1)
                        pe.wait_ge(s["xT_ready"], g + 1)
                        for i in range(GS):
                            ins = nc.tensor.matmul(pl[:, bass.ds(g * GS + i, 1), :], xT[p][:, i * T:(i + 1) * T],
                                                   W.router[:, :], start=True, stop=True)
                        ins.then_inc(s["l_mm"], 1)
                    walk_groups(pe, body)

                @block.scalar
                def _(act):
                    A_ = nc.scalar.activation

                    def body(g, p):
                        act.wait_ge(s["t_mm"], g + 1)
                        if due(g - 1):
                            act.wait_ge(s["l_mm"], g - 1)
                        if due(g - 1):
                            act.wait_ge(s["lo_ready"], g - 1)
                        A_(xT[p][:, :], pt[p][:, :], ACT.Copy).then_inc(s["xT_ready"], 1)
                        act.wait_ge(s["xT_ready"], g + 1)
                        A_(x_hi[:, bass.ds(g, 1), :], bc(xT[p][:, :], 1, 1), ACT.Copy).then_inc(s["hi_ready"], 1)
                    walk_groups(act, body)
                    act.wait_ge(W.loaded, W.all())
                    A_(gu_hi[:, :, :, :], W.gu[:, :, :, :], ACT.Copy).then_inc(s["gu_hi_ready"], 1)
                    act.wait_ge(s["l_ready"], 1)
                    A_(sigm[:, :, :], logits[:, :, :], ACT.Sigmoid).then_inc(s["sigm_ready"], 1)

                @block.vector
                def _(dve):
                    V = nc.vector
                    dve.wait_ge(s["rstd"], LN_STEPS)

                    def body(g, p):
                        if isinstance(g, int) and g == 1:
                            dve.wait_ge(s["rstd"], 2 * LN_STEPS)
                        if due(g - 1):
                            dve.wait_ge(s["t_mm"], g - 1)
                        for i in range(GS):
                            b = bass.ds(g * GS + i, 1)
                            ins = V.tensor_scalar(xh[p][:, i:i + 1, :], S.x[:, b, :], S.mean[:, b],
                                                  S.rstd[:, b], ALU.subtract, ALU.mult)
                        ins.then_inc(s["xh_ready"], 1)
                    walk_groups(dve, body)
                    dve.wait_ge(s["l_mm"], NG)
                    dve.wait_ge(W.loaded, W.all())
                    V.tensor_copy(logits[:, :, :], pl[:, :, :]).then_inc(s["l_ready"], 1)
                    dve.wait_ge(s["l_ready"], 1)

                    V.tensor_tensor(sel[:, :, :], logits[:, :, :], bc(W.bias[:, :], 1, NB), ALU.add).then_inc(s["route"], 1)
                    dve.wait_ge(s["route"], 1)
                    V.tensor_reduce(top[:, :], sel[:, :, :], AX.X, ALU.max).then_inc(s["route"], 1)
                    dve.wait_ge(s["route"], 2)
                    V.tensor_tensor(best[:, :, :], sel[:, :, :], bc(top[:, :], 2, E0), ALU.is_equal).then_inc(s["route"], 1)
                    dve.wait_ge(s["route"], 3)
                    V.tensor_tensor(best[:, :, :], best[:, :, :], bc(W.order[:, :], 1, NB), ALU.mult).then_inc(s["route"], 1)
                    dve.wait_ge(s["route"], 4)
                    V.tensor_reduce(pick[:, :], best[:, :, :], AX.X, ALU.max).then_inc(s["route"], 1)
                    dve.wait_ge(s["route"], 5)
                    V.tensor_tensor(first[:, :, :], best[:, :, :], bc(pick[:, :], 2, E0), ALU.is_equal).then_inc(s["route"], 1)
                    dve.wait_ge(s["route"], 6)
                    V.scalar_tensor_tensor(sel[:, :, :], first[:, :, :], BELOW, sel[:, :, :], ALU.mult, ALU.add).then_inc(s["route"], 1)
                    dve.wait_ge(s["route"], 7)
                    V.tensor_reduce(top[:, :], sel[:, :, :], AX.X, ALU.max).then_inc(s["route"], 1)
                    dve.wait_ge(s["route"], 8)
                    V.tensor_tensor(best[:, :, :], sel[:, :, :], bc(top[:, :], 2, E0), ALU.is_equal).then_inc(s["route"], 1)
                    dve.wait_ge(s["route"], 9)
                    V.tensor_tensor(best[:, :, :], best[:, :, :], bc(W.order[:, :], 1, NB), ALU.mult).then_inc(s["route"], 1)
                    dve.wait_ge(s["route"], 10)
                    V.tensor_reduce(pick[:, :], best[:, :, :], AX.X, ALU.max).then_inc(s["route"], 1)
                    dve.wait_ge(s["route"], 11)
                    V.tensor_tensor(second[:, :, :], best[:, :, :], bc(pick[:, :], 2, E0), ALU.is_equal).then_inc(s["route"], 1)
                    dve.wait_ge(s["route"], 12)
                    V.tensor_tensor(first[:, :, :], first[:, :, :], second[:, :, :], ALU.add).then_inc(s["route"], 1)
                    dve.wait_ge(s["route"], 13)
                    dve.wait_ge(s["sigm_ready"], 1)
                    V.tensor_tensor(c[:, :, :], first[:, :, :], sigm[:, :, :], ALU.mult)
                    dve.wait_ge(s["gu_hi_ready"], 1)
                    V.tensor_tensor(gu_lo[:, :, :, :], W.gu[:, :, :, :], gu_hi[:, :, :, :].bitcast(F32),
                                    ALU.subtract).then_inc(s["gu_lo_ready"], 1)

                @block.gpsimd
                def _(pool):
                    for part, cols in enumerate(LN_PARTS):
                        S.ln_scalars(pool, s["rstd"], LN_EPS, cols, part * LN_STEPS)

                    def body(g, p):
                        pool.wait_ge(s["hi_ready"], g + 1)
                        b = bass.ds(g, 1)
                        nc.gpsimd.tensor_tensor(x_lo[:, b, :], bc(xT[p][:, :], 1, 1), x_hi[:, b, :].bitcast(F32),
                                                ALU.subtract).then_inc(s["lo_ready"], 1)
                    walk_groups(pool, body)

        act_of = [A.sb(f"act_of{k}", [128, GT]) for k in range(2)]
        h = [A.sb(f"h{k}", [128, MC, GT]) for k in range(2)]
        total = A.sb("total", [128, GS, D])
        pg = [A.ps(f"pg{k}", [128, GT]) for k in range(2)]
        pu = [A.ps(f"pu{k}", [128, GT]) for k in range(2)]
        pd = [A.ps(f"pd{k}", [128, GS, D]) for k in range(2)]
        s = {n: A.sem(n) for n in "g_mm u_mm silu_ready h_ready d_mm total_ready x_ready stats".split()}

        def walk(eng, unit):
            def both(j):
                for p in range(2):
                    for e in range(NE):
                        unit(2 * j + p, e, (p * NE + e) % 2)
            both(0)
            with eng.Fori(1, NG // 2) as j:
                both(j)

        with nc.Block() as block:

            @block.tensor
            def _(pe):
                mm = nc.tensor.matmul

                def project(g, e, k):
                    U = NE * g + e
                    xs = [x[:, bass.ds(g, 1), :] for x in (x_hi, x_lo)]
                    for c_ in range(MC):
                        cols = slice(c_ * 128, (c_ + 1) * 128)
                        if due(MC * (U - 1) + c_ + 1):
                            pe.wait_ge(s["silu_ready"], MC * (U - 1) + c_ + 1)
                        split_pass(mm, pg[c_][:, :], gu_hi[:, e, 0, cols], gu_lo[:, e, 0, cols], *xs,
                                   True, True).then_inc(s["g_mm"], 1)
                        if due(MC * (U - 1) + c_ + 1):
                            pe.wait_ge(s["h_ready"], MC * (U - 1) + c_ + 1)
                        split_pass(mm, pu[c_][:, :], gu_hi[:, e, 1, cols], gu_lo[:, e, 1, cols], *xs,
                                   True, True).then_inc(s["u_mm"], 1)

                def back(g, e, k):
                    U = NE * g + e
                    pe.wait_ge(s["h_ready"], MC * (U + 1))
                    if due(U - 1):
                        pe.wait_ge(s["total_ready"], U - 1)
                    for i in range(GS):
                        for c_ in range(MC):
                            ins = mm(pd[k][:, i, :], h[k][:, c_, i * T:(i + 1) * T], W.down[:, e, c_, :],
                                     start=c_ == 0, stop=c_ == MC - 1)
                    ins.then_inc(s["d_mm"], 1)

                def unit(g, e, k):
                    project(g, e, k)
                    if e:
                        back(g, e - 1, 1 - k)
                    elif not (isinstance(g, int) and g == 0):
                        back(g - 1, NE - 1, 1 - k)
                walk(pe, unit)
                back(NG - 1, NE - 1, (NG * NE - 1) % 2)

            @block.scalar
            def _(act):
                def unit(g, e, k):
                    U = NE * g + e
                    for c_ in range(MC):
                        act.wait_ge(s["g_mm"], MC * U + c_ + 1)
                        if due(MC * (U - 1) + c_ + 1):
                            act.wait_ge(s["h_ready"], MC * (U - 1) + c_ + 1)
                        nc.scalar.activation(act_of[c_][:, :], pg[c_][:, :], ACT.Silu).then_inc(s["silu_ready"], 1)
                walk(act, unit)

            @block.vector
            def _(dve):
                V = nc.vector

                def gated(g, e, k):
                    U = NE * g + e
                    for c_ in range(MC):
                        dve.wait_ge(s["silu_ready"], MC * U + c_ + 1)
                        dve.wait_ge(s["u_mm"], MC * U + c_ + 1)
                        if due(U - 1):
                            dve.wait_ge(s["d_mm"], U - 1)
                        V.tensor_tensor(h[k][:, c_, :], act_of[c_][:, :], pu[c_][:, :], ALU.mult
                                        ).then_inc(s["h_ready"], 1)

                def add(g, e, k):
                    U = NE * g + e
                    dve.wait_ge(s["d_mm"], U + 1)
                    if due(U):
                        dve.wait_ge(s["total_ready"], U)
                    if e == NE - 1:
                        V.tensor_tensor(total[:, :, :], total[:, :, :], pd[k][:, :, :], ALU.add
                                        ).then_inc(s["total_ready"], 1)
                        dve.wait_ge(s["total_ready"], U + 1)
                        V.tensor_tensor(seqs(S.x, g), seqs(S.x, g), total[:, :, :], ALU.add
                                        ).then_inc(s["x_ready"], 1)
                        dve.wait_ge(s["x_ready"], g + 1)
                        S.next_stats(dve, g, s["stats"])
                        return
                    if e == 0:
                        if due(g):
                            dve.wait_ge(s["x_ready"], g)
                    for i in range(GS):
                        weight = c[:, bass.ds(g * GS + i, 1), e]
                        if e == 0:
                            ins = V.tensor_scalar(total[:, i, :], pd[k][:, i, :], weight, None, ALU.mult)
                        else:
                            ins = V.scalar_tensor_tensor(total[:, i, :], pd[k][:, i, :], weight, total[:, i, :],
                                                         ALU.mult, ALU.add)
                    ins.then_inc(s["total_ready"], 1)

                def unit(g, e, k):
                    gated(g, e, k)
                    if e:
                        add(g, e - 1, 1 - k)
                    elif not (isinstance(g, int) and g == 0):
                        add(g - 1, NE - 1, 1 - k)
                walk(dve, unit)
                add(NG - 1, NE - 1, (NG * NE - 1) % 2)


def window_weights(nc, ctx, w):
    W = Weights(nc, ctx, "dw_")
    W.wq = W.tile("wq", [128, HL * HDL], w["wq"])
    W.wkv = W.tile("wkv", [128, 2 * KVL * HDL], w["wkv"])
    W.wo = W.tile("wo", [128, HL // 2, D], w["wo"])
    W.outside32 = W.tile("outside32", [128, T], w["outside"])
    W.qnw, W.knw = W.tile("qnw", [128, 1], w["qnw"]), W.tile("knw", [128, 1], w["knw"])
    return W


def window_attention_layer(nc, S, W, ahead):
    NP = HL // 2
    NH = HL + KVL
    EPS = 1e-6
    with ExitStack() as ctx:
        A = Alloc(nc, ctx, "d_")
        outside = A.sb("outside", [128, T], BF16)
        kscale = A.sb("kscale", [128, 1])
        xh = A.sb("xh", [128, 1, D])
        xT = A.sb("xT", [128, T])
        sq = A.sb("sq", [128, NH, HDL])
        ssq, mean_sq, r = (A.sb(n, [128, NH]) for n in ("ssq", "mean_sq", "r"))
        qn = A.sb("qn", [128, HL, HDL])
        kn = A.sb("kn", [128, KVL, 2, HDL])
        v_early = [A.sb(f"v_early{p}", [128, KVL, HDL]) for p in range(2)]
        v = [A.sb(f"v{p}", [128, KVL, HDL]) for p in range(2)]
        qT = [A.sb(f"qT{p}", [128, NP, T]) for p in range(2)]
        kT = [A.sb(f"kT{p}", [128, KVL, 2, T]) for p in range(2)]
        top, den, rden = ([A.sb(f"{n}{q}", [128, QH]) for q in range(NQ)] for n in ("top", "den", "rden"))
        pr = [A.sb(f"pr{q}", [128, QH, T]) for q in range(NQ)]
        prT = [A.sb(f"prT{q}", [128, QH, T]) for q in range(2)]
        cT = [A.sb(f"cT{p}", [128, NP, T]) for p in range(2)]
        ps = [A.ps(f"ps{k}", [128, QH, T]) for k in range(2)]
        pt = A.ps("pt", [128, QH, T])
        py = A.ps("py", [128, 512])
        pq = [A.ps(f"pq{k}", [128, 512]) for k in range(2)]
        pkv = A.ps("pkv", [128, 512])
        px = A.ps("px", [128, 512])
        s = {n: A.sem(n) for n in """prep kscale rstd xh_ready t_mm xT_ready qkv_mm sq_ready ssq_ready
            ms_ready r_ready qn_ready kn_ready ve_ready v_ready qkT_mm qT_ready kT_ready s_mm top_ready sub_ready
            exp_ready den_ready rden_ready norm_ready pt_mm prT_ready y_mm cT_ready o_mm x_ready stats kT_zero""".split()}
        with nc.Block() as block:

            @block.sync
            def _(sp):
                ahead.load(sp)

            @block.tensor
            def _(pe):
                mm, tr = nc.tensor.matmul, nc.tensor.transpose
                pe.wait_ge(W.loaded, W.all())
                pe.wait_ge(s["prep"], 1)

                def turn(b, q):
                    t = b.quad(q)
                    pe.wait_ge(s["norm_ready"], t + 1)
                    if due(t):
                        pe.wait_ge(s["prT_ready"], t)
                    for i in range(QH):
                        ins = tr(pt[:, i, :], pr[q][:, i, :], S.ident[:, :])
                    ins.then_inc(s["pt_mm"], 1)

                def scores(b, q):
                    t = b.quad(q)
                    if q == 0:
                        pe.wait_ge(s["qT_ready"], 2 * (b.n + 1))
                        pe.wait_ge(s["kT_ready"], 2 * (b.n + 1))
                    if due(t - 1):
                        pe.wait_ge(s["sub_ready"], t - 1)
                    mm(ps[q % 2][:, :, :], S.ident_bf[:, :], bc(outside[:, :], 1, QH), start=True, stop=False)
                    for k in range(2):
                        ins = mm(ps[q % 2][:, 2 * k:2 * k + 2, :], qT[b.p][:, 2 * q + k, :], kT[b.p][:, q, :, :],
                                 start=False, stop=k == 1)
                    ins.then_inc(s["s_mm"], 1)

                def values(b, q):
                    t = b.quad(q)
                    pe.wait_ge(s["prT_ready"], t + 1)
                    if q == 0:
                        pe.wait_ge(s["v_ready"], b.n + 1)
                    if due(t):
                        pe.wait_ge(s["cT_ready"], t)
                    for k in range(2):
                        ins = mm(py[64 * k:64 * k + 64, 0:2 * T], v[b.p][:, q, :], prT[q % 2][:, k:QH:2, :],
                                 start=True, stop=True)
                    ins.then_inc(s["y_mm"], 1)

                def slot(b, q):
                    if b.real():
                        turn(b, q)
                    nxt = b.plus(1)
                    if nxt.real():
                        scores(nxt, q)
                    n = b.plus(3)
                    o = b.plus(-1)
                    if q == 1 and n.real():
                        pe.wait_ge(s["xh_ready"], n.n + 1)
                        if due(n.n - 4):
                            pe.wait_ge(s["x_ready"], n.n - 4)
                        tr(px[:, 0:T], xh[:, 0, :], S.ident[:, :]).then_inc(s["t_mm"], 1)
                    if q == 2 and n.real():
                        pe.wait_ge(s["xT_ready"], n.n + 1)
                        if due(2 * n.n):
                            pe.wait_ge(s["qT_ready"], 2 * n.n)
                        if due(2 * n.n):
                            pe.wait_ge(s["kT_ready"], 2 * n.n)
                        for k in range(2):
                            mm(pq[k][:, :], xT[:, :], W.wq[:, 512 * k:512 * k + 512], start=True, stop=True
                               ).then_inc(s["qkv_mm"], 1)
                        mm(pkv[:, :], xT[:, :], W.wkv[:, :], start=True, stop=True).then_inc(s["qkv_mm"], 1)
                    m = b.plus(2)
                    if q == 1 and m.real():
                        pe.wait_ge(s["qn_ready"], 2 * (m.n + 1))
                        pe.wait_ge(s["kn_ready"], m.n + 1)
                        pe.wait_ge(s["ve_ready"], m.n + 1)
                        for k in range(2):
                            for i in range(4):
                                pair = 4 * k + i
                                ins = tr(pq[k][:, i * T:(i + 1) * T], qn[:, 2 * pair:2 * pair + 2, :], S.ident[:, :])
                            ins.then_inc(s["qkT_mm"], 1)
                        for i in range(KVL):
                            ins = tr(pkv[:, i * T:(i + 1) * T], kn[:, i, :, :], S.ident[:, :])
                        ins.then_inc(s["qkT_mm"], 1)
                    if q == 2 and o.real():
                        pe.wait_ge(s["cT_ready"], NQ * (o.n + 1))
                        if due(o.n):
                            pe.wait_ge(s["x_ready"], o.n)
                        if n.real():
                            pe.wait_ge(s["xT_ready"], n.n + 1)
                        for i in range(NP):
                            ins = mm(px[:, T:2 * T], cT[o.p][:, i, :], W.wo[:, i, :], start=i == 0, stop=i == NP - 1)
                        ins.then_inc(s["o_mm"], 1)
                    last = b if q else b.plus(-1)
                    if last.real():
                        values(last, (q - 1) % NQ)

                walk_sequences(pe, slot, 3)

            @block.scalar
            def _(act):
                A_ = nc.scalar.activation
                act.wait_ge(s["kscale"], 2)
                act.wait_ge(s["kT_zero"], 2)

                def slot(b, q):
                    y = b if q >= 2 else b.plus(-1)
                    if y.real():
                        qy = (q - 2) % NQ
                        t = y.quad(qy)
                        act.wait_ge(s["y_mm"], t + 1)
                        if due(y.n - 1):
                            act.wait_ge(s["o_mm"], y.n - 1)
                        A_(cT[y.p][:, 2 * qy:2 * qy + 2, :], py[:, 0:2 * T].rearrange("p (i t) -> p i t", t=T),
                           ACT.Copy).then_inc(s["cT_ready"], 1)
                    e = b if q < 2 else b.plus(1)
                    if e.real():
                        qe = (q + 2) % NQ
                        act.wait_ge(s["sub_ready"], e.quad(qe) + 1)
                        A_(pr[qe][:, :, :], pr[qe][:, :, :], ACT.Exp).then_inc(s["exp_ready"], 1)
                    if b.real():
                        t = b.quad(q)
                        act.wait_ge(s["pt_mm"], t + 1)
                        if due(t - 1):
                            act.wait_ge(s["y_mm"], t - 1)
                        A_(prT[q % 2][:, :, :], pt[:, :, :], ACT.Copy).then_inc(s["prT_ready"], 1)
                    n = b.plus(3)
                    m = b.plus(2)
                    if q == 1 and n.real():
                        act.wait_ge(s["t_mm"], n.n + 1)
                        if due(3 * n.n):
                            act.wait_ge(s["qkv_mm"], 3 * n.n)
                        A_(xT[:, :], px[:, 0:T], ACT.Copy).then_inc(s["xT_ready"], 1)
                    if q == 1 and m.real():
                        if due(NQ * (m.n - 1)):
                            act.wait_ge(s["s_mm"], NQ * (m.n - 1))
                        for k in range(2):
                            act.wait_ge(s["qkT_mm"], 3 * m.n + k + 1)
                            A_(qT[m.p][:, 4 * k:4 * k + 4, :], pq[k][:, :].rearrange("p (i t) -> p i t", t=T),
                               ACT.Copy).then_inc(s["qT_ready"], 1)
                        act.wait_ge(s["qkT_mm"], 3 * m.n + 3)
                        for k in range(2):
                            half = slice(64 * k, 64 * k + 64)
                            A_(kT[m.p][half, :, k, :], pkv[half, :].rearrange("p (i t) -> p i t", t=T), ACT.Copy,
                               scale=kscale[half, 0:1]).then_inc(s["kT_ready"], 1)
                    if q == 2 and n.real():
                        if due(n.n):
                            act.wait_ge(s["ssq_ready"], n.n)
                        for k in range(2):
                            act.wait_ge(s["qkv_mm"], 3 * n.n + k + 1)
                            A_(sq[:, 8 * k:8 * k + 8, :], pq[k][:, :].rearrange("p (h d) -> p h d", d=HDL),
                               ACT.Square).then_inc(s["sq_ready"], 1)
                        act.wait_ge(s["qkv_mm"], 3 * n.n + 3)
                        A_(sq[:, HL:NH, :], pkv[:, 0:256].rearrange("p (h d) -> p h d", d=HDL),
                           ACT.Square).then_inc(s["sq_ready"], 1)
                    if q == 3 and n.real():
                        if due(n.n - 1):
                            act.wait_ge(s["v_ready"], n.n - 1)
                        A_(v_early[n.p][:, :, :], pkv[:, 256:512].rearrange("p (h d) -> p h d", d=HDL),
                           ACT.Copy).then_inc(s["ve_ready"], 1)

                walk_sequences(act, slot, 3)

            @block.vector
            def _(dve):
                V = nc.vector
                dve.wait_ge(W.loaded, W.all())
                for p in range(2):
                    V.memset(kT[p][:, :, :, :], 0.0).then_inc(s["kT_zero"], 1)
                V.tensor_copy(outside[:, :], W.outside32[:, :]).then_inc(s["prep"], 1)
                V.tensor_tensor(kscale[:, :], W.qnw[:, :], W.knw[:, :], ALU.mult).then_inc(s["kscale"], 1)
                dve.wait_ge(s["kscale"], 1)
                V.tensor_scalar(kscale[:, :], kscale[:, :], HDL ** -0.5, None, ALU.mult).then_inc(s["kscale"], 1)
                dve.wait_ge(s["rstd"], LN_STEPS)

                def slot(b, q):
                    d = b if q < 3 else b.plus(1)
                    if d.real():
                        qd = (q + 1) % NQ
                        t = d.quad(qd)
                        dve.wait_ge(s["exp_ready"], t + 1)
                        V.tensor_reduce(den[qd][:, :], pr[qd][:, :, :], AX.X, ALU.add).then_inc(s["den_ready"], 1)
                    a = b if q < 1 else b.plus(1)
                    if a.real():
                        qa = (q + 3) % NQ
                        t = a.quad(qa)
                        dve.wait_ge(s["s_mm"], t + 1)
                        V.tensor_reduce(top[qa][:, :], ps[qa % 2][:, :, :], AX.X, ALU.max
                                        ).then_inc(s["top_ready"], 1)
                    if d.real():
                        t = d.quad(qd)
                        dve.wait_ge(s["den_ready"], t + 1)
                        if due(t - 3):
                            dve.wait_ge(s["norm_ready"], t - 3)
                        V.reciprocal(rden[qd][:, :], den[qd][:, :]).then_inc(s["rden_ready"], 1)
                    if a.real():
                        t = a.quad(qa)
                        dve.wait_ge(s["top_ready"], t + 1)
                        if due(t - 3):
                            dve.wait_ge(s["pt_mm"], t - 3)
                        V.tensor_tensor(pr[qa][:, :, :], ps[qa % 2][:, :, :], bc(top[qa][:, :], 2, T),
                                        ALU.subtract).then_inc(s["sub_ready"], 1)
                    n = b.plus(3)
                    m = b.plus(2)
                    if q == 0 and n.real():
                        if isinstance(n.n, int) and n.n == GS:
                            dve.wait_ge(s["rstd"], 2 * LN_STEPS)
                        if due(n.n):
                            dve.wait_ge(s["t_mm"], n.n)
                        i = bass.ds(n.n, 1)
                        V.tensor_scalar(xh[:, :, :], S.x[:, i, :], S.mean[:, i], S.rstd[:, i],
                                        ALU.subtract, ALU.mult).then_inc(s["xh_ready"], 1)
                    if q == 3 and n.real():
                        dve.wait_ge(s["sq_ready"], 3 * (n.n + 1))
                        if due(n.n):
                            dve.wait_ge(s["ms_ready"], n.n)
                        V.tensor_reduce(ssq[:, :], sq[:, :, :], AX.X, ALU.add).then_inc(s["ssq_ready"], 1)
                        dve.wait_ge(s["ssq_ready"], n.n + 1)
                        if due(n.n):
                            dve.wait_ge(s["r_ready"], n.n)
                        V.tensor_scalar(mean_sq[:, :], ssq[:, :], 1.0 / HDL, EPS, ALU.mult, ALU.add
                                        ).then_inc(s["ms_ready"], 1)
                    if q == 0 and m.real():
                        dve.wait_ge(s["r_ready"], m.n + 1)
                        if due(3 * m.n):
                            dve.wait_ge(s["qkT_mm"], 3 * m.n)
                        for k in range(2):
                            V.tensor_tensor(qn[:, 8 * k:8 * k + 8, :], pq[k][:, :].rearrange("p (h d) -> p h d", d=HDL),
                                            bc(r[:, 8 * k:8 * k + 8], 2, HDL), ALU.mult).then_inc(s["qn_ready"], 1)
                        dve.wait_ge(s["ve_ready"], m.n + 1)
                        V.tensor_tensor(kn[:, :, :, :],
                                        bc(pkv[:, 0:256].rearrange("p (h d) -> p h d", d=HDL), 2, 2),
                                        bc(bc(r[:, HL:NH], 2, 2), 3, HDL).to_broadcast([128, KVL, 2, HDL]), ALU.mult
                                        ).then_inc(s["kn_ready"], 1)
                    c = b.plus(1)
                    if q == 2 and c.real():
                        dve.wait_ge(s["ve_ready"], c.n + 1)
                        if due(NQ * (c.n - 1)):
                            dve.wait_ge(s["y_mm"], NQ * (c.n - 1))
                        V.tensor_copy(v[c.p][:, :, :], v_early[c.p][:, :, :]).then_inc(s["v_ready"], 1)
                    o = b.plus(-1)
                    if q == 3 and o.real():
                        i = bass.ds(o.n, 1)
                        dve.wait_ge(s["o_mm"], o.n + 1)
                        V.tensor_tensor(S.x[:, i, :], S.x[:, i, :], bc(px[:, T:2 * T], 1, 1), ALU.add
                                        ).then_inc(s["x_ready"], 1)
                        dve.wait_ge(s["x_ready"], o.n + 1)
                        V.bn_stats(S.bn[:, i, :], S.x[:, i, :]).then_inc(s["stats"], 1)

                walk_sequences(dve, slot, 3)

            @block.gpsimd
            def _(pool):
                P = nc.gpsimd
                for part, cols in enumerate(LN_PARTS):
                    S.ln_scalars(pool, s["rstd"], LN_EPS, cols, part * LN_STEPS)

                def slot(b, q):
                    d = b if q < 3 else b.plus(1)
                    if d.real():
                        qd = (q + 1) % NQ
                        t = d.quad(qd)
                        pool.wait_ge(s["rden_ready"], t + 1)
                        P.tensor_tensor(pr[qd][:, :, :], pr[qd][:, :, :], bc(rden[qd][:, :], 2, T), ALU.mult
                                        ).then_inc(s["norm_ready"], 1)
                    n = b.plus(3)
                    if q == 3 and n.real():
                        pool.wait_ge(s["ms_ready"], n.n + 1)
                        if due(2 * n.n):
                            pool.wait_ge(s["qn_ready"], 2 * n.n)
                        if due(n.n):
                            pool.wait_ge(s["kn_ready"], n.n)
                        P.tensor_tensor(r[:, :], mean_sq[:, :], S.minus_half[:, 0:NH], ALU.pow
                                        ).then_inc(s["r_ready"], 1)

                walk_sequences(pool, slot, 3)


LO = 32


def moe_top1_weights(nc, ctx, w):
    W = Weights(nc, ctx, "fw_")
    W.router = W.tile("router", [128, E1], w["router"])
    W.order = W.tile("order", [128, E1], w["order"].partition_broadcast(128))
    W.b1 = W.alloc.sb("b1", [LO + E1, M1])
    W.part(W.b1[0:E1, :], w["b1"])
    W.part(W.b1[LO:LO + E1, :], w["b1"])
    W.pick_row32 = W.tile("pick_row32", [E1, E1], w["pick_row"])
    W.bo, W.gamma, W.beta = (W.tile(n, [128, D], w[n].partition_broadcast(128)) for n in ("bo", "gamma", "beta"))
    W.w1 = W.tile("w1", [128, E1, M1], w["w1"])
    W.wo = W.tile("wo", [128, M1 // 128, D], w["wo"])
    return W


def moe_top1_layer(nc, S, W, out_d):
    FC = M1 // 128
    OUT_EPS = 1e-12
    with ExitStack() as ctx:
        A = Alloc(nc, ctx, "f_")
        w1_hi, w1_lo = (A.sb(n, [128, E1, M1], F32R) for n in ("w1_hi", "w1_lo"))
        b1_parts = A.sb("b1_parts", [128, M1], F32R)
        pick_row = A.sb("pick_row", [128, E1, 128], F32R)
        x_hi, x_lo = (A.sb(n, [128, NG, GT], F32R) for n in ("x_hi", "x_lo"))
        chosenT = A.sb("chosenT", [128, NG, GT], F32R)
        with ExitStack() as ctx1:
            B = Alloc(nc, ctx1, "f1_")
            xh = [B.sb(f"xh{p}", [128, GS, D]) for p in range(2)]
            xT = [B.sb(f"xT{p}", [128, GT]) for p in range(2)]
            best = B.sb("best", [128, NB, E1])
            chosen = B.sb("chosen", [128, NB, 128])
            top, pick = B.sb("top", [128, NB]), B.sb("pick", [128, NB])
            pt = [B.ps(f"pt{k}", [128, GT]) for k in range(2)]
            pl = B.ps("pl", [128, NB, E1])
            pc = [B.ps(f"pc{k}", [128, GT]) for k in range(2)]
            s = {n: B.sem(n) for n in """rstd xh_ready t_mm xT_ready hi_ready lo_ready l_mm w1_hi_ready w1_lo_ready
                b1_zero b1_hi_ready b1_lo_ready zero route chosen_ready c_mm chosenT_ready pick_row_ready""".split()}
            with nc.Block() as block:

                @block.tensor
                def _(pe):
                    pe.wait_ge(W.loaded, W.all())

                    def body(g, p):
                        pe.wait_ge(s["xh_ready"], g + 1)
                        if due(g - 1):
                            pe.wait_ge(s["xT_ready"], g - 1)
                        for i in range(GS):
                            ins = nc.tensor.transpose(pt[p][:, i * T:(i + 1) * T], xh[p][:, i, :], S.ident[:, :])
                        ins.then_inc(s["t_mm"], 1)
                        pe.wait_ge(s["xT_ready"], g + 1)
                        for i in range(GS):
                            ins = nc.tensor.matmul(pl[:, bass.ds(g * GS + i, 1), :], xT[p][:, i * T:(i + 1) * T],
                                                   W.router[:, :], start=True, stop=True)
                        ins.then_inc(s["l_mm"], 1)
                    walk_groups(pe, body)
                    pe.wait_ge(s["chosen_ready"], 1)
                    for g in range(NG):
                        if due(g - 1):
                            pe.wait_ge(s["chosenT_ready"], g - 1)
                        for i in range(GS):
                            ins = nc.tensor.transpose(pc[g % 2][:, i * T:(i + 1) * T],
                                                      chosen[:, g * GS + i, :], S.ident[:, :])
                        ins.then_inc(s["c_mm"], 1)

                @block.scalar
                def _(act):
                    A_ = nc.scalar.activation

                    def body(g, p):
                        act.wait_ge(s["t_mm"], g + 1)
                        if due(g - 1):
                            act.wait_ge(s["l_mm"], g - 1)
                        if due(g - 1):
                            act.wait_ge(s["lo_ready"], g - 1)
                        A_(xT[p][:, :], pt[p][:, :], ACT.Copy).then_inc(s["xT_ready"], 1)
                        act.wait_ge(s["xT_ready"], g + 1)
                        A_(x_hi[:, bass.ds(g, 1), :], bc(xT[p][:, :], 1, 1), ACT.Copy).then_inc(s["hi_ready"], 1)
                    walk_groups(act, body)
                    act.wait_ge(W.loaded, W.all())
                    A_(w1_hi[:, :, :], W.w1[:, :, :], ACT.Copy).then_inc(s["w1_hi_ready"], 1)
                    for g in range(NG):
                        act.wait_ge(s["c_mm"], g + 1)
                        A_(chosenT[:, g, :], pc[g % 2][:, :], ACT.Copy).then_inc(s["chosenT_ready"], 1)

                @block.vector
                def _(dve):
                    V = nc.vector
                    V.memset(chosen[:, :, :], 0.0).then_inc(s["zero"], 1)
                    V.memset(pick_row[:, :, :].bitcast(F32), 0.0)
                    V.memset(b1_parts[:, :].bitcast(F32), 0.0).then_inc(s["b1_zero"], 1)
                    dve.wait_ge(s["rstd"], LN_STEPS)

                    def body(g, p):
                        if isinstance(g, int) and g == 1:
                            dve.wait_ge(s["rstd"], 2 * LN_STEPS)
                        if due(g - 1):
                            dve.wait_ge(s["t_mm"], g - 1)
                        for i in range(GS):
                            b = bass.ds(g * GS + i, 1)
                            ins = V.tensor_scalar(xh[p][:, i:i + 1, :], S.x[:, b, :], S.mean[:, b],
                                                  S.rstd[:, b], ALU.subtract, ALU.mult)
                        ins.then_inc(s["xh_ready"], 1)
                    walk_groups(dve, body)
                    dve.wait_ge(W.loaded, W.all())
                    dve.wait_ge(s["b1_zero"], 1)
                    V.tensor_copy(b1_parts[0:E1, :], W.b1[0:E1, :]).then_inc(s["b1_hi_ready"], 1)
                    V.tensor_copy(b1_parts[LO:LO + E1, :], W.b1[LO:LO + E1, :]).then_inc(s["b1_hi_ready"], 1)
                    dve.wait_ge(s["b1_hi_ready"], 2)
                    V.tensor_tensor(b1_parts[LO:LO + E1, :], W.b1[LO:LO + E1, :],
                                    b1_parts[LO:LO + E1, :].bitcast(F32), ALU.subtract).then_inc(s["b1_lo_ready"], 1)
                    V.tensor_copy(pick_row[0:E1, :, :], bc(W.pick_row32[:, :], 2, 128)).then_inc(s["pick_row_ready"], 1)
                    dve.wait_ge(s["l_mm"], NG)
                    dve.wait_ge(s["zero"], 1)
                    V.tensor_reduce(top[:, :], pl[:, :, :], AX.X, ALU.max).then_inc(s["route"], 1)
                    dve.wait_ge(s["route"], 1)
                    V.tensor_tensor(best[:, :, :], pl[:, :, :], bc(top[:, :], 2, E1), ALU.is_equal).then_inc(s["route"], 1)
                    dve.wait_ge(s["route"], 2)
                    V.tensor_tensor(best[:, :, :], best[:, :, :], bc(W.order[:, :], 1, NB), ALU.mult).then_inc(s["route"], 1)
                    dve.wait_ge(s["route"], 3)
                    V.tensor_reduce(pick[:, :], best[:, :, :], AX.X, ALU.max).then_inc(s["route"], 1)
                    dve.wait_ge(s["route"], 4)
                    for first in (0, LO):
                        ins = V.tensor_tensor(chosen[:, :, first:first + E1], best[:, :, :], bc(pick[:, :], 2, E1),
                                              ALU.is_equal)
                    ins.then_inc(s["chosen_ready"], 1)
                    dve.wait_ge(s["w1_hi_ready"], 1)
                    V.tensor_tensor(w1_lo[:, :, :], W.w1[:, :, :], w1_hi[:, :, :].bitcast(F32), ALU.subtract
                                    ).then_inc(s["w1_lo_ready"], 1)

                @block.gpsimd
                def _(pool):
                    for part, cols in enumerate(LN_PARTS):
                        S.ln_scalars(pool, s["rstd"], LN_EPS, cols, part * LN_STEPS)

                    def body(g, p):
                        pool.wait_ge(s["hi_ready"], g + 1)
                        b = bass.ds(g, 1)
                        nc.gpsimd.tensor_tensor(x_lo[:, b, :], bc(xT[p][:, :], 1, 1), x_hi[:, b, :].bitcast(F32),
                                                ALU.subtract).then_inc(s["lo_ready"], 1)
                    walk_groups(pool, body)

        xm_hi, xm_lo = ([A.sb(f"{n}{k}", [128, GT], F32R) for k in range(2)] for n in ("xm_hi", "xm_lo"))
        gelu = A.sb("gelu", [128, FC, GT])
        y = A.sb("y", [128, GS, D])
        norm = A.sb("norm", [128, GS, D])
        scaled = A.sb("scaled", [128, GS, D])
        resid = A.sb("resid", [128, GS, D])
        ybn = A.sb("ybn", [128, GS, 6])
        ymv = A.sb("ymv", [128, GS, 2])
        yve, yr = A.sb("yve", [128, GS]), A.sb("yr", [128, GS])
        pi = [A.ps(f"pi{f}", [128, GT]) for f in range(FC)]
        pm = [A.ps(f"pm{k}", [128, GT]) for k in range(2)]
        py = A.ps("py", [128, GS, D])
        s = {n: A.sem(n) for n in """m_mm hi_ready lo_ready i_mm gelu_ready o_mm xn_ready xnb_ready y_ready bn_ready
            mv_ready ve_ready r_ready norm_ready scaled_ready resid_ready x_ready""".split()}
        stored = A.sem("stored")

        def walk(eng, unit):
            def group(g):
                for e in range(E1):
                    unit(g, e)
            group(0)
            with eng.Fori(1, NG) as g:
                group(g)

        def behind(g, e, at):
            return e == at and not (isinstance(g, int) and g == 0)

        with nc.Block() as block:

            @block.sync
            def _(sp):
                for g in range(NG):
                    sp.wait_ge(s["x_ready"], g + 1)
                    sp.dma_start(out_d[g * GS:(g + 1) * GS].rearrange("b t d -> t b d"),
                                 S.x[:, g * GS:(g + 1) * GS, :]).then_inc(stored, 16)
                sp.wait_ge(stored, 16 * NG)

            @block.tensor
            def _(pe):
                mm = nc.tensor.matmul

                def spread(g, e):
                    U = E1 * g + e
                    if due(U - 1):
                        pe.wait_ge(s["lo_ready"], U - 1)
                    mm(pm[e % 2][:, :], pick_row[:, e, :], chosenT[:, bass.ds(g, 1), :],
                       start=True, stop=True).then_inc(s["m_mm"], 1)

                def project_out(g):
                    pe.wait_ge(s["gelu_ready"], FC * (g + 1))
                    pe.wait_ge(s["y_ready"], g)
                    for i in range(GS):
                        for f in range(FC):
                            ins = mm(py[:, i, :], gelu[:, f, i * T:(i + 1) * T], W.wo[:, f, :],
                                     start=f == 0, stop=f == FC - 1)
                    ins.then_inc(s["o_mm"], 1)

                def unit(g, e):
                    U = E1 * g + e
                    if e == 0:
                        spread(g, 0)
                        spread(g, 1)
                        for f in range(FC):
                            if due(FC * (g - 1) + f + 1):
                                pe.wait_ge(s["gelu_ready"], FC * (g - 1) + f + 1)
                            mm(pi[f][:, :], b1_parts[:, f * 128:(f + 1) * 128], chosenT[:, bass.ds(g, 1), :],
                               start=True, stop=False)
                    pe.wait_ge(s["hi_ready"], U + 1)
                    pe.wait_ge(s["lo_ready"], U + 1)
                    for f in range(FC):
                        cols = slice(f * 128, (f + 1) * 128)
                        split_pass(mm, pi[f][:, :], w1_hi[:, e, cols], w1_lo[:, e, cols], xm_hi[e % 2][:, :],
                                   xm_lo[e % 2][:, :], False, e == E1 - 1).then_inc(s["i_mm"], 1)
                    if 2 <= e + 2 < E1:
                        spread(g, e + 2)
                    if behind(g, e, 1):
                        project_out(g - 1)
                walk(pe, unit)
                project_out(NG - 1)

            @block.scalar
            def _(act):
                def unit(g, e):
                    if e < E1 - 1:
                        return
                    if due(g):
                        act.wait_ge(s["o_mm"], g)
                    for f in range(FC):
                        act.wait_ge(s["i_mm"], FC * (E1 * g + E1 - 1) + f + 1)
                        nc.scalar.activation(gelu[:, f, :], pi[f][:, :], ACT.Gelu).then_inc(s["gelu_ready"], 1)
                walk(act, unit)

            @block.vector
            def _(dve):
                V = nc.vector

                def finish(g):
                    dve.wait_ge(s["norm_ready"], g)
                    for i in range(GS):
                        b = bass.ds(g * GS + i, 1)
                        ins = V.tensor_scalar(y[:, i:i + 1, :], S.x[:, b, :], S.mean[:, b], S.rstd[:, b],
                                              ALU.subtract, ALU.mult)
                    ins.then_inc(s["xn_ready"], 1)
                    dve.wait_ge(s["xn_ready"], g + 1)
                    V.tensor_tensor(y[:, :, :], y[:, :, :], bc(W.bo[:, :], 1, GS), ALU.add).then_inc(s["xnb_ready"], 1)
                    dve.wait_ge(s["xnb_ready"], g + 1)
                    dve.wait_ge(s["o_mm"], g + 1)
                    V.tensor_tensor(y[:, :, :], y[:, :, :], py[:, :, :], ALU.add).then_inc(s["y_ready"], 1)
                    dve.wait_ge(s["y_ready"], g + 1)
                    for i in range(GS):
                        ins = V.bn_stats(ybn[:, i, :], y[:, i, :])
                    ins.then_inc(s["bn_ready"], 1)

                def scale(g):
                    for i in range(GS):
                        ins = V.bn_aggr(ymv[:, i, :], ybn[:, i, :])
                    ins.then_inc(s["mv_ready"], 1)
                    dve.wait_ge(s["mv_ready"], g + 1)
                    V.tensor_scalar(yve[:, :], ymv[:, :, 1], OUT_EPS, None, ALU.add).then_inc(s["ve_ready"], 1)
                    dve.wait_ge(s["r_ready"], g + 1)
                    for i in range(GS):
                        ins = V.tensor_scalar(norm[:, i, :], y[:, i, :], ymv[:, i, 0:1], yr[:, i:i + 1],
                                              ALU.subtract, ALU.mult)
                    ins.then_inc(s["norm_ready"], 1)
                    dve.wait_ge(s["norm_ready"], g + 1)
                    V.tensor_tensor(scaled[:, :, :], norm[:, :, :], bc(W.gamma[:, :], 1, GS), ALU.mult
                                    ).then_inc(s["scaled_ready"], 1)
                    dve.wait_ge(s["scaled_ready"], g + 1)
                    dve.wait_ge(s["resid_ready"], g + 1)
                    V.tensor_tensor(seqs(S.x, g), resid[:, :, :], scaled[:, :, :], ALU.add).then_inc(s["x_ready"], 1)

                def unit(g, e):
                    U = E1 * g + e
                    k = e % 2
                    dve.wait_ge(s["m_mm"], U + 1)
                    if due(FC * (U - 1)):
                        dve.wait_ge(s["i_mm"], FC * (U - 1))
                    if behind(g, e, 4):
                        dve.wait_ge(s["bn_ready"], g)
                    for part, x, ready in ((xm_hi, x_hi, "hi_ready"), (xm_lo, x_lo, "lo_ready")):
                        V.tensor_tensor(bc(part[k][:, :], 1, 1), x[:, bass.ds(g, 1), :].bitcast(F32),
                                        bc(pm[k][:, :], 1, 1), ALU.mult).then_inc(s[ready], 1)
                    if behind(g, e, 3):
                        finish(g - 1)
                    if behind(g, e, 4):
                        scale(g - 1)
                walk(dve, unit)
                finish(NG - 1)
                dve.wait_ge(s["bn_ready"], NG)
                scale(NG - 1)

            @block.gpsimd
            def _(pool):
                P = nc.gpsimd

                def finish(g):
                    if due(g):
                        pool.wait_ge(s["x_ready"], g)
                    P.tensor_tensor(resid[:, :, :], seqs(S.x, g), bc(W.beta[:, :], 1, GS), ALU.add
                                    ).then_inc(s["resid_ready"], 1)
                    pool.wait_ge(s["ve_ready"], g + 1)
                    P.tensor_tensor(yr[:, :], yve[:, :], S.minus_half[:, 0:GS], ALU.pow).then_inc(s["r_ready"], 1)
                finish(0)
                with pool.Fori(1, NG) as g:
                    finish(g)


def program(nc, a, out):
    with ExitStack() as ctx:
        S = Shared(nc, Alloc(nc, ctx, ""))
        
        def of(prefix):
            return {k[2:]: v for k, v in a.items() if k.startswith(prefix)}

        cross0 = cross_weights(nc, ctx, of("B_"), 0)
        with ExitStack() as first:
            mamba = mamba_weights(nc, first, of("A_"))
            load_layer(nc, S, a["x"], a["ident"], mamba, cross0)
            mamba_layer(nc, S, mamba)
        moe2 = moe_top2_weights(nc, ctx, of("C_"))
        cross_attention_layer(nc, S, of("B_"), 0, cross0, moe2)
        window = window_weights(nc, ctx, of("D_"))
        moe_top2_layer(nc, S, moe2, window)
        cross1 = cross_weights(nc, ctx, of("E_"), 1)
        window_attention_layer(nc, S, window, cross1)
        moe1 = moe_top1_weights(nc, ctx, of("F_"))
        cross_attention_layer(nc, S, of("E_"), 1, cross1, moe1)
        moe_top1_layer(nc, S, moe1, out)


def layout(inputs):
    f = {k: np.asarray(v) for k, v in inputs.items()}
    a = {"x": f["x"], "ident": np.eye(128, dtype=np.float32)}

    def col(v):
        return v.reshape(-1, 128).T

    a["A_sel32"] = np.tile(np.eye(2 * NS, dtype=np.float32), (3, 1))
    a["A_gamma"], a["A_beta"] = col(f["L0_attn_gamma"]), col(f["L0_attn_beta"])
    for p in "fb":
        q, r = f"A_{p}", f"L0_attn_{p}_"
        a[q + "conv_w"] = f[r + "conv_w"][:, 0, :].T
        a[q + "in_wT"] = f[r + "in_w"].T
        a[q + "conv_b"] = col(f[r + "conv_b"])
        rows = f[r + "xproj_w"]
        spread = np.concatenate([rows[DR:], rows[DR:], rows[DR:], rows[:DR]]).T
        a[q + "xprojT"] = spread.reshape(CH, 128, -1).transpose(1, 0, 2)
        a[q + "dt_wT"] = f[r + "dt_w"].T
        a[q + "dt_b"] = col(f[r + "dt_b"])
        a[q + "A_log"] = f[r + "A_log"].reshape(CH, 128, NS).transpose(1, 0, 2)
        a[q + "D"] = col(f[r + "D"])
        a[q + "out_wT"] = f[r + "out_w"].T.reshape(CH, 128, D).transpose(1, 0, 2)
    wkv, bkv = f["L0_xattn_Wkv"], f["L0_xattn_bkv"]
    ctxT = f["ctx_1024"].transpose(2, 0, 1).reshape(D, NB * TC)
    head_of = np.repeat(np.eye(HX, dtype=np.float32), DKX, axis=0)
    mask = f["mask_Bx1xS2_if1"][:, 0, :]
    a.update({"B_wq": f["L0_xattn_Wq"], "B_wk": wkv[:, :D], "B_wv": wkv[:, D:], "B_wo": f["L0_xattn_Wout"],
              "B_bq": col(f["L0_xattn_bq"]), "B_bk": col(bkv[:D]), "B_bv": bkv[D:], "B_bo": f["L0_xattn_bout"],
              "B_hmask": head_of, "B_ctxT": ctxT, "B_mrow": mask.reshape(-1)})
    n = "L0_ffn_"
    gate, up, dn = (np.concatenate([f[n + r], f[n + s]]) for r, s in (
        ("gate_proj_w", "shared_gate_w"), ("up_proj_w", "shared_up_w"), ("down_proj_w", "shared_down_w")))
    a.update({"C_router": f[n + "gate_w"].T, "C_bias": f[n + "beta"], "C_order": E0 - np.arange(E0, dtype=np.float32),
              "C_gu": np.stack([gate, up], 1).transpose(2, 0, 1, 3),
              "C_down": dn.reshape(E0 + 1, M0 // 128, 128, D).transpose(2, 0, 1, 3)})
    n = "L1_attn_"
    i, j = np.arange(T)[:, None], np.arange(T)[None, :]
    a.update({"D_wq": f[n + "wq"].T, "D_wkv": np.concatenate([f[n + "wk"], f[n + "wv"]]).T,
              "D_wo": f[n + "wo"].T.reshape(HL // 2, 128, D).transpose(1, 0, 2),
              "D_outside": np.where((i >= j) & (i - j < WIN), 0.0, MASKED).astype(np.float32),
              "D_qnw": np.tile(f[n + "q_norm_w"], 2)[:, None], "D_knw": np.tile(f[n + "k_norm_w"], 2)[:, None]})
    a.update({"E_wq": f["L1_xattn_Wq"].T, "E_wk": f["L1_xattn_Wk"].T, "E_wv": f["L1_xattn_Wv"].T,
              "E_wo": f["L1_xattn_Wo"].T, "E_bq": col(f["L1_xattn_bq"]), "E_bk": col(f["L1_xattn_bk"]),
              "E_bv": f["L1_xattn_bv"], "E_bo": f["L1_xattn_bo"], "E_mask": f["mask_Bx1xSxS2_ik0"][:, 0],
              "E_hmask": np.repeat(np.eye(HX, dtype=np.float32), DKX, axis=0),
              "E_ctxT": f["ctx_1024"].transpose(2, 0, 1).reshape(D, NB * TC)})
    n = "L1_ffn_"
    a.update({"F_router": f[n + "Wr"].T, "F_order": E1 - np.arange(E1, dtype=np.float32),
              "F_pick_row": np.eye(E1, dtype=np.float32), "F_w1": f[n + "W1"].transpose(1, 0, 2),
              "F_wo": f[n + "Wo"].reshape(M1 // 128, 128, D).transpose(1, 0, 2)})
    a.update({"F_" + k: f[n + k] for k in ("b1", "bo", "gamma", "beta")})
    return {k: np.ascontiguousarray(v) for k, v in a.items()}


def kernel(**inputs):
    import concourse.bacc as bacc
    from concourse.bass_utils import run_bass_kernel_spmd

    nc = bacc.Bacc("TRN2", target_bir_lowering=False, num_devices=1)
    arrays, args = {}, {}
    for name, v in layout(inputs).items():
        arrays["in_" + name] = v
        args[name] = nc.dram_tensor("in_" + name, v.shape, mybir.dt.from_np(v.dtype), kind="ExternalInput").ap()
    out = nc.dram_tensor("out_x", (NB, T, D), F32, kind="ExternalOutput").ap()
    program(nc, args, out)
    r = run_bass_kernel_spmd(nc, [arrays], core_ids=[0])
    return r.results[0]["out_x"]
```
